# Optimizing a Trainium2 kernel written in Bass

```python
import numpy as np
import jax
import jax.numpy as jnp

def _softmax(x, axis=-1):
    return jax.nn.softmax(x, axis=axis)

def _gelu(x):
    return jax.nn.gelu(x, approximate=True)

def _silu(x):
    return jax.nn.silu(x)

def _sigmoid(x):
    return jax.nn.sigmoid(x)

def _layernorm(x, axis=-1, eps=1e-05):
    m = jnp.mean(x, axis=axis, keepdims=True)
    v = jnp.var(x, axis=axis, keepdims=True)
    return (x - m) / jnp.sqrt(v + eps)

def _scatter_add(tgt, idx, src, axis=0):
    return tgt.at[idx].add(src)

def _segment_sum(src, seg, n):
    return jax.ops.segment_sum(src, seg, n)
kernel_name = 'mk_gnn_resnorm_d2_gnn_r64_bcba51'

def setup_inputs(seed: int=0):
    np.random.seed(seed)
    _w = jnp.asarray

    def _rec_inputs():
        import jax
        import jax.numpy as jnp
        _gk = jax.random.key(seed)
        x = -0.000202 + 1 * jax.random.normal(jax.random.fold_in(_gk, 1), (100000, 128), jnp.float32)
        src = jax.random.randint(jax.random.fold_in(_gk, 2), (25000,), 0, 100000, jnp.int32)
        dst = jax.random.randint(jax.random.fold_in(_gk, 3), (25000,), 0, 100000, jnp.int32)
        _o = jnp.argsort(dst, stable=True)
        src = src[_o]
        dst = dst[_o]
        edge_attr_50 = jax.random.uniform(jax.random.fold_in(_gk, 13), (25000, 50), jnp.float32, 0.0, 1)
        edge_weight = jax.random.uniform(jax.random.fold_in(_gk, 15), (25000,), jnp.float32, 0.0, 0.999998)
        return (x, src, dst, edge_attr_50, edge_weight)
    x, src, dst, edge_attr_50, edge_weight = _rec_inputs()

    def _L0_gnn_setup():
        import jax, jax.numpy as jnp
        import numpy as np
        N = 50000
        E = 12500
        D_NODE = 128
        D_MSG = 64
        R = 50
        H = 4
        C = D_MSG // H

        def _segment_softmax(alpha, seg, num_segments):
            amax = jax.ops.segment_max(alpha, seg, num_segments=num_segments)
            amax = jnp.where(jnp.isfinite(amax), amax, 0.0)
            ex = jnp.exp(alpha - amax[seg])
            den = jax.ops.segment_sum(ex, seg, num_segments=num_segments)
            return ex / den[seg]
        key = jax.random.key(seed)
        ks = jax.random.split(key, 16)
        s = 0.05
        inp = {'x': jax.random.normal(ks[0], (N, D_NODE), dtype=jnp.float32), 'edge_attr': jax.random.uniform(ks[1], (E, R), dtype=jnp.float32), 'edge_index': jax.random.randint(ks[2], (2, E), 0, N, dtype=jnp.int64), 'batch': jnp.zeros((N,), dtype=jnp.int64), 'W_n2m': jax.random.normal(ks[3], (D_NODE, D_MSG), dtype=jnp.float32) * s, 'W_edge': jax.random.normal(ks[4], (R, D_MSG), dtype=jnp.float32) * s, 'W_q': jax.random.normal(ks[5], (D_MSG, D_MSG), dtype=jnp.float32) * s, 'b_q': jnp.zeros((D_MSG,), dtype=jnp.float32), 'W_k': jax.random.normal(ks[6], (D_MSG, D_MSG), dtype=jnp.float32) * s, 'b_k': jnp.zeros((D_MSG,), dtype=jnp.float32), 'W_v': jax.random.normal(ks[7], (D_MSG, D_MSG), dtype=jnp.float32) * s, 'b_v': jnp.zeros((D_MSG,), dtype=jnp.float32), 'W_e': jax.random.normal(ks[8], (D_MSG, D_MSG), dtype=jnp.float32) * s, 'W_skip': jax.random.normal(ks[9], (D_MSG, D_MSG), dtype=jnp.float32) * s, 'b_skip': jnp.zeros((D_MSG,), dtype=jnp.float32), 'W_beta': jax.random.normal(ks[10], (3 * D_MSG, 1), dtype=jnp.float32) * s, 'W_m2n': jax.random.normal(ks[11], (D_MSG, D_NODE), dtype=jnp.float32) * s}
        return inp
    _L0_gnn_all = _L0_gnn_setup()
    _L0_gnn_in = {k: v for k, v in _L0_gnn_all.items() if k in ('W_n2m', 'W_edge', 'W_q', 'b_q', 'W_k', 'b_k', 'W_v', 'b_v', 'W_e', 'W_skip', 'b_skip', 'W_beta', 'W_m2n')}
    del _L0_gnn_all

    def _L1_gnn_setup():
        import jax, jax.numpy as jnp
        import numpy as np
        N_NODES = 50000
        N_EDGES = 10000
        D_IN = 128
        D_HID = 128
        key = jax.random.key(seed)
        ks = jax.random.split(key, 7)
        X = jax.random.normal(ks[0], (N_NODES, D_IN), dtype=jnp.float32)
        w1 = jax.random.normal(ks[1], (D_IN, D_HID), dtype=jnp.float32) * 0.05
        w2 = jax.random.normal(ks[2], (D_IN, D_HID), dtype=jnp.float32) * 0.05
        b = jax.random.normal(ks[3], (D_HID,), dtype=jnp.float32) * 0.05
        edge_weight = jax.random.uniform(ks[4], (N_EDGES,), dtype=jnp.float32)
        edge_src = jax.random.randint(ks[5], (N_EDGES,), 0, N_NODES, dtype=jnp.int32)
        edge_dst = jax.random.randint(ks[6], (N_EDGES,), 0, N_NODES, dtype=jnp.int32)
        return {'X': X, 'w1': w1, 'w2': w2, 'b': b, 'edge_weight': edge_weight, 'edge_src': edge_src, 'edge_dst': edge_dst}
    _L1_gnn_all = _L1_gnn_setup()
    _L1_gnn_in = {k: v for k, v in _L1_gnn_all.items() if k in ('w1', 'w2', 'b')}
    del _L1_gnn_all
    return {'x': x, 'src': src, 'dst': dst, 'edge_attr_50': edge_attr_50, 'edge_weight': edge_weight, 'L0_gnn_W_n2m': _L0_gnn_in['W_n2m'], 'L0_gnn_W_edge': _L0_gnn_in['W_edge'], 'L0_gnn_W_q': _L0_gnn_in['W_q'], 'L0_gnn_b_q': _L0_gnn_in['b_q'], 'L0_gnn_W_k': _L0_gnn_in['W_k'], 'L0_gnn_b_k': _L0_gnn_in['b_k'], 'L0_gnn_W_v': _L0_gnn_in['W_v'], 'L0_gnn_b_v': _L0_gnn_in['b_v'], 'L0_gnn_W_e': _L0_gnn_in['W_e'], 'L0_gnn_W_skip': _L0_gnn_in['W_skip'], 'L0_gnn_b_skip': _L0_gnn_in['b_skip'], 'L0_gnn_W_beta': _L0_gnn_in['W_beta'], 'L0_gnn_W_m2n': _L0_gnn_in['W_m2n'], 'L1_gnn_w1': _L1_gnn_in['w1'], 'L1_gnn_w2': _L1_gnn_in['w2'], 'L1_gnn_b': _L1_gnn_in['b']}

def reference(x, src, dst, edge_attr_50, edge_weight, L0_gnn_W_n2m, L0_gnn_W_edge, L0_gnn_W_q, L0_gnn_b_q, L0_gnn_W_k, L0_gnn_b_k, L0_gnn_W_v, L0_gnn_b_v, L0_gnn_W_e, L0_gnn_W_skip, L0_gnn_b_skip, L0_gnn_W_beta, L0_gnn_W_m2n, L1_gnn_w1, L1_gnn_w2, L1_gnn_b):
    import jax
    import jax.numpy as jnp

    def _L0_gnn_ref(x, edge_attr, edge_index, batch, W_n2m, W_edge, W_q, b_q, W_k, b_k, W_v, b_v, W_e, W_skip, b_skip, W_beta, W_m2n):
        import jax, jax.numpy as jnp
        import numpy as np
        N = 50000
        E = 12500
        D_NODE = 128
        D_MSG = 64
        R = 50
        H = 4
        C = D_MSG // H

        def _segment_softmax(alpha, seg, num_segments):
            amax = jax.ops.segment_max(alpha, seg, num_segments=num_segments)
            amax = jnp.where(jnp.isfinite(amax), amax, 0.0)
            ex = jnp.exp(alpha - amax[seg])
            den = jax.ops.segment_sum(ex, seg, num_segments=num_segments)
            return ex / den[seg]
        src, dst = (edge_index[0], edge_index[1])
        n = x.shape[0]
        xm = x @ W_n2m
        e = edge_attr @ W_edge
        q = (xm @ W_q + b_q).reshape(n, H, C)
        k = (xm @ W_k + b_k).reshape(n, H, C)
        v = (xm @ W_v + b_v).reshape(n, H, C)
        ee = (e @ W_e).reshape(-1, H, C)
        k_e = k[src] + ee
        alpha = jnp.sum(q[dst] * k_e, axis=-1) / jnp.sqrt(jnp.float32(C))
        alpha = _segment_softmax(alpha, dst, n)
        msg = (v[src] + ee) * alpha[..., None]
        out = jax.ops.segment_sum(msg, dst, num_segments=n).reshape(n, H * C)
        x_r = xm @ W_skip + b_skip
        beta = jax.nn.sigmoid(jnp.concatenate([out, x_r, out - x_r], axis=-1) @ W_beta)
        out = beta * x_r + (1.0 - beta) * out
        return out @ W_m2n

    def _L1_gnn_ref(X, w1, w2, b, edge_weight, edge_src, edge_dst):
        import jax, jax.numpy as jnp
        import numpy as np
        N_NODES = 50000
        N_EDGES = 10000
        D_IN = 128
        D_HID = 128
        X0 = jnp.einsum('ab,bc->ac', X, w1)
        X1 = jnp.einsum('ab,bc->ac', X, w2)
        msgs = X1[edge_src] * edge_weight[:, None]
        agg = jax.ops.segment_sum(msgs, edge_dst, num_segments=X.shape[0])
        return jax.nn.relu(X0 + agg + b)
    edge_index = jnp.stack([src, dst])
    batch0 = jnp.zeros((100000,), jnp.int32)
    x = _layernorm(x + _L0_gnn_ref(x, edge_attr_50, edge_index, batch0, L0_gnn_W_n2m, L0_gnn_W_edge, L0_gnn_W_q, L0_gnn_b_q, L0_gnn_W_k, L0_gnn_b_k, L0_gnn_W_v, L0_gnn_b_v, L0_gnn_W_e, L0_gnn_W_skip, L0_gnn_b_skip, L0_gnn_W_beta, L0_gnn_W_m2n), axis=-1)
    x = _layernorm(x + _L1_gnn_ref(x, L1_gnn_w1, L1_gnn_w2, L1_gnn_b, edge_weight, src, dst), axis=-1)
    return x

_drawn_inputs = setup_inputs


def setup_inputs(seed=0):
    import zlib

    import numpy as np

    out = dict(_drawn_inputs(seed))
    spreads = {'L0_gnn_b_q': (0.0, 0.8),
     'L0_gnn_b_k': (0.0, 2.0),
     'L0_gnn_b_v': (0.0, 2.0),
     'L0_gnn_b_skip': (0.0, 0.409)}
    factors = {'edge_attr_50': 8.0,
     'L0_gnn_W_edge': 8.0,
     'L0_gnn_W_q': 8.0,
     'L0_gnn_W_k': 28.834,
     'L0_gnn_W_v': 9.287,
     'L0_gnn_W_e': 7.247,
     'L0_gnn_W_beta': 8.0}
    for name, (base, spread) in spreads.items():
        noise = np.random.default_rng([zlib.crc32(name.encode()), seed]).standard_normal(out[name].shape)
        drawn = base * np.exp(spread * noise) if base else spread * noise
        out[name] = jnp.asarray(drawn.astype(out[name].dtype))
    for name, factor in factors.items():
        out[name] = (out[name] * factor).astype(out[name].dtype)
    return out
```

```python
from contextlib import ExitStack

import concourse.bass as bass
from concourse import mybir

F32 = mybir.dt.float32
BF16 = mybir.dt.bfloat16
I32 = mybir.dt.int32
ALU = mybir.AluOpType
ACT = mybir.ActivationFunctionType
AX_X = mybir.AxisListType.X

P = 128
D = 128
DM = 64
R = 50
H = 4
C = DM // H
NJ = 4
GN = NJ * P
U = 4
EPS = 1e-5
FAR = 1e38
TOP = 88.0
QSCALE = 1.0 / C ** 0.5


def wait(eng, sem, value):
    if not (isinstance(value, int) and value <= 0):
        eng.wait_ge(sem, value)


def live(k, lag, n):
    return not isinstance(k, int) or 0 <= k - lag < n


def back(k, u, it, lag):
    return k - lag, (u - lag) % U, it + (u - lag) // U


def run_steps(eng, n, lag, step):
    for u in range(U):
        step(u, u, 0)
    with eng.Fori(1, n // U - 1) as it:
        for u in range(U):
            step(it * U + u, u, it)
    for k in range(n - U, n + lag):
        step(k, k % U, k // U)


def gnn_kernel(nc, x, xT, src, dst, ea, ew, w_n2mT, w_edgeT, w_q, b_q, w_k, b_k, w_v, b_v,
               w_e, w_skip, b_skip, w_beta, w_m2n, w_1, w_2, b_1, out):
    N = x.shape[0]
    E = src.shape[1]
    T = -(-E // (P * U)) * U
    EP = P * T
    G = -(-N // (GN * U)) * U
    assert G == T and G * GN - N < GN and EP - E < T
    VLAST = T - (EP - E)

    h_tab = nc.dram_tensor("h_tab", (N, D), F32, kind="Internal").ap()
    hd_scr = nc.dram_tensor("hd_scr", (T, P, D), F32, kind="Internal").ap()
    dst_s = nc.dram_tensor("dst_s", (1, EP + 2), I32, kind="Internal").ap()
    ea_s = nc.dram_tensor("ea_s", (EP, R), F32, kind="Internal").ap()
    ea_t = ea_s.rearrange("(p t) r -> p t r", p=P)

    with ExitStack() as ctx:
        def sb(name, shape, dt=F32):
            return ctx.enter_context(nc.sbuf_tensor(name, shape, dt))

        def sem(name):
            return ctx.enter_context(nc.semaphore(name))

        pt = ctx.enter_context(nc.psum_tensor("pt", [P, 2, 512], F32))
        pk = ctx.enter_context(nc.psum_tensor("pk", [P, 2, 512], F32))
        pd = ctx.enter_context(nc.psum_tensor("pd", [P, 2, NJ, 256], F32))

        big = sb("big", [P, D * T])
        xdT_all = big[:, :].rearrange("p (t n) -> p t n", t=T)
        agg = big[:, :].rearrange("p (f t) -> p f t", t=T)
        val = sb("val", [P, H, C, T])
        alpha = sb("alpha", [P, H, T])
        rmax = sb("rmax", [P, H, T + 1])
        decay = sb("decay", [P, H, T])
        cdec = sb("cdec", [P, H, T])
        rden = sb("rden", [P, H, T])
        same = sb("same", [P, T])
        far = sb("far", [P, T])
        pfar = sb("pfar", [P, T])
        psame = pfar
        ones_t = sb("ones_t", [P, T])
        ew_t = sb("ew_t", [P, T])
        gidx = sb("gidx", [P, T, 2], I32)
        sidx = sb("sidx", [P, T], I32)

        ring_a = sb("ring_a", [P, U, D])
        ring_b = sb("ring_b", [P, U, D])
        pair = sb("pair", [P, 2, 2 * D])
        ring_d = pair[:, :, 0:D]
        ring_c = pair[:, :, D:2 * D]
        ring_e = sb("ring_e", [P, 2, D])
        ring_f = sb("ring_f", [P, 2, D])
        ea_in = sb("ea_in", [P, U, R])
        q_sb = sb("q_sb", [P, 2, DM])
        prod = sb("prod", [P, 2, DM])
        o1, o2 = (prod[:, i, :].rearrange("p (h c) -> p h c", h=H) for i in range(2))
        o3 = sb("o3", [P, 2, P])
        xg = sb("xg", [P, U, GN])
        xgT = sb("xgT", [P, 2, GN])
        hpre = sb("hpre", [P, 2, GN])
        hout = sb("hout", [P, 2, GN])
        idx2 = sb("idx2", [P, U, 2], I32)
        em = sb("em", [P, 2, NJ])
        ep = sb("ep", [P, 2, NJ])
        beta = sb("beta", [P, 2, NJ])
        stats = sb("stats", [P, 2, NJ, 6])
        mv = sb("mv", [P, 2, NJ, 2])
        lv = sb("lv", [P, 2, NJ])
        rs = sb("rs", [P, 2, NJ])

        ident = sb("ident", [P, P])
        a_kv = sb("a_kv", [P, 2 * DM])
        a_q = sb("a_q", [P, DM])
        b_kvq = sb("b_kvq", [R + 1, 3 * DM])
        w_sx = sb("w_sx", [P, 2 * D + 1])
        r_o = sb("r_o", [DM, 2 * D + 1])
        r_c = sb("r_c", [DM, D + 1])
        ones3 = sb("ones3", [3, P], BF16)
        bias3 = sb("bias3", [3, 3 * D + 1], BF16)
        w1_sb = sb("w1_sb", [P, D])
        w2_sb = sb("w2_sb", [P, D])
        n2mT = hpre[0:DM, 0, 0:D]
        kvq_w = hpre[0:DM, 0, D:D + 3 * DM]
        e_w = hpre[0:DM, 0, 320:384]
        skip_w = hpre[0:DM, 0, 384:448]
        edgeT = hpre[0:DM, 0, 448:448 + R]
        m2n_w = hpre[0:DM, 1, 0:D]
        beta_w = hpre[0:DM, 1, 128:131]
        bskip = hpre[0:DM, 1, 132:133]
        wnsT = hpre[0:DM, 1, 136:264]
        brow = hout[0:1, 0, 0:3 * D + 1]
        brow_r = hout[0:1, 1, 0:3 * D + 1]
        brow_b = val[0:1, 0, :, :].rearrange("p c t -> p (c t)")[:, 0:1200].bitcast(BF16)\
            .rearrange("p (i n) -> p i n", i=3)[:, :, 0:3 * D + 1]
        d_int = [cdec[:, h, :].bitcast(I32) for h in range(3)]
        s_int = cdec[:, 3, :].bitcast(I32)
        d_f = [decay[:, h, :] for h in range(3)]
        nend = decay[:, 3, :]
        clip = rden[:, 0, :]
        pad_i = rden[0:1, 1, 0:P].bitcast(I32)
        zrows = big[0:EP - E, 0:R]
        sum_a = hpre[:, 0, 0:D]
        sum_b = hpre[:, 0, D:2 * D]
        keepT = hpre[:, 0, 2 * D:3 * D]
        cumT = hpre[:, 1, 0:P + 1]
        carm = sb("carm", [P, H])
        carn = sb("carn", [P, DM + H])
        carg = cdec[:, 0, 0:D]

        S = {n: sem(n) for n in (
            "w_in", "pad_in", "edge_in", "edge_in2", "padded", "id0", "id1", "fills", "gp_fill", "wprod", "wcopy",
            "rows", "rows_in", "dsteps", "issued",
            "idx_a", "t_a", "xsT_a", "kv_a", "q_a", "v_a", "pr_a", "al_a",
            "mm_d1", "cl_d1", "em_d1", "ep_d1", "be_d1", "pre_d1", "bn_d1", "mv_d1", "lv_d1", "rs_d1", "out_d1",
            "sc", "sc_pe", "sc_act", "sc_pool",
            "o_b1", "os_b1", "t_b1", "oT_b1", "mm_b1", "cl_b1", "em_b1", "xb_b1", "ep_b1", "be_b1", "pre_b1", "bn_b1",
            "mv_b1", "lv_b1", "rs_b1", "h_b1", "idx_b1",
            "idx_b2", "agg_b2", "t_d2", "hT_d2", "mm_d2", "u_d2", "bn_d2", "mv_d2", "lv_d2", "rs_d2", "out_d2",
            "ag_c", "t_c", "tc_c", "mm_c", "u_c", "bn_c", "mv_c", "lv_c", "rs_c", "z_c", "idx_c")}
        ring = {n: [sem(f"{n}{u}") for u in range(U)] for n in (
            "xs_in", "xd_in", "ea_in", "xg_in", "xgT_in", "xdT_mv", "h_st",
            "xl_in", "hd_st", "h_sc", "hs_in", "hg_in", "z_st", "hd_in", "z_sc")}
        last = T // U * 16

        n0 = N - GN

        def node0(g):
            return n0 if isinstance(g, int) and g == G - 1 else g * GN

        def rows_of(tab, g):
            b = node0(g)
            if isinstance(b, int):
                return tab[b:b + GN, :].rearrange("(p j) f -> p (j f)", j=NJ)
            return tab[bass.ds(b, GN), :].rearrange("(p j) f -> p (j f)", j=NJ)

        block = ctx.enter_context(nc.Block())

        @block.sync
        def _(sp):
            loads = [(n2mT, w_n2mT), (kvq_w[:, 0:DM], w_k), (kvq_w[:, DM:2 * DM], w_v),
                     (kvq_w[:, 2 * DM:3 * DM], w_q), (e_w, w_e), (skip_w, w_skip), (edgeT, w_edgeT),
                     (m2n_w, w_m2n), (beta_w, w_beta), (bskip, b_skip), (w1_sb[:, :], w_1), (w2_sb[:, :], w_2),
                     (b_kvq[R:R + 1, 0:DM], b_k), (b_kvq[R:R + 1, DM:2 * DM], b_v),
                     (b_kvq[R:R + 1, 2 * DM:3 * DM], b_q)]
            sp.wait_ge(S["fills"], 1)
            for to, of in loads:
                sp.dma_start(to, of).then_inc(S["w_in"], 16)
            sp.dma_start(brow[0:1, 2 * D + 1:3 * D + 1], b_1).then_inc(S["w_in"], 16)
            sp.wait_ge(S["padded"], 1)
            sp.dma_start(dst_s[0:1, 0:1], pad_i[0:1, P - 1:P]).then_inc(S["pad_in"], 16)
            sp.dma_start(dst_s[0:1, 1:E + 1], dst).then_inc(S["pad_in"], 16)
            sp.dma_start(dst_s[0:1, E + 1:EP + 2], pad_i[0:1, 0:EP + 1 - E]).then_inc(S["pad_in"], 16)
            sp.dma_start(ea_s[0:E, :], ea).then_inc(S["pad_in"], 16)
            sp.dma_start(ea_s[E:EP, :], zrows).then_inc(S["pad_in"], 16)
            sp.wait_ge(S["fills"], 2)
            sp.dma_start(s_int[0:P - 1, :], src[0:1, 0:(P - 1) * T].rearrange("a (p t) -> (a p) t", t=T))\
                .then_inc(S["edge_in"], 16)
            sp.dma_start(s_int[P - 1:P, 0:VLAST], src[0:1, (P - 1) * T:E]).then_inc(S["edge_in"], 16)
            sp.dma_start(ew_t[0:P - 1, :], ew[0:1, 0:(P - 1) * T].rearrange("a (p t) -> (a p) t", t=T))\
                .then_inc(S["edge_in"], 16)
            sp.dma_start(ew_t[P - 1:P, 0:VLAST], ew[0:1, (P - 1) * T:E]).then_inc(S["edge_in"], 16)
            sp.wait_ge(S["pad_in"], 5 * 16)
            for i, shift in enumerate((1, 0, 2)):
                sp.dma_start(d_int[i], dst_s[0:1, shift:shift + EP].rearrange("a (p t) -> (a p) t", t=T))\
                    .then_inc(S["edge_in"], 16)
            sp.wait_ge(S["rows"], 1)
            for i in range(3):
                sp.dma_start(bias3[i:i + 1, :], brow_b[0:1, i, :]).then_inc(S["rows_in"], 16)

            def step_a(k, u, it):
                if live(k, 0, T):
                    wait(sp, S["t_a"], k - U + 1)
                    sp.dma_start(ea_in[:, u, :], ea_t[:, k, :] if isinstance(k, int)
                                 else ea_t[:, bass.ds(k, 1), :].rearrange("p a r -> p (a r)"))\
                        .then_inc(ring["ea_in"][u], 16)
                    wait(sp, S["pre_d1"], k - U + 1)
                    sp.dma_start(xg[:, u, :], rows_of(x, k)).then_inc(ring["xg_in"][u], 16)
                    wait(sp, S["mm_d1"], k - 1)
                    sp.dma_start(xgT[:, u % 2, :], xT[k, :, :] if isinstance(k, int)
                                 else xT[bass.ds(k, 1), :, :].rearrange("a p n -> (a p) n"))\
                        .then_inc(ring["xgT_in"][u], 16)
                if live(k, 2, T):
                    j, ju, _ = back(k, u, it, 2)
                    wait(sp, S["xsT_a"], j + 1)
                    sp.dma_start(xdT_all[:, j, :] if isinstance(j, int)
                                 else xdT_all[:, bass.ds(j, 1), :].rearrange("p a n -> p (a n)"),
                                 ring_c[:, ju % 2, :]).then_inc(ring["xdT_mv"][ju], 16)
                    wait(sp, S["out_d1"], j + 1)
                    if isinstance(j, int) and j == G - 1:
                        for q in range(U):
                            sp.wait_ge(ring["h_st"][q], last - (16 if q == ju else 0))
                    sp.dma_start(rows_of(h_tab, j), hout[:, j % 2 if isinstance(j, int) else ju % 2, :])\
                        .then_inc(ring["h_st"][ju], 16)
            run_steps(sp, T, 2, step_a)

            for q in range(U):
                sp.wait_ge(ring["xdT_mv"][q], last)

            def step_b1(k, u, it):
                if live(k, 0, T):
                    if isinstance(k, int) and k < U:
                        sp.wait_ge(S["t_a"], T)
                    wait(sp, S["mm_b1"], k - U + 1)
                    sp.dma_start(ring_a[:, u, :], xdT_all[:, k, :] if isinstance(k, int)
                                 else xdT_all[:, bass.ds(k, 1), :].rearrange("p a n -> p (a n)"))\
                        .then_inc(ring["xl_in"][u], 16)
                if live(k, 3, T):
                    j, ju, _ = back(k, u, it, 3)
                    wait(sp, S["h_b1"], j + 1)
                    sp.dma_start(hd_scr[j, :, :] if isinstance(j, int)
                                 else hd_scr[bass.ds(j, 1), :, :].rearrange("a p n -> (a p) n"),
                                 ring_b[:, ju, :]).then_inc(ring["hd_st"][ju], 16)
            run_steps(sp, T, 3, step_b1)

            def step_b2(k, u, it):
                if live(k, 0, G):
                    wait(sp, S["u_d2"], k - U + 1)
                    sp.dma_start(xg[:, u, :], rows_of(h_tab, k)).then_inc(ring["hg_in"][u], 16)
                if live(k, 3, G):
                    j, ju, _ = back(k, u, it, 3)
                    wait(sp, S["out_d2"], j + 1)
                    if isinstance(j, int) and j == G - 1:
                        for q in range(U):
                            sp.wait_ge(ring["z_st"][q], last - (16 if q == ju else 0))
                    sp.dma_start(rows_of(out, j), hout[:, ju % 2, :]).then_inc(ring["z_st"][ju], 16)
            for q in range(U):
                sp.wait_ge(ring["h_sc"][q], last)
                sp.wait_ge(ring["hd_st"][q], last)
            run_steps(sp, G, 3, step_b2)

            def step_c(k, u, it):
                if live(k, 0, T):
                    wait(sp, S["u_c"], k - U + 1)
                    sp.dma_start(ring_a[:, u, :], hd_scr[k, :, :] if isinstance(k, int)
                                 else hd_scr[bass.ds(k, 1), :, :].rearrange("a p n -> (a p) n"))\
                        .then_inc(ring["hd_in"][u], 16)
            sp.wait_ge(S["agg_b2"], T)
            run_steps(sp, T, 0, step_c)
            for q in range(U):
                sp.wait_ge(ring["z_st"][q], last)
                sp.wait_ge(ring["z_sc"][q], last)

        @block.gpsimd
        def _(gp):
            gp.memset(ident[:, :], 0.0).then_inc(S["id0"], 1)
            gp.wait_ge(S["id0"], 1)
            gp.affine_select(out=ident[:, :], in_=ident[:, :], compare_op=ALU.not_equal, fill=1.0, base=0,
                             pattern=[[-1, P]], channel_multiplier=1).then_inc(S["id1"], 1)
            gp.wait_ge(S["dsteps"], 1)
            top_row = gp.to_reg(N - 1)

            def step_a(k, u, it):
                wait(gp, S["t_a"], k - U + 1)
                gp.tensor_copy(idx2[:, u, :], gidx[:, k, :] if isinstance(k, int)
                               else gidx[:, bass.ds(k, 1), :].rearrange("p a i -> p (a i)"))\
                    .then_inc(S["idx_a"], 1)
                wait(gp, S["idx_a"], k + 1)
                gp.sem_inc(S["issued"], 1)
                for i, (rg, s) in enumerate(((ring_a, "xs_in"), (ring_b, "xd_in"))):
                    gp.indirect_dma_start(out=rg[:, u, :], out_offset=None, in_=x[:, :],
                                          in_offset=bass.IndirectOffsetOnAxis(ap=idx2[:, u, i:i + 1], axis=0))\
                        .then_inc(ring[s][u], 16)
            run_steps(gp, T, 0, step_a)

            gp.wait_ge(S["sc_act"], 2)
            vh = val[:, H - 1, :, :]
            gp.tensor_tensor(vh, vh, alpha[:, H - 1, :].rearrange("p (a t) -> p a t", a=1).to_broadcast([P, C, T]),
                             ALU.mult).then_inc(S["sc_pool"], 1)

            for q in range(U):
                gp.wait_ge(ring["h_st"][q], last)

            def step_b1(k, u, it):
                wait(gp, ring["h_sc"][u], 16 * it)
                gp.tensor_copy(idx2[:, u, 0:1], sidx[:, k:k + 1] if isinstance(k, int)
                               else sidx[:, bass.ds(k, 1)]).then_inc(S["idx_b1"], 1)
                wait(gp, S["idx_b1"], k + 1)
                wait(gp, S["h_b1"], k + 1)
                gp.sem_inc(S["issued"], 1)
                gp.indirect_dma_start(out=h_tab[:, :],
                                      out_offset=bass.IndirectOffsetOnAxis(ap=idx2[:, u, 0:1], axis=0),
                                      in_=ring_b[:, u, :], in_offset=None, bounds_check=top_row,
                                      oob_is_err=False).then_inc(ring["h_sc"][u], 16)
            run_steps(gp, T, 0, step_b1)
            for q in range(U):
                gp.wait_ge(ring["h_sc"][q], last)

            def step_b2(k, u, it):
                if isinstance(k, int) and k < U:
                    gp.wait_ge(S["mm_b1"], T)
                wait(gp, S["agg_b2"], k - U + 1)
                gp.tensor_copy(idx2[:, u, 0:1], gidx[:, k, 0:1] if isinstance(k, int)
                               else gidx[:, bass.ds(k, 1), 0:1].rearrange("p a i -> p (a i)"))\
                    .then_inc(S["idx_b2"], 1)
                wait(gp, S["idx_b2"], k + 1)
                gp.sem_inc(S["issued"], 1)
                gp.indirect_dma_start(out=ring_a[:, u, :], out_offset=None, in_=h_tab[:, :],
                                      in_offset=bass.IndirectOffsetOnAxis(ap=idx2[:, u, 0:1], axis=0))\
                    .then_inc(ring["hs_in"][u], 16)
            run_steps(gp, T, 0, step_b2)
            for q in range(U):
                gp.wait_ge(ring["z_st"][q], last)
                gp.wait_ge(ring["hs_in"][q], last)

            def step_c(k, u, it):
                wait(gp, ring["z_sc"][u], 16 * it)
                gp.tensor_copy(idx2[:, u, 0:1], sidx[:, k:k + 1] if isinstance(k, int)
                               else sidx[:, bass.ds(k, 1)]).then_inc(S["idx_c"], 1)
                wait(gp, S["idx_c"], k + 1)
                wait(gp, S["z_c"], k + 1)
                gp.sem_inc(S["issued"], 1)
                gp.indirect_dma_start(out=out[:, :],
                                      out_offset=bass.IndirectOffsetOnAxis(ap=idx2[:, u, 0:1], axis=0),
                                      in_=ring_b[:, u, :], in_offset=None, bounds_check=top_row,
                                      oob_is_err=False).then_inc(ring["z_sc"][u], 16)
            run_steps(gp, T, 0, step_c)

        @block.tensor
        def _(pe):
            pe.wait_ge(S["w_in"], 16 * 16)
            pe.matmul(pk[:, 0, 0:3 * DM], n2mT, kvq_w, start=True, stop=True).then_inc(S["wprod"], 1)
            pe.matmul(pk[0:R, 1, 0:DM], edgeT, e_w, start=True, stop=True).then_inc(S["wprod"], 1)
            pe.matmul(pt[0:DM, 0, 0:P], skip_w, n2mT, start=True, stop=True).then_inc(S["wprod"], 1)
            pe.wait_ge(S["wcopy"], 2)
            pe.matmul(pt[:, 1, 0:D + 1], wnsT, r_c[:, :], start=True, stop=True).then_inc(S["wprod"], 1)
            pe.matmul(pd[0:1, 0, 0, 0:D + 1], bskip, r_c[:, :], start=True, stop=True).then_inc(S["wprod"], 1)
            pe.wait_ge(S["wcopy"], 5)
            pe.wait_ge(S["rows_in"], 3 * 16)
            pe.wait_ge(S["id1"], 1)

            def step_a(k, u, it):
                if live(k, 0, T):
                    wait(pe, ring["xs_in"][u], 16 * (it + 1))
                    wait(pe, ring["xd_in"][u], 16 * (it + 1))
                    wait(pe, ring["ea_in"][u], 16 * (it + 1))
                    wait(pe, S["xsT_a"], k - 1)
                    pe.transpose(pt[:, u % 2, 0:P], ring_a[:, u, :], ident[:, :])
                    pe.transpose(pt[:, u % 2, P:2 * P], ring_b[:, u, :], ident[:, :])
                    pe.transpose(pt[0:R, u % 2, 2 * P:3 * P], ea_in[:, u, :], ident[:, :]).then_inc(S["t_a"], 1)
                    wait(pe, ring["xgT_in"][u], 16 * (it + 1))
                    wait(pe, S["pre_d1"], k - 1)
                    for j in range(NJ):
                        o = pd[:, u % 2, j, 0:D + 1]
                        pe.matmul(o, ones3[:, :], bias3[:, 0:D + 1], start=True, stop=False)
                        mm = pe.matmul(o, xgT[:, u % 2, j * P:(j + 1) * P], w_sx[:, 0:D + 1],
                                       start=False, stop=True)
                    mm.then_inc(S["mm_d1"], 1)
                if live(k, 1, T):
                    j, ju, _ = back(k, u, it, 1)
                    wait(pe, S["xsT_a"], j + 1)
                    wait(pe, S["v_a"], j - 1)
                    wait(pe, S["pr_a"], j - 1)
                    pe.matmul(pk[:, ju % 2, 0:3 * DM], ring_e[0:R + 1, ju % 2, :], b_kvq[:, :], start=True, stop=False)
                    pe.matmul(pk[:, ju % 2, 0:2 * DM], ring_d[:, ju % 2, :], a_kv[:, :], start=False, stop=False)
                    pe.matmul(pk[:, ju % 2, 2 * DM:3 * DM], ring_c[:, ju % 2, :], a_q[:, :], start=False, stop=True)\
                        .then_inc(S["kv_a"], 1)
            run_steps(pe, T, 1, step_a)

            pe.wait_ge(S["sc"], 1)
            pe.transpose(pt[0:H, 0, 0:P], sum_a[:, 0:H], ident[:, :])
            pe.transpose(pt[0:H, 0, P:2 * P], sum_b[:, 0:H], ident[:, :]).then_inc(S["sc_pe"], 1)
            pe.wait_ge(S["sc"], 2)
            pe.transpose(pt[:, 1, 0:H], cumT[0:H, 0:P], ident[0:H, 0:H]).then_inc(S["sc_pe"], 1)
            pe.wait_ge(S["sc"], 4)
            pe.transpose(pt[0:DM + H, 0, 0:P], sum_a[:, 0:DM + H], ident[:, :])
            pe.transpose(pt[0:DM + H, 0, P:2 * P], sum_b[:, 0:DM + H], ident[:, :]).then_inc(S["sc_pe"], 1)
            pe.wait_ge(S["sc"], 5)
            pe.transpose(pt[:, 1, 0:DM + H], cumT[0:DM + H, 0:P], ident[0:DM + H, 0:DM + H]).then_inc(S["sc_pe"], 1)

            def step_b1(k, u, it):
                if live(k, 0, T):
                    wait(pe, S["os_b1"], k + 1)
                    wait(pe, S["oT_b1"], k - 1)
                    if isinstance(k, int) and k < 2:
                        pe.wait_ge(S["sc"], 6)
                    pe.transpose(pt[:, u % 2, 0:P], o3[:, u % 2, :], ident[:, :]).then_inc(S["t_b1"], 1)
                if live(k, 1, T):
                    j, ju, itj = back(k, u, it, 1)
                    wait(pe, ring["xl_in"][ju], 16 * (itj + 1))
                    wait(pe, S["oT_b1"], j + 1)
                    wait(pe, S["pre_b1"], j - 1)
                    o = pk[:, ju % 2, 0:2 * D + 1]
                    pe.matmul(o, ones3[:, :], bias3[:, 0:2 * D + 1], start=True, stop=False)
                    pe.matmul(o, ring_a[:, ju, :], w_sx[:, :], start=False, stop=False)
                    pe.matmul(o, ring_d[0:DM, ju % 2, :], r_o[:, :], start=False, stop=True)\
                        .then_inc(S["mm_b1"], 1)
            run_steps(pe, T, 1, step_b1)
            pe.wait_ge(S["pre_b1"], T)

            def step_b2(k, u, it):
                if live(k, 0, G):
                    wait(pe, ring["hg_in"][u], 16 * (it + 1))
                    wait(pe, S["hT_d2"], k - 1)
                    for j in range(NJ):
                        mm = pe.transpose(pt[:, u % 2, j * P:(j + 1) * P], xg[:, u, j * D:(j + 1) * D], ident[:, :])
                    mm.then_inc(S["t_d2"], 1)
                if live(k, 1, G):
                    g, gu, _ = back(k, u, it, 1)
                    wait(pe, S["hT_d2"], g + 1)
                    wait(pe, S["u_d2"], g - 1)
                    for j in range(NJ):
                        o = pk[:, gu % 2, j * D:(j + 1) * D]
                        pe.matmul(o, ones3[:, :], bias3[:, 2 * D + 1:3 * D + 1], start=True, stop=False)
                        mm = pe.matmul(o, xgT[:, gu % 2, j * P:(j + 1) * P], w1_sb[:, :], start=False, stop=True)
                    mm.then_inc(S["mm_d2"], 1)
            run_steps(pe, G, 1, step_b2)
            pe.wait_ge(S["u_d2"], G)

            pe.wait_ge(S["sc"], 7)
            pe.transpose(pt[:, 0, 0:P], sum_a, ident[:, :])
            pe.transpose(pt[:, 0, P:2 * P], sum_b, ident[:, :]).then_inc(S["sc_pe"], 1)
            pe.wait_ge(S["sc"], 8)
            pe.transpose(pt[:, 1, 0:D], cumT[:, 0:P], ident[:, :]).then_inc(S["sc_pe"], 1)

            def step_c(k, u, it):
                if live(k, 0, T):
                    wait(pe, S["ag_c"], k + 1)
                    wait(pe, ring["hd_in"][u], 16 * (it + 1))
                    wait(pe, S["tc_c"], k - 1)
                    pe.transpose(pt[:, u % 2, 0:P], ring_a[:, u, :], ident[:, :])
                    pe.transpose(pt[:, u % 2, P:2 * P], ring_d[:, u % 2, :], ident[:, :]).then_inc(S["t_c"], 1)
                if live(k, 1, T):
                    j, ju, _ = back(k, u, it, 1)
                    wait(pe, S["tc_c"], j + 1)
                    wait(pe, S["u_c"], j - 1)
                    o = pk[:, ju % 2, 0:D]
                    pe.matmul(o, ones3[:, :], bias3[:, 2 * D + 1:3 * D + 1], start=True, stop=False)
                    pe.matmul(o, xgT[:, ju % 2, 0:P], w1_sb[:, :], start=False, stop=False)
                    pe.matmul(o, xgT[:, ju % 2, P:2 * P], w2_sb[:, :], start=False, stop=True)\
                        .then_inc(S["mm_c"], 1)
            run_steps(pe, T, 1, step_c)

        def inv_std(act, mean_var, log_v, r, mv_sem, lv_sem, rs_sem, j):
            wait(act, mv_sem, j + 1)
            act.activation(log_v, mean_var, ACT.Ln, bias=eps_c[:, 0:1]).then_inc(lv_sem, 1)
            wait(act, lv_sem, j + 1)
            act.activation(r, log_v, ACT.Exp, scale=-0.5).then_inc(rs_sem, 1)

        def exp_minus(act, e, logit, cl_sem, em_sem, j):
            act.activation(e, logit, ACT.Relu, bias=top_c[:, 0:1]).then_inc(cl_sem, 1)
            wait(act, cl_sem, j + 1)
            act.activation(e, e, ACT.Exp, bias=top_c[:, 0:1], scale=-1.0).then_inc(em_sem, 1)

        eps_c = sb("eps_c", [P, 1])
        top_c = sb("top_c", [P, 1])

        @block.scalar
        def _(act):
            act.preload_act_table_set("natural_log_exp_and_others")
            act.wait_ge(S["wprod"], 1)
            act.activation(a_kv[:, :], pk[:, 0, 0:2 * DM], ACT.Copy)
            act.activation(a_q[:, :], pk[:, 0, 2 * DM:3 * DM], ACT.Copy)
            act.wait_ge(S["wprod"], 2)
            act.activation(b_kvq[0:R, 0:DM], pk[0:R, 1, 0:DM], ACT.Copy)
            act.activation(b_kvq[0:R, DM:2 * DM], pk[0:R, 1, 0:DM], ACT.Copy)
            act.wait_ge(S["wprod"], 3)
            act.activation(wnsT, pt[0:DM, 0, 0:P], ACT.Copy).then_inc(S["wcopy"], 1)
            act.wait_ge(S["wprod"], 4)
            act.activation(w_sx[:, 0:D + 1], pt[:, 1, 0:D + 1], ACT.Copy).then_inc(S["wcopy"], 1)
            act.wait_ge(S["id1"], 1)
            act.activation(w_sx[:, D + 1:2 * D + 1], ident[:, :], ACT.Copy).then_inc(S["wcopy"], 1)

            def step_a(k, u, it):
                if live(k, 0, T):
                    wait(act, S["t_a"], k + 1)
                    wait(act, S["kv_a"], k - 1)
                    if live(k, 2, T):
                        _, su, sit = back(k, u, it, 2)
                        wait(act, ring["xdT_mv"][su], 16 * (sit + 1))
                    act.activation(pair[:, u % 2, :], pt[:, u % 2, 0:2 * P], ACT.Copy)
                    act.activation(ring_e[0:R, u % 2, :], pt[0:R, u % 2, 2 * P:3 * P], ACT.Copy)\
                        .then_inc(S["xsT_a"], 1)
                    wait(act, S["mm_d1"], k + 1)
                    wait(act, S["pre_d1"], k - 1)
                    exp_minus(act, em[:, u % 2, :], pd[:, u % 2, :, D], S["cl_d1"], S["em_d1"], k)
                if live(k, 1, T):
                    j, ju, _ = back(k, u, it, 1)
                    inv_std(act, mv[:, ju % 2, :, 1], lv[:, ju % 2, :], rs[:, ju % 2, :],
                            S["mv_d1"], S["lv_d1"], S["rs_d1"], j)
                    wait(act, S["kv_a"], j + 1)
                    wait(act, S["pr_a"], j - 1)
                    kv = pk[:, ju % 2, DM:2 * DM].rearrange("p (h c) -> p h c", h=H)
                    vo = val[:, :, :, j] if isinstance(j, int) else \
                        val[:, :, :, bass.ds(j, 1)].rearrange("p h c a -> p h (c a)")
                    act.activation(vo, kv, ACT.Copy).then_inc(S["v_a"], 1)
                    act.activation(q_sb[:, ju % 2, :], pk[:, ju % 2, 2 * DM:3 * DM], ACT.Copy).then_inc(S["q_a"], 1)
            run_steps(act, T, 1, step_a)

            act.wait_ge(S["sc"], 3)
            act.activation(decay[:, :, :], decay[:, :, :], ACT.Exp).then_inc(S["sc_act"], 1)
            act.activation(alpha[:, :, :], alpha[:, :, :], ACT.Exp).then_inc(S["sc_act"], 1)

            def step_b1(k, u, it):
                if live(k, 0, T):
                    wait(act, S["t_b1"], k + 1)
                    wait(act, S["mm_b1"], k - 1)
                    act.activation(ring_d[0:DM, u % 2, :], pt[0:DM, u % 2, 0:P], ACT.Copy).then_inc(S["oT_b1"], 1)
                if live(k, 1, T):
                    j, ju, _ = back(k, u, it, 1)
                    wait(act, S["mm_b1"], j + 1)
                    wait(act, S["pre_b1"], j - 1)
                    exp_minus(act, em[:, ju % 2, 0:1], pk[:, ju % 2, D:D + 1], S["cl_b1"], S["em_b1"], j)
                    act.activation(ring_c[:, ju % 2, :], pk[:, ju % 2, D + 1:2 * D + 1], ACT.Copy)\
                        .then_inc(S["xb_b1"], 1)
                if live(k, 2, T):
                    j, ju, _ = back(k, u, it, 2)
                    inv_std(act, mv[:, ju % 2, 0, 1:2], lv[:, ju % 2, 0:1], rs[:, ju % 2, 0:1],
                            S["mv_b1"], S["lv_b1"], S["rs_b1"], j)
            run_steps(act, T, 2, step_b1)

            def step_b2(k, u, it):
                if live(k, 0, G):
                    wait(act, S["t_d2"], k + 1)
                    wait(act, S["mm_d2"], k - 1)
                    act.activation(xgT[:, u % 2, :], pt[:, u % 2, :], ACT.Copy).then_inc(S["hT_d2"], 1)
                    wait(act, ring["hs_in"][u], 16 * (it + 1))
                    if isinstance(k, int):
                        ao, es = agg[:, :, k], ew_t[:, k:k + 1]
                    else:
                        ao, es = agg[:, :, bass.ds(k, 1)].rearrange("p f a -> p (f a)"), ew_t[:, bass.ds(k, 1)]
                    act.activation(ao, ring_a[:, u, :], ACT.Copy, scale=es).then_inc(S["agg_b2"], 1)
                if live(k, 2, G):
                    j, ju, _ = back(k, u, it, 2)
                    inv_std(act, mv[:, ju % 2, :, 1], lv[:, ju % 2, :], rs[:, ju % 2, :],
                            S["mv_d2"], S["lv_d2"], S["rs_d2"], j)
            run_steps(act, T, 2, step_b2)

            def step_c(k, u, it):
                if live(k, 0, T):
                    wait(act, S["t_c"], k + 1)
                    wait(act, S["mm_c"], k - 1)
                    act.activation(xgT[:, u % 2, 0:2 * P], pt[:, u % 2, 0:2 * P], ACT.Copy).then_inc(S["tc_c"], 1)
                if live(k, 2, T):
                    j, ju, _ = back(k, u, it, 2)
                    inv_std(act, mv[:, ju % 2, 0, 1:2], lv[:, ju % 2, 0:1], rs[:, ju % 2, 0:1],
                            S["mv_c"], S["lv_c"], S["rs_c"], j)
            run_steps(act, T, 2, step_c)

        @block.vector
        def _(dve):
            chain = [0]
            s_ch = sem("chain")

            def link(ins):
                chain[0] += 1
                ins.then_inc(s_ch, 1)
                dve.wait_ge(s_ch, chain[0])

            dve.memset(b_kvq[:, :], 0.0)
            dve.memset(brow, 0.0).then_inc(S["fills"], 1)
            dve.memset(pad_i[0:1, 0:P - 1], N)
            dve.memset(pad_i[0:1, P - 1:P], -1)
            dve.memset(zrows, 0.0).then_inc(S["padded"], 1)
            dve.memset(s_int, 0)
            dve.memset(ew_t[:, :], 0.0).then_inc(S["fills"], 1)
            dve.memset(eps_c[:, :], EPS)
            dve.memset(top_c[:, :], TOP)
            dve.memset(o3[:, :, :], 0.0)
            dve.memset(ring_e[:, :, :], 1.0)
            dve.memset(ones3[:, :], 1.0)
            link(dve.memset(ones_t[:, :], 1.0))
            dve.wait_ge(S["w_in"], 16 * 16)
            dve.tensor_copy(r_c[:, 0:D], m2n_w)
            dve.tensor_copy(r_o[:, D + 1:2 * D + 1], m2n_w)
            dve.tensor_scalar(r_o[:, 0:D], m2n_w, -1.0, None, ALU.mult)
            dve.tensor_tensor(r_o[:, D:D + 1], beta_w[:, 0:1], beta_w[:, 2:3], ALU.add)
            dve.tensor_tensor(r_c[:, D:D + 1], beta_w[:, 1:2], beta_w[:, 2:3], ALU.subtract).then_inc(S["wcopy"], 1)
            dve.wait_ge(S["wprod"], 5)
            link(dve.tensor_copy(brow[0:1, 0:D + 1], pd[0:1, 0, 0, 0:D + 1]))
            link(dve.tensor_copy(brow_b[0:1, 0, :], brow))
            link(dve.tensor_tensor(brow_r, brow, brow_b[0:1, 0, :], ALU.subtract))
            link(dve.tensor_copy(brow_b[0:1, 1, :], brow_r))
            link(dve.tensor_tensor(brow, brow_r, brow_b[0:1, 1, :], ALU.subtract))
            dve.tensor_copy(brow_b[0:1, 2, :], brow).then_inc(S["rows"], 1)
            dve.wait_ge(S["edge_in"], 7 * 16)
            for i in range(2):
                dve.tensor_copy(d_f[i], d_int[i])
            link(dve.tensor_copy(d_f[2], d_int[2]))
            dve.tensor_copy(gidx[:, :, 0], s_int)
            dve.tensor_scalar(clip, d_f[0], float(N - 1), None, ALU.min)
            dve.tensor_tensor(nend, d_f[0], d_f[2], ALU.is_equal)
            link(dve.tensor_tensor(same[:, :], d_f[0], d_f[1], ALU.is_equal))
            dve.tensor_copy(gidx[:, :, 1], clip)
            dve.tensor_scalar(far[:, :], same[:, :], -1.0, FAR, ALU.add, ALU.mult)
            link(dve.scalar_tensor_tensor(out=d_f[1], in0=nend, scalar=float(N), in1=d_f[0], op0=ALU.mult, op1=ALU.add))
            dve.tensor_copy(sidx[:, :], d_f[1])
            dve.tensor_tensor_scan(pfar[:, :], far[:, :], far[:, :], 0.0, ALU.min, ALU.min)\
                .then_inc(S["dsteps"], 1)
            dve.tensor_copy(em[:, 0, 0:1], ones_t[:, 0:1]).then_inc(S["wcopy"], 1)

            def row_stats(pieces, ju, n):
                for i in range(n):
                    ins = dve.bn_stats(stats[:, ju % 2, i, :], pieces(i))
                return ins

            def mean_var(ju, n):
                for i in range(n):
                    ins = dve.bn_aggr(mv[:, ju % 2, i, :], stats[:, ju % 2, i, :])
                return ins

            def normalise(to, pieces, ju, n):
                for i in range(n):
                    ins = dve.tensor_scalar(to(i), pieces(i), mv[:, ju % 2, i, 0:1], rs[:, ju % 2, i:i + 1],
                                            ALU.subtract, ALU.mult)
                return ins

            def step_a(k, u, it):
                if live(k, 1, T):
                    j, ju, _ = back(k, u, it, 1)
                    wait(dve, S["q_a"], j + 1)
                    dve.scalar_tensor_tensor(out=prod[:, ju % 2, :], in0=pk[:, ju % 2, 0:DM], scalar=QSCALE,
                                             in1=q_sb[:, ju % 2, :], op0=ALU.mult, op1=ALU.mult).then_inc(S["pr_a"], 1)
                    wait(dve, S["pr_a"], j + 1)
                    ao = alpha[:, :, j:j + 1] if isinstance(j, int) else alpha[:, :, bass.ds(j, 1)]
                    dve.reduce_sum(ao, prod[:, ju % 2, :].rearrange("p (h c) -> p h c", h=H), AX_X)\
                        .then_inc(S["al_a"], 1)
                if live(k, 0, T):
                    wait(dve, S["em_d1"], k + 1)
                    dve.tensor_scalar(ep[:, u % 2, :], em[:, u % 2, :], 1.0, None, ALU.add).then_inc(S["ep_d1"], 1)
                    wait(dve, S["ep_d1"], k + 1)
                    dve.reciprocal(beta[:, u % 2, :], ep[:, u % 2, :]).then_inc(S["be_d1"], 1)
                    wait(dve, S["be_d1"], k + 1)
                    wait(dve, ring["xg_in"][u], 16 * (it + 1))
                    wait(dve, S["out_d1"], k - 1)
                    for j in range(NJ):
                        ins = dve.scalar_tensor_tensor(
                            out=hpre[:, u % 2, j * D:(j + 1) * D], in0=pd[:, u % 2, j, 0:D],
                            scalar=beta[:, u % 2, j:j + 1], in1=xg[:, u, j * D:(j + 1) * D],
                            op0=ALU.mult, op1=ALU.add)
                    ins.then_inc(S["pre_d1"], 1)
                    wait(dve, S["pre_d1"], k + 1)
                    row_stats(lambda i: hpre[:, u % 2, i * D:(i + 1) * D], u, NJ).then_inc(S["bn_d1"], 1)
                    wait(dve, S["bn_d1"], k + 1)
                if live(k, 1, T):
                    j, ju, itj = back(k, u, it, 1)
                    wait(dve, S["rs_d1"], j + 1)
                    if live(j, 2, T):
                        _, su, sit = back(j, ju, itj, 2)
                        wait(dve, ring["h_st"][su], 16 * (sit + 1))
                    normalise(lambda i: hout[:, ju % 2, i * D:(i + 1) * D],
                              lambda i: hpre[:, ju % 2, i * D:(i + 1) * D], ju, NJ).then_inc(S["out_d1"], 1)
                if live(k, 0, T):
                    mean_var(u, NJ).then_inc(S["mv_d1"], 1)
            run_steps(dve, T, 1, step_a)

            dve.wait_ge(S["v_a"], T)
            dve.wait_ge(S["al_a"], T)
            for h in range(H):
                ins = dve.tensor_tensor_scan(rmax[:, h, 1:T + 1], far[:, :], alpha[:, h, :], -FAR, ALU.add, ALU.max)
            link(ins)
            dve.tensor_copy(sum_a[:, 0:H], rmax[:, :, T])
            dve.tensor_copy(sum_b[:, 0:H], pfar[:, T - 1:T].to_broadcast([P, H])).then_inc(S["sc"], 1)
            dve.wait_ge(S["sc_pe"], 1)
            dve.memset(cumT[0:H, 0:1], -FAR)
            link(dve.tensor_copy(keepT[0:H, :], pt[0:H, 0, P:2 * P]))
            dve.tensor_tensor_scan(cumT[0:H, 1:P + 1], keepT[0:H, :], pt[0:H, 0, 0:P], -FAR, ALU.add, ALU.max)\
                .then_inc(S["sc"], 1)
            dve.wait_ge(S["sc_pe"], 2)
            dve.tensor_copy(carm[:, :], pt[:, 1, 0:H])
            link(dve.tensor_copy(rmax[:, :, 0], pt[:, 1, 0:H]))
            for h in range(H):
                ins = dve.scalar_tensor_tensor(out=rmax[:, h, 1:T + 1], in0=pfar[:, :], scalar=carm[:, h:h + 1],
                                               in1=rmax[:, h, 1:T + 1], op0=ALU.add, op1=ALU.max)
            link(ins)
            dve.tensor_tensor(alpha[:, :, :], alpha[:, :, :], rmax[:, :, 1:T + 1], ALU.subtract)
            link(dve.tensor_tensor(decay[:, :, :], rmax[:, :, 0:T], rmax[:, :, 1:T + 1], ALU.subtract))
            dve.tensor_tensor(decay[:, :, :], decay[:, :, :],
                              far[:, :].rearrange("p (a t) -> p a t", a=1).to_broadcast([P, H, T]), ALU.add)\
                .then_inc(S["sc"], 1)
            dve.wait_ge(S["sc_act"], 1)
            for h in range(H):
                dve.tensor_tensor_scan(cdec[:, h, :], decay[:, h, :], ones_t[:, :], 1.0, ALU.mult, ALU.mult)
            dve.wait_ge(S["sc_act"], 2)
            for h in range(H):
                dve.tensor_tensor_scan(rden[:, h, :], decay[:, h, :], alpha[:, h, :], 0.0, ALU.mult, ALU.add)
            for h in range(H - 1):
                vh = val[:, h, :, :]
                ins = dve.tensor_tensor(vh, vh, alpha[:, h, :].rearrange("p (a t) -> p a t", a=1)
                                        .to_broadcast([P, C, T]), ALU.mult)
            link(ins)
            for h in range(H):
                if h == H - 1:
                    dve.wait_ge(S["sc_pool"], 1)
                for c in range(C):
                    ins = dve.tensor_tensor_scan(val[:, h, c, :], decay[:, h, :], val[:, h, c, :], 0.0, ALU.mult, ALU.add)
            link(ins)
            dve.tensor_copy(sum_a[:, 0:DM].rearrange("p (h c) -> p h c", h=H), val[:, :, :, T - 1])
            dve.tensor_copy(sum_a[:, DM:DM + H], rden[:, :, T - 1])
            dve.tensor_copy(sum_b[:, 0:DM].rearrange("p (h c) -> p h c", h=H),
                            cdec[:, :, T - 1:T].to_broadcast([P, H, C]))
            dve.tensor_copy(sum_b[:, DM:DM + H], cdec[:, :, T - 1]).then_inc(S["sc"], 1)
            dve.wait_ge(S["sc_pe"], 3)
            dve.memset(cumT[0:DM + H, 0:1], 0.0)
            link(dve.tensor_copy(keepT[0:DM + H, :], pt[0:DM + H, 0, P:2 * P]))
            dve.tensor_tensor_scan(cumT[0:DM + H, 1:P + 1], keepT[0:DM + H, :], pt[0:DM + H, 0, 0:P], 0.0,
                                   ALU.mult, ALU.add).then_inc(S["sc"], 1)
            dve.wait_ge(S["sc_pe"], 4)
            link(dve.tensor_copy(carn[:, :], pt[:, 1, 0:DM + H]))
            for h in range(H):
                ins = dve.scalar_tensor_tensor(out=rden[:, h, :], in0=cdec[:, h, :], scalar=carn[:, DM + h:DM + h + 1],
                                               in1=rden[:, h, :], op0=ALU.mult, op1=ALU.add)
            link(ins)
            link(dve.reciprocal(rden[:, :, :], rden[:, :, :]))
            dve.memset(em[:, 0, 0:1], 0.0).then_inc(S["sc"], 1)

            car_v = carn[:, 0:DM].rearrange("p (h c) -> p h c", h=H)

            def at(t3, k):
                a = t3[:, :, k:k + 1] if isinstance(k, int) else t3[:, :, bass.ds(k, 1)]
                return a.to_broadcast([P, H, C])

            def step_b1(k, u, it):
                if live(k, 0, T):
                    vk = val[:, :, :, k] if isinstance(k, int) else \
                        val[:, :, :, bass.ds(k, 1)].rearrange("p h c a -> p h (c a)")
                    dve.tensor_tensor(o1, at(cdec, k), car_v, ALU.mult).then_inc(S["o_b1"], 1)
                    wait(dve, S["o_b1"], 2 * k + 1)
                    dve.tensor_tensor(o2, o1, vk, ALU.add).then_inc(S["o_b1"], 1)
                    wait(dve, S["o_b1"], 2 * k + 2)
                    wait(dve, S["t_b1"], k - 1)
                    dve.tensor_tensor(o3[:, u % 2, 0:DM].rearrange("p (h c) -> p h c", h=H), o2,
                                      at(rden, k), ALU.mult).then_inc(S["os_b1"], 1)
                if live(k, 2, T):
                    j, ju, _ = back(k, u, it, 2)
                    wait(dve, S["em_b1"], j + 1)
                    dve.tensor_scalar(ep[:, ju % 2, 0:1], em[:, ju % 2, 0:1], 1.0, None, ALU.add)\
                        .then_inc(S["ep_b1"], 1)
                    wait(dve, S["ep_b1"], j + 1)
                    dve.reciprocal(beta[:, ju % 2, 0:1], ep[:, ju % 2, 0:1]).then_inc(S["be_b1"], 1)
                    wait(dve, S["be_b1"], j + 1)
                    wait(dve, S["xb_b1"], j + 1)
                    wait(dve, S["h_b1"], j - 1)
                    dve.scalar_tensor_tensor(out=ring_f[:, ju % 2, :], in0=pk[:, ju % 2, 0:D],
                                             scalar=beta[:, ju % 2, 0:1], in1=ring_c[:, ju % 2, :],
                                             op0=ALU.mult, op1=ALU.add).then_inc(S["pre_b1"], 1)
                    wait(dve, S["pre_b1"], j + 1)
                    row_stats(lambda i: ring_f[:, ju % 2, :], ju, 1).then_inc(S["bn_b1"], 1)
                    wait(dve, S["bn_b1"], j + 1)
                if live(k, 3, T):
                    j, ju, itj = back(k, u, it, 3)
                    wait(dve, S["rs_b1"], j + 1)
                    wait(dve, ring["h_sc"][ju], 16 * itj)
                    wait(dve, ring["hd_st"][ju], 16 * itj)
                    normalise(lambda i: ring_b[:, ju, :], lambda i: ring_f[:, ju % 2, :], ju, 1)\
                        .then_inc(S["h_b1"], 1)
                if live(k, 2, T):
                    mean_var(back(k, u, it, 2)[1], 1).then_inc(S["mv_b1"], 1)
            run_steps(dve, T, 3, step_b1)

            def step_b2(k, u, it):
                if live(k, 1, G):
                    j, ju, itj = back(k, u, it, 1)
                    wait(dve, S["out_d2"], j - 1)
                    wait(dve, S["mm_d2"], j + 1)
                    wait(dve, ring["hg_in"][ju], 16 * (itj + 1))
                    dve.scalar_tensor_tensor(out=hpre[:, ju % 2, :], in0=pk[:, ju % 2, :], scalar=0.0,
                                             in1=xg[:, ju, :], op0=ALU.max, op1=ALU.add).then_inc(S["u_d2"], 1)
                    wait(dve, S["u_d2"], j + 1)
                    row_stats(lambda i: hpre[:, ju % 2, i * D:(i + 1) * D], ju, NJ).then_inc(S["bn_d2"], 1)
                    wait(dve, S["bn_d2"], j + 1)
                if live(k, 2, G):
                    j, ju, itj = back(k, u, it, 2)
                    wait(dve, S["rs_d2"], j + 1)
                    if live(j, 2, G):
                        _, su, sit = back(j, ju, itj, 2)
                        wait(dve, ring["z_st"][su], 16 * (sit + 1))
                    else:
                        for q in range(U):
                            dve.wait_ge(ring["h_st"][q], last)
                    normalise(lambda i: hout[:, ju % 2, i * D:(i + 1) * D],
                              lambda i: hpre[:, ju % 2, i * D:(i + 1) * D], ju, NJ).then_inc(S["out_d2"], 1)
                if live(k, 1, G):
                    mean_var(back(k, u, it, 1)[1], NJ).then_inc(S["mv_d2"], 1)
            run_steps(dve, G, 2, step_b2)

            dve.tensor_tensor_scan(psame[:, :], same[:, :], ones_t[:, :], 1.0, ALU.mult, ALU.mult)
            dve.wait_ge(S["agg_b2"], T)
            for f in range(D):
                ins = dve.tensor_tensor_scan(agg[:, f, :], same[:, :], agg[:, f, :], 0.0, ALU.mult, ALU.add)
            link(ins)
            dve.tensor_copy(sum_a, agg[:, :, T - 1])
            dve.tensor_copy(sum_b, psame[:, T - 1:T].to_broadcast([P, D])).then_inc(S["sc"], 1)
            dve.wait_ge(S["sc_pe"], 5)
            dve.memset(cumT[:, 0:1], 0.0)
            link(dve.tensor_copy(keepT, pt[:, 0, P:2 * P]))
            dve.tensor_tensor_scan(cumT[:, 1:P + 1], keepT, pt[:, 0, 0:P], 0.0, ALU.mult, ALU.add)\
                .then_inc(S["sc"], 1)
            dve.wait_ge(S["sc_pe"], 6)
            link(dve.tensor_copy(carg, pt[:, 1, 0:D]))

            def step_c(k, u, it):
                if live(k, 0, T):
                    wait(dve, S["t_c"], k - 1)
                    if isinstance(k, int):
                        ak, sk = agg[:, :, k], psame[:, k:k + 1]
                    else:
                        ak, sk = agg[:, :, bass.ds(k, 1)].rearrange("p f a -> p (f a)"), psame[:, bass.ds(k, 1)]
                    dve.scalar_tensor_tensor(out=ring_d[:, u % 2, :], in0=carg, scalar=sk, in1=ak,
                                             op0=ALU.mult, op1=ALU.add).then_inc(S["ag_c"], 1)
                if live(k, 2, T):
                    j, ju, itj = back(k, u, it, 2)
                    wait(dve, S["z_c"], j - 1)
                    wait(dve, S["mm_c"], j + 1)
                    wait(dve, ring["hd_in"][ju], 16 * (itj + 1))
                    dve.scalar_tensor_tensor(out=ring_f[:, ju % 2, :], in0=pk[:, ju % 2, 0:D], scalar=0.0,
                                             in1=ring_a[:, ju, :], op0=ALU.max, op1=ALU.add).then_inc(S["u_c"], 1)
                    wait(dve, S["u_c"], j + 1)
                    row_stats(lambda i: ring_f[:, ju % 2, :], ju, 1).then_inc(S["bn_c"], 1)
                    wait(dve, S["bn_c"], j + 1)
                if live(k, 3, T):
                    j, ju, itj = back(k, u, it, 3)
                    wait(dve, S["rs_c"], j + 1)
                    wait(dve, ring["z_sc"][ju], 16 * itj)
                    normalise(lambda i: ring_b[:, ju, :], lambda i: ring_f[:, ju % 2, :], ju, 1)\
                        .then_inc(S["z_c"], 1)
                if live(k, 2, T):
                    mean_var(back(k, u, it, 2)[1], 1).then_inc(S["mv_c"], 1)
            run_steps(dve, T, 3, step_c)


_OUT = ((100000, 128), "float32")


def kernel(**inputs):
    import numpy as _np
    import concourse.bacc as _bacc
    from concourse import mybir as _mybir
    from concourse.bass_utils import run_bass_kernel_spmd as _run

    a = {k: _np.ascontiguousarray(v) for k, v in inputs.items()}
    x = a["x"]
    n = x.shape[0]
    whole = n // GN
    groups = _np.concatenate([x[:whole * GN], x[n - GN:]]).reshape(whole + 1, P, NJ, D)
    row = lambda v: v.reshape(1, -1)
    arrays = {
        "x": x, "xT": _np.ascontiguousarray(groups.transpose(0, 3, 2, 1).reshape(whole + 1, D, GN)),
        "src": row(a["src"]), "dst": row(a["dst"]), "ea": a["edge_attr_50"], "ew": row(a["edge_weight"]),
        "w_n2mT": _np.ascontiguousarray(a["L0_gnn_W_n2m"].T), "w_edgeT": _np.ascontiguousarray(a["L0_gnn_W_edge"].T),
        "w_q": a["L0_gnn_W_q"], "b_q": row(a["L0_gnn_b_q"]), "w_k": a["L0_gnn_W_k"], "b_k": row(a["L0_gnn_b_k"]),
        "w_v": a["L0_gnn_W_v"], "b_v": row(a["L0_gnn_b_v"]), "w_e": a["L0_gnn_W_e"], "w_skip": a["L0_gnn_W_skip"],
        "b_skip": a["L0_gnn_b_skip"].reshape(-1, 1),
        "w_beta": _np.ascontiguousarray(a["L0_gnn_W_beta"].reshape(3, DM).T), "w_m2n": a["L0_gnn_W_m2n"],
        "w_1": a["L1_gnn_w1"], "w_2": a["L1_gnn_w2"], "b_1": row(a["L1_gnn_b"]),
    }
    nc = _bacc.Bacc("TRN2", target_bir_lowering=False, num_devices=1)
    args = {k: nc.dram_tensor(f"in_{k}", v.shape, _mybir.dt.from_np(v.dtype), kind="ExternalInput").ap()
            for k, v in arrays.items()}
    out = nc.dram_tensor("out_z", _OUT[0], _mybir.dt.from_np(_np.dtype(_OUT[1])), kind="ExternalOutput").ap()
    gnn_kernel(nc, out=out, **args)
    r = _run(nc, [{f"in_{k}": v for k, v in arrays.items()}], core_ids=[0])
    return r.results[0]["out_z"]
```

```python
from contextlib import ExitStack

import concourse.bass as bass
from concourse import mybir

F32 = mybir.dt.float32
BF16 = mybir.dt.bfloat16
I32 = mybir.dt.int32
ALU = mybir.AluOpType
ACT = mybir.ActivationFunctionType
AX_X = mybir.AxisListType.X

P = 128
D = 128
DM = 64
R = 50
H = 4
C = DM // H
NJ = 4
GN = NJ * P
U = 4
EPS = 1e-5
FAR = 1e38
TOP = 88.0
NA = 3
QSCALE = 1.0 / C ** 0.5


def wait(eng, sem, value):
    if not (isinstance(value, int) and value <= 0):
        eng.wait_ge(sem, value)


def live(k, lag, n):
    return not isinstance(k, int) or 0 <= k - lag < n


def back(k, u, it, lag):
    return k - lag, (u - lag) % U, it + (u - lag) // U


def run_steps(eng, n, lag, step):
    for u in range(U):
        step(u, u, 0)
    with eng.Fori(1, n // U - 1) as it:
        for u in range(U):
            step(it * U + u, u, it)
    for k in range(n - U, n + lag):
        step(k, k % U, k // U)


def gnn_kernel(nc, x, xT, src, dst, ea, ew, w_n2mT, w_edgeT, w_q, b_q, w_k, b_k, w_v, b_v,
               w_e, w_skip, b_skip, w_beta, w_m2n, w_1, w_2, b_1, out):
    N = x.shape[0]
    E = src.shape[1]
    T = -(-E // (P * U)) * U
    EP = P * T
    G = -(-N // (GN * U)) * U
    assert G == T and G * GN - N < GN and EP - E < T
    VLAST = T - (EP - E)

    h_tab = nc.dram_tensor("h_tab", (N, D), F32, kind="Internal").ap()
    hd_scr = nc.dram_tensor("hd_scr", (T, P, D), F32, kind="Internal").ap()
    dst_tab = nc.dram_tensor("dst_s", (EP + 2, 1), I32, kind="Internal").ap()
    ea_s = nc.dram_tensor("ea_s", (EP, R), F32, kind="Internal").ap()
    ea_t = ea_s.rearrange("(p t) r -> p t r", p=P)
    src_tab = nc.dram_tensor("src_s", (E, 1), I32, kind="Internal").ap()
    ew_tab = nc.dram_tensor("ew_s", (E, 1), F32, kind="Internal").ap()
    dst_s, src_s, ew_s = (tab.rearrange("n a -> a n") for tab in (dst_tab, src_tab, ew_tab))

    with ExitStack() as ctx:
        def sb(name, shape, dt=F32):
            return ctx.enter_context(nc.sbuf_tensor(name, shape, dt))

        def sem(name):
            return ctx.enter_context(nc.semaphore(name))

        pt = ctx.enter_context(nc.psum_tensor("pt", [P, 2, 512], F32))
        pk = ctx.enter_context(nc.psum_tensor("pk", [P, 2, 512], F32))
        pd = ctx.enter_context(nc.psum_tensor("pd", [P, 2, NJ, 256], F32))

        big = sb("big", [P, D * T])
        xdT_all = big[:, :].rearrange("p (t n) -> p t n", t=T)
        agg = big[:, :].rearrange("p (f t) -> p f t", t=T)
        val = sb("val", [P, H, C, T])
        alpha = sb("alpha", [P, H, T])
        scan_buf = sb("scan_buf", [P, H * (4 * T + 1)])

        def scan_part(first, n):
            return scan_buf[:, H * first:H * (first + n)].rearrange("p (h t) -> p h t", h=H)
        rmax = scan_part(0, T + 1)
        decay = scan_part(T + 1, T)
        cdec = scan_part(2 * T + 1, T)
        rden = scan_part(3 * T + 1, T)
        same = sb("same", [P, T])
        far = sb("far", [P, T])
        pfar = sb("pfar", [P, T])
        psame = pfar
        ones_t = sb("ones_t", [P, T])
        ew_t = sb("ew_t", [P, T])
        gidx = sb("gidx", [P, T, 2], I32)
        sidx = sb("sidx", [P, T], I32)

        ring_a = sb("ring_a", [P, U, D])
        ring_b = sb("ring_b", [P, U, D])
        pair = sb("pair", [P, 2, 2 * D])
        ring_d = pair[:, :, 0:D]
        ring_c = pair[:, :, D:2 * D]
        ring_e = sb("ring_e", [P, 2, D])
        ring_f = ring_e
        ea_in = sb("ea_in", [P, U, R])
        q_sb = sb("q_sb", [P, 2, DM])
        prod = sb("prod", [P, 2, DM])
        o1, o2 = (prod[:, i, :].rearrange("p (h c) -> p h c", h=H) for i in range(2))
        o3 = sb("o3", [P, 2, P])
        xg = sb("xg", [P, U, GN])
        xgT = scan_buf[:, 0:U * GN].rearrange("p (u n) -> p u n", u=U)
        hpre = sb("hpre", [P, U, GN])
        hout_own = sb("hout", [P, 2, GN])
        hout = [hout_own[:, 0, :], hout_own[:, 1, :],
                scan_buf[:, U * GN:(U + 1) * GN], scan_buf[:, (U + 1) * GN:(U + 2) * GN]]
        idx2 = sb("idx2", [P, U, 2], I32)
        em = sb("em", [P, 2, NJ])
        ep = sb("ep", [P, 2, NJ])
        beta = sb("beta", [P, 2, NJ])
        stats = sb("stats", [P, U, NJ, 6])
        mv = sb("mv", [P, U, NJ, 2])
        lv = sb("lv", [P, U, NJ])
        rs = sb("rs", [P, U, NJ])
        nb = sb("nb", [P, U, NJ])

        ident = sb("ident", [P, P])
        a_kv = sb("a_kv", [P, 2 * DM])
        a_q = sb("a_q", [P, DM])
        b_kvq = sb("b_kvq", [P, 3 * DM])
        w_sx = sb("w_sx", [P, 2 * D + 1])
        r_o = sb("r_o", [DM, 2 * D + 1])
        r_c = sb("r_c", [DM, D + 1])
        ones3 = sb("ones3", [P, P], BF16)
        bias3 = sb("bias3", [P, 3 * D + 1], BF16)
        w1_sb = sb("w1_sb", [P, D])
        w2_sb = sb("w2_sb", [P, D])
        n2mT = hpre[0:DM, 0, 0:D]
        kvq_w = hpre[0:DM, 0, D:D + 3 * DM]
        e_w = hpre[0:DM, 0, 320:384]
        skip_w = hpre[0:DM, 0, 384:448]
        edgeT = hpre[0:DM, 0, 448:448 + R]
        m2n_w = hpre[0:DM, 1, 0:D]
        beta_w = hpre[0:DM, 1, 128:131]
        bskip = hpre[0:DM, 1, 132:133]
        wnsT = hpre[0:DM, 1, 136:264]
        brow = hout_own[0:1, 0, 0:3 * D + 1]
        brow_r = hout_own[0:1, 1, 0:3 * D + 1]
        brow_b = val[0:1, 0, :, :].rearrange("p c t -> p (c t)")[:, 0:1200].bitcast(BF16)\
            .rearrange("p (i n) -> p i n", i=3)[:, :, 0:3 * D + 1]
        d_int = [val[:, 1, c, :].bitcast(I32) for c in range(3)]
        s_int = val[:, 1, 3, :].bitcast(I32)
        d_f = [val[:, 1, 4 + c, :] for c in range(3)]
        nend = val[:, 1, 7, :]
        clip = val[:, 1, 8, :]
        pad_i = val[0:1, 1, 9, 0:P].bitcast(I32)
        zrows = big[0:EP - E, 0:R]
        dst_all = big[:, 0:EP]
        CH = EP // 8
        jrow = val[:, 2, :, :].rearrange("p c t -> p (c t)")[:, 0:CH]
        hits = val[:, 3, :, :].rearrange("p c t -> p (c t)")[:, 0:CH]
        eidx, rank, part = alpha[:, 0, :], alpha[:, 1, :], alpha[:, 2, :]
        rank_i = alpha[:, 0, :].bitcast(I32)
        rank1_i = alpha[:, 3, :].bitcast(I32)
        drop = val[:, 1, 10, :]
        drop_p = val[:, 1, 11, 0:1]
        drop_row = val[0:1, 1, 12, 0:P]
        drop_i = val[0:1, 1, 13, 0:1].bitcast(I32)
        one_dst, one_src, one_ew = (q_sb[:, 0, i:i + 1] for i in range(3))
        sum_a = hpre[:, 0, 0:D]
        sum_b = hpre[:, 0, D:2 * D]
        keepT = hpre[:, 0, 2 * D:3 * D]
        cumT = hpre[:, 1, 0:P + 1]
        carm = sb("carm", [P, H])
        carn = sb("carn", [P, DM + H])
        carg = rden[:, 0, 0:D]

        S = {n: sem(n) for n in (
            "w_in", "pad_in", "edge_in", "edge_in2", "padded", "id0", "id1", "fills", "gp_fill", "wprod", "wcopy",
            "rows", "rows_in", "dsteps", "issued", "drops", "drop_in", "checked", "ordered",
            "g_all", "g_iota", "g_rank", "ranked", "g_one", "g_ea", "g_out", "g_back",
            "idx_a", "t_a", "xsT_a", "kv_a", "q_a", "v_a", "pr_a", "al_a",
            "mm_d1", "cl_d1", "em_d1", "ep_d1", "be_d1", "pre_d1", "bn_d1", "mv_d1", "lv_d1", "rs_d1", "out_d1", "na_d1",
            "sc", "sc_pe", "sc_act", "sc_pool",
            "o_b1", "os_b1", "t_b1", "oT_b1", "mm_b1", "cl_b1", "em_b1", "xb_b1", "ep_b1", "be_b1", "pre_b1", "bn_b1",
            "mv_b1", "lv_b1", "rs_b1", "h_b1", "idx_b1",
            "idx_b2", "agg_b2", "t_d2", "hT_d2", "mm_d2", "u_d2", "bn_d2", "mv_d2", "lv_d2", "rs_d2", "out_d2", "na_d2",
            "ag_c", "t_c", "tc_c", "mm_c", "u_c", "bn_c", "mv_c", "lv_c", "rs_c", "z_c", "idx_c")}
        ring = {n: [sem(f"{n}{u}") for u in range(U)] for n in (
            "xs_in", "xd_in", "ea_in", "xg_in", "xgT_in", "xdT_mv", "h_st",
            "xl_in", "hd_st", "h_sc", "hs_in", "hg_in", "z_st", "hd_in", "z_sc")}
        last = T // U * 16

        n0 = N - GN

        def node0(g):
            return n0 if isinstance(g, int) and g == G - 1 else g * GN

        def rows_of(tab, g):
            b = node0(g)
            if isinstance(b, int):
                return tab[b:b + GN, :].rearrange("(p j) f -> p (j f)", j=NJ)
            return tab[bass.ds(b, GN), :].rearrange("(p j) f -> p (j f)", j=NJ)

        block = ctx.enter_context(nc.Block())

        @block.sync
        def _(sp):
            loads = [(n2mT, w_n2mT), (kvq_w[:, 0:DM], w_k), (kvq_w[:, DM:2 * DM], w_v),
                     (kvq_w[:, 2 * DM:3 * DM], w_q), (e_w, w_e), (skip_w, w_skip), (edgeT, w_edgeT),
                     (m2n_w, w_m2n), (beta_w, w_beta), (bskip, b_skip), (w1_sb[:, :], w_1), (w2_sb[:, :], w_2),
                     (b_kvq[R:R + 1, 0:DM], b_k), (b_kvq[R:R + 1, DM:2 * DM], b_v),
                     (b_kvq[R:R + 1, 2 * DM:3 * DM], b_q)]
            sp.wait_ge(S["fills"], 1)
            for to, of in loads:
                sp.dma_start(to, of).then_inc(S["w_in"], 16)
            sp.dma_start(brow[0:1, 2 * D + 1:3 * D + 1], b_1).then_inc(S["w_in"], 16)
            sp.wait_ge(S["padded"], 1)
            sp.dma_start(dst_s[0:1, 0:1], pad_i[0:1, P - 1:P]).then_inc(S["pad_in"], 16)
            sp.dma_start(dst_s[0:1, 1:E + 1], dst).then_inc(S["pad_in"], 16)
            sp.dma_start(dst_s[0:1, E + 1:EP + 2], pad_i[0:1, 0:EP + 1 - E]).then_inc(S["pad_in"], 16)
            sp.dma_start(ea_s[0:E, :], ea).then_inc(S["pad_in"], 16)
            sp.dma_start(ea_s[E:EP, :], zrows).then_inc(S["pad_in"], 16)
            sp.wait_ge(S["fills"], 2)
            sp.dma_start(s_int[0:P - 1, :], src[0:1, 0:(P - 1) * T].rearrange("a (p t) -> (a p) t", t=T))\
                .then_inc(S["edge_in"], 16)
            sp.dma_start(s_int[P - 1:P, 0:VLAST], src[0:1, (P - 1) * T:E]).then_inc(S["edge_in"], 16)
            sp.dma_start(ew_t[0:P - 1, :], ew[0:1, 0:(P - 1) * T].rearrange("a (p t) -> (a p) t", t=T))\
                .then_inc(S["edge_in"], 16)
            sp.dma_start(ew_t[P - 1:P, 0:VLAST], ew[0:1, (P - 1) * T:E]).then_inc(S["edge_in"], 16)
            sp.wait_ge(S["pad_in"], 5 * 16)
            for i, shift in enumerate((1, 0, 2)):
                sp.dma_start(d_int[i], dst_s[0:1, shift:shift + EP].rearrange("a (p t) -> (a p) t", t=T))\
                    .then_inc(S["edge_in"], 16)
            sp.wait_ge(S["drops"], 1)
            sp.dma_start(drop_row, drop_p).then_inc(S["drop_in"], 16)
            sp.wait_ge(S["rows"], 1)
            for i in range(3):
                sp.dma_start(bias3[i:i + 1, :], brow_b[0:1, i, :]).then_inc(S["rows_in"], 16)
            sp.wait_ge(S["ordered"], 1)

            def step_a(k, u, it):
                if live(k, 0, T):
                    wait(sp, S["t_a"], k - U + 1)
                    sp.dma_start(ea_in[:, u, :], ea_t[:, k, :] if isinstance(k, int)
                                 else ea_t[:, bass.ds(k, 1), :].rearrange("p a r -> p (a r)"))\
                        .then_inc(ring["ea_in"][u], 16)
                    wait(sp, S["pre_d1"], k - U + 1)
                    sp.dma_start(xg[:, u, :], rows_of(x, k)).then_inc(ring["xg_in"][u], 16)
                    wait(sp, S["mm_d1"], k - U + 1)
                    sp.dma_start(xgT[:, u, :], xT[k, :, :] if isinstance(k, int)
                                 else xT[bass.ds(k, 1), :, :].rearrange("a p n -> (a p) n"))\
                        .then_inc(ring["xgT_in"][u], 16)
            run_steps(sp, T, 0, step_a)

            for q in range(U):
                sp.wait_ge(ring["xdT_mv"][q], last)

            def step_b1(k, u, it):
                if live(k, 0, T):
                    if isinstance(k, int) and k < U:
                        sp.wait_ge(S["t_a"], T)
                    wait(sp, S["mm_b1"], k - U + 1)
                    sp.dma_start(ring_a[:, u, :], xdT_all[:, k, :] if isinstance(k, int)
                                 else xdT_all[:, bass.ds(k, 1), :].rearrange("p a n -> p (a n)"))\
                        .then_inc(ring["xl_in"][u], 16)
                if live(k, 3, T):
                    j, ju, _ = back(k, u, it, 3)
                    wait(sp, S["h_b1"], j + 1)
                    sp.dma_start(hd_scr[j, :, :] if isinstance(j, int)
                                 else hd_scr[bass.ds(j, 1), :, :].rearrange("a p n -> (a p) n"),
                                 ring_b[:, ju, :]).then_inc(ring["hd_st"][ju], 16)
            run_steps(sp, T, 3, step_b1)

            def step_b2(k, u, it):
                if live(k, 0, G):
                    wait(sp, S["u_d2"], k - U + 1)
                    sp.dma_start(xg[:, u, :], rows_of(h_tab, k)).then_inc(ring["hg_in"][u], 16)
            for q in range(U):
                sp.wait_ge(ring["h_sc"][q], last)
                sp.wait_ge(ring["hd_st"][q], last)
            run_steps(sp, G, 0, step_b2)

            def step_c(k, u, it):
                if live(k, 0, T):
                    wait(sp, S["u_c"], k - U + 1)
                    sp.dma_start(ring_a[:, u, :], hd_scr[k, :, :] if isinstance(k, int)
                                 else hd_scr[bass.ds(k, 1), :, :].rearrange("a p n -> (a p) n"))\
                        .then_inc(ring["hd_in"][u], 16)
            sp.wait_ge(S["agg_b2"], T)
            run_steps(sp, T, 0, step_c)
            for q in range(U):
                sp.wait_ge(ring["z_st"][q], last)
                sp.wait_ge(ring["z_sc"][q], last)

        @block.gpsimd
        def _(gp):
            gp.memset(ident[:, :], 0.0).then_inc(S["id0"], 1)
            gp.wait_ge(S["id0"], 1)
            gp.affine_select(out=ident[:, :], in_=ident[:, :], compare_op=ALU.not_equal, fill=1.0, base=0,
                             pattern=[[-1, P]], channel_multiplier=1).then_inc(S["id1"], 1)
            gp.wait_ge(S["checked"], 1)
            unsorted = gp.value_load(drop_i, min_val=0, max_val=1)
            with gp.If(unsorted > 0):
                gp.dma_start(dst_all.bitcast(I32), dst_s[0:1, 1:EP + 1].to_broadcast([P, EP])).then_inc(S["g_all"], 16)
                gp.iota(jrow.bitcast(I32), [[1, CH]], base=0, channel_multiplier=0).then_inc(S["g_iota"], 1)
                gp.iota(eidx.bitcast(I32), [[1, T]], base=0, channel_multiplier=T).then_inc(S["g_iota"], 1)
                gp.memset(ea_in[:, 0, :], 0.0).then_inc(S["g_one"], 1)
                gp.wait_ge(S["g_one"], 1)
                gp.wait_ge(S["ranked"], 1)
                top_edge, top_place = gp.to_reg(E - 1), gp.to_reg(E)

                def send(t, last_row, seen):
                    col = lambda a: a[:, bass.ds(t, 1)]
                    gp.dma_start(ea_in[0:P - 1, 0, :], ea[0:(P - 1) * T, :].rearrange("(p t) r -> p t r", t=T)
                                 [:, bass.ds(t, 1), :].rearrange("p a r -> p (a r)")).then_inc(S["g_ea"], 16)
                    if last_row:
                        gp.dma_start(ea_in[P - 1:P, 0, :], ea[bass.ds(t + (P - 1) * T, 1), :]).then_inc(S["g_ea"], 16)
                    gp.tensor_copy(idx2[:, 0, 0:1], col(rank_i)).then_inc(S["g_one"], 1)
                    gp.tensor_copy(idx2[:, 0, 1:2], col(rank1_i)).then_inc(S["g_one"], 1)
                    gp.tensor_copy(one_dst.bitcast(I32), col(d_int[0])).then_inc(S["g_one"], 1)
                    gp.tensor_copy(one_src.bitcast(I32), col(s_int)).then_inc(S["g_one"], 1)
                    gp.tensor_copy(one_ew, col(ew_t)).then_inc(S["g_one"], 1)
                    gp.wait_ge(S["g_one"], 1 + 5 * (t + 1))
                    gp.wait_ge(S["g_ea"], seen + (32 if last_row else 16))
                    gp.sem_inc(S["issued"], 1)
                    for tab, one, i, top in ((src_tab[:, :], one_src.bitcast(I32), 0, top_edge),
                                             (ew_tab[:, :], one_ew, 0, top_edge),
                                             (ea_s[:, :], ea_in[:, 0, :], 0, top_edge),
                                             (dst_tab[:, :], one_dst.bitcast(I32), 1, top_place)):
                        gp.indirect_dma_start(out=tab, in_=one, in_offset=None, bounds_check=top, oob_is_err=False,
                                              out_offset=bass.IndirectOffsetOnAxis(ap=idx2[:, 0, i:i + 1], axis=0))\
                            .then_inc(S["g_out"], 16)
                    gp.wait_ge(S["g_out"], 64 * (t + 1))

                with gp.Fori(0, VLAST) as t:
                    send(t, True, 32 * t)
                with gp.Fori(VLAST, T) as t:
                    send(t, False, 16 * t + 16 * VLAST)
                gp.dma_start(s_int[0:P - 1, :], src_s[0:1, 0:(P - 1) * T].rearrange("a (p t) -> (a p) t", t=T))\
                    .then_inc(S["g_back"], 16)
                gp.dma_start(s_int[P - 1:P, 0:VLAST], src_s[0:1, (P - 1) * T:E]).then_inc(S["g_back"], 16)
                gp.dma_start(ew_t[0:P - 1, :], ew_s[0:1, 0:(P - 1) * T].rearrange("a (p t) -> (a p) t", t=T))\
                    .then_inc(S["g_back"], 16)
                gp.dma_start(ew_t[P - 1:P, 0:VLAST], ew_s[0:1, (P - 1) * T:E]).then_inc(S["g_back"], 16)
                for i, shift in enumerate((1, 0, 2)):
                    gp.dma_start(d_int[i], dst_s[0:1, shift:shift + EP].rearrange("a (p t) -> (a p) t", t=T))\
                        .then_inc(S["g_back"], 16)
                gp.wait_ge(S["g_back"], 7 * 16)
            gp.sem_inc(S["ordered"], 1)
            gp.wait_ge(S["dsteps"], 1)
            top_row = gp.to_reg(N - 1)

            def step_a(k, u, it):
                wait(gp, S["t_a"], k - U + 1)
                gp.tensor_copy(idx2[:, u, :], gidx[:, k, :] if isinstance(k, int)
                               else gidx[:, bass.ds(k, 1), :].rearrange("p a i -> p (a i)"))\
                    .then_inc(S["idx_a"], 1)
                wait(gp, S["idx_a"], k + 1)
                gp.sem_inc(S["issued"], 1)
                for i, (rg, s) in enumerate(((ring_a, "xs_in"), (ring_b, "xd_in"))):
                    gp.indirect_dma_start(out=rg[:, u, :], out_offset=None, in_=x[:, :],
                                          in_offset=bass.IndirectOffsetOnAxis(ap=idx2[:, u, i:i + 1], axis=0))\
                        .then_inc(ring[s][u], 16)
            run_steps(gp, T, 0, step_a)

            gp.wait_ge(S["sc_act"], 2)
            vh = val[:, H - 1, :, :]
            gp.tensor_tensor(vh, vh, alpha[:, H - 1, :].rearrange("p (a t) -> p a t", a=1).to_broadcast([P, C, T]),
                             ALU.mult).then_inc(S["sc_pool"], 1)

            for q in range(U):
                gp.wait_ge(ring["h_st"][q], last)

            def step_b1(k, u, it):
                wait(gp, ring["h_sc"][u], 16 * it)
                gp.tensor_copy(idx2[:, u, 0:1], sidx[:, k:k + 1] if isinstance(k, int)
                               else sidx[:, bass.ds(k, 1)]).then_inc(S["idx_b1"], 1)
                wait(gp, S["idx_b1"], k + 1)
                wait(gp, S["h_b1"], k + 1)
                gp.sem_inc(S["issued"], 1)
                gp.indirect_dma_start(out=h_tab[:, :],
                                      out_offset=bass.IndirectOffsetOnAxis(ap=idx2[:, u, 0:1], axis=0),
                                      in_=ring_b[:, u, :], in_offset=None, bounds_check=top_row,
                                      oob_is_err=False).then_inc(ring["h_sc"][u], 16)
            run_steps(gp, T, 0, step_b1)
            for q in range(U):
                gp.wait_ge(ring["h_sc"][q], last)

            def step_b2(k, u, it):
                if isinstance(k, int) and k < U:
                    gp.wait_ge(S["mm_b1"], T)
                wait(gp, S["agg_b2"], k - U + 1)
                gp.tensor_copy(idx2[:, u, 0:1], gidx[:, k, 0:1] if isinstance(k, int)
                               else gidx[:, bass.ds(k, 1), 0:1].rearrange("p a i -> p (a i)"))\
                    .then_inc(S["idx_b2"], 1)
                wait(gp, S["idx_b2"], k + 1)
                gp.sem_inc(S["issued"], 1)
                gp.indirect_dma_start(out=ring_a[:, u, :], out_offset=None, in_=h_tab[:, :],
                                      in_offset=bass.IndirectOffsetOnAxis(ap=idx2[:, u, 0:1], axis=0))\
                    .then_inc(ring["hs_in"][u], 16)
            run_steps(gp, T, 0, step_b2)
            for q in range(U):
                gp.wait_ge(ring["z_st"][q], last)
                gp.wait_ge(ring["hs_in"][q], last)

            def step_c(k, u, it):
                wait(gp, ring["z_sc"][u], 16 * it)
                gp.tensor_copy(idx2[:, u, 0:1], sidx[:, k:k + 1] if isinstance(k, int)
                               else sidx[:, bass.ds(k, 1)]).then_inc(S["idx_c"], 1)
                wait(gp, S["idx_c"], k + 1)
                wait(gp, S["z_c"], k + 1)
                gp.sem_inc(S["issued"], 1)
                gp.indirect_dma_start(out=out[:, :],
                                      out_offset=bass.IndirectOffsetOnAxis(ap=idx2[:, u, 0:1], axis=0),
                                      in_=ring_b[:, u, :], in_offset=None, bounds_check=top_row,
                                      oob_is_err=False).then_inc(ring["z_sc"][u], 16)
            run_steps(gp, T, 0, step_c)

        @block.tensor
        def _(pe):
            pe.wait_ge(S["w_in"], 16 * 16)
            pe.matmul(pk[:, 0, 0:3 * DM], n2mT, kvq_w, start=True, stop=True).then_inc(S["wprod"], 1)
            pe.matmul(pk[0:R, 1, 0:DM], edgeT, e_w, start=True, stop=True).then_inc(S["wprod"], 1)
            pe.matmul(pt[0:DM, 0, 0:P], skip_w, n2mT, start=True, stop=True).then_inc(S["wprod"], 1)
            pe.wait_ge(S["wcopy"], 2)
            pe.matmul(pt[:, 1, 0:D + 1], wnsT, r_c[:, :], start=True, stop=True).then_inc(S["wprod"], 1)
            pe.matmul(pd[0:1, 0, 0, 0:D + 1], bskip, r_c[:, :], start=True, stop=True).then_inc(S["wprod"], 1)
            pe.wait_ge(S["wcopy"], 5)
            pe.wait_ge(S["rows_in"], 3 * 16)
            pe.wait_ge(S["id1"], 1)

            def step_a(k, u, it):
                if live(k, 1, T):
                    j, ju, _ = back(k, u, it, 1)
                    wait(pe, S["xsT_a"], j + 1)
                    wait(pe, S["v_a"], j - 1)
                    wait(pe, S["pr_a"], j - 1)
                    pe.matmul(pk[:, ju % 2, 0:3 * DM], ring_e[:, ju % 2, :], b_kvq[:, :], start=True, stop=False)
                    pe.matmul(pk[:, ju % 2, 0:2 * DM], ring_d[:, ju % 2, :], a_kv[:, :], start=False, stop=False)
                    pe.matmul(pk[:, ju % 2, 2 * DM:3 * DM], ring_c[:, ju % 2, :], a_q[:, :], start=False, stop=True)\
                        .then_inc(S["kv_a"], 1)
                if live(k, 0, T):
                    wait(pe, ring["xs_in"][u], 16 * (it + 1))
                    wait(pe, ring["xd_in"][u], 16 * (it + 1))
                    wait(pe, ring["ea_in"][u], 16 * (it + 1))
                    wait(pe, S["xsT_a"], k - 1)
                    pe.transpose(pt[:, u % 2, 0:P], ring_a[:, u, :], ident[:, :])
                    pe.transpose(pt[:, u % 2, P:2 * P], ring_b[:, u, :], ident[:, :])
                    pe.transpose(pt[0:R, u % 2, 2 * P:3 * P], ea_in[:, u, :], ident[:, :]).then_inc(S["t_a"], 1)
                    wait(pe, ring["xgT_in"][u], 16 * (it + 1))
                    wait(pe, S["pre_d1"], k - 1)
                    for j in range(NJ):
                        o = pd[:, u % 2, j, 0:D + 1]
                        pe.matmul(o, ones3[:, :], bias3[:, 0:D + 1], start=True, stop=False)
                        mm = pe.matmul(o, xgT[:, u, j * P:(j + 1) * P], w_sx[:, 0:D + 1],
                                       start=False, stop=True)
                    mm.then_inc(S["mm_d1"], 1)
            run_steps(pe, T, 1, step_a)

            pe.wait_ge(S["sc"], 1)
            pe.transpose(pt[0:H, 0, 0:P], sum_a[:, 0:H], ident[:, :])
            pe.transpose(pt[0:H, 0, P:2 * P], sum_b[:, 0:H], ident[:, :]).then_inc(S["sc_pe"], 1)
            pe.wait_ge(S["sc"], 2)
            pe.transpose(pt[:, 1, 0:H], cumT[0:H, 0:P], ident[0:H, 0:H]).then_inc(S["sc_pe"], 1)
            pe.wait_ge(S["sc"], 4)
            pe.transpose(pt[0:DM + H, 0, 0:P], sum_a[:, 0:DM + H], ident[:, :])
            pe.transpose(pt[0:DM + H, 0, P:2 * P], sum_b[:, 0:DM + H], ident[:, :]).then_inc(S["sc_pe"], 1)
            pe.wait_ge(S["sc"], 5)
            pe.transpose(pt[:, 1, 0:DM + H], cumT[0:DM + H, 0:P], ident[0:DM + H, 0:DM + H]).then_inc(S["sc_pe"], 1)

            def step_b1(k, u, it):
                if live(k, 0, T):
                    wait(pe, S["os_b1"], k + 1)
                    wait(pe, S["oT_b1"], k - 1)
                    if isinstance(k, int) and k < 2:
                        pe.wait_ge(S["sc"], 6)
                    pe.transpose(pt[:, u % 2, 0:P], o3[:, u % 2, :], ident[:, :]).then_inc(S["t_b1"], 1)
                if live(k, 1, T):
                    j, ju, itj = back(k, u, it, 1)
                    wait(pe, ring["xl_in"][ju], 16 * (itj + 1))
                    wait(pe, S["oT_b1"], j + 1)
                    wait(pe, S["pre_b1"], j - 1)
                    o = pk[:, ju % 2, 0:2 * D + 1]
                    pe.matmul(o, ones3[:, :], bias3[:, 0:2 * D + 1], start=True, stop=False)
                    pe.matmul(o, ring_a[:, ju, :], w_sx[:, :], start=False, stop=False)
                    pe.matmul(o, ring_d[0:DM, ju % 2, :], r_o[:, :], start=False, stop=True)\
                        .then_inc(S["mm_b1"], 1)
            run_steps(pe, T, 1, step_b1)
            pe.wait_ge(S["pre_b1"], T)

            def step_b2(k, u, it):
                if live(k, 0, G):
                    wait(pe, ring["hg_in"][u], 16 * (it + 1))
                    wait(pe, S["hT_d2"], k - 1)
                    for j in range(NJ):
                        mm = pe.transpose(pt[:, u % 2, j * P:(j + 1) * P], xg[:, u, j * D:(j + 1) * D], ident[:, :])
                    mm.then_inc(S["t_d2"], 1)
                if live(k, 1, G):
                    g, gu, _ = back(k, u, it, 1)
                    wait(pe, S["hT_d2"], g + 1)
                    wait(pe, S["u_d2"], g - 1)
                    for j in range(NJ):
                        o = pk[:, gu % 2, j * D:(j + 1) * D]
                        pe.matmul(o, ones3[:, :], bias3[:, 2 * D + 1:3 * D + 1], start=True, stop=False)
                        mm = pe.matmul(o, xgT[:, gu % 2, j * P:(j + 1) * P], w1_sb[:, :], start=False, stop=True)
                    mm.then_inc(S["mm_d2"], 1)
            run_steps(pe, G, 1, step_b2)
            pe.wait_ge(S["u_d2"], G)

            pe.wait_ge(S["sc"], 7)
            pe.transpose(pt[:, 0, 0:P], sum_a, ident[:, :])
            pe.transpose(pt[:, 0, P:2 * P], sum_b, ident[:, :]).then_inc(S["sc_pe"], 1)
            pe.wait_ge(S["sc"], 8)
            pe.transpose(pt[:, 1, 0:D], cumT[:, 0:P], ident[:, :]).then_inc(S["sc_pe"], 1)

            def step_c(k, u, it):
                if live(k, 0, T):
                    wait(pe, S["ag_c"], k + 1)
                    wait(pe, ring["hd_in"][u], 16 * (it + 1))
                    wait(pe, S["tc_c"], k - 1)
                    pe.transpose(pt[:, u % 2, 0:P], ring_a[:, u, :], ident[:, :])
                    pe.transpose(pt[:, u % 2, P:2 * P], ring_d[:, u % 2, :], ident[:, :]).then_inc(S["t_c"], 1)
                if live(k, 1, T):
                    j, ju, _ = back(k, u, it, 1)
                    wait(pe, S["tc_c"], j + 1)
                    wait(pe, S["u_c"], j - 1)
                    o = pk[:, ju % 2, 0:D]
                    pe.matmul(o, ones3[:, :], bias3[:, 2 * D + 1:3 * D + 1], start=True, stop=False)
                    pe.matmul(o, xgT[:, ju % 2, 0:P], w1_sb[:, :], start=False, stop=False)
                    pe.matmul(o, xgT[:, ju % 2, P:2 * P], w2_sb[:, :], start=False, stop=True)\
                        .then_inc(S["mm_c"], 1)
            run_steps(pe, T, 1, step_c)

        def inv_std(act, mean_var, log_v, r, mv_sem, lv_sem, rs_sem, j):
            wait(act, mv_sem, j + 1)
            act.activation(log_v, mean_var, ACT.Ln, bias=eps_c[:, 0:1]).then_inc(lv_sem, 1)
            wait(act, lv_sem, j + 1)
            act.activation(r, log_v, ACT.Exp, scale=-0.5).then_inc(rs_sem, 1)

        def exp_minus(act, e, logit, cl_sem, em_sem, j):
            act.activation(e, logit, ACT.Relu, bias=top_c[:, 0:1]).then_inc(cl_sem, 1)
            wait(act, cl_sem, j + 1)
            act.activation(e, e, ACT.Exp, bias=top_c[:, 0:1], scale=-1.0).then_inc(em_sem, 1)

        eps_c = sb("eps_c", [P, 1])
        top_c = sb("top_c", [P, 1])

        @block.scalar
        def _(act):
            act.preload_act_table_set("natural_log_exp_and_others")
            act.wait_ge(S["wprod"], 1)
            act.activation(a_kv[:, :], pk[:, 0, 0:2 * DM], ACT.Copy)
            act.activation(a_q[:, :], pk[:, 0, 2 * DM:3 * DM], ACT.Copy)
            act.wait_ge(S["wprod"], 2)
            act.activation(b_kvq[0:R, 0:DM], pk[0:R, 1, 0:DM], ACT.Copy)
            act.activation(b_kvq[0:R, DM:2 * DM], pk[0:R, 1, 0:DM], ACT.Copy)
            act.wait_ge(S["wprod"], 3)
            act.activation(wnsT, pt[0:DM, 0, 0:P], ACT.Copy).then_inc(S["wcopy"], 1)
            act.wait_ge(S["wprod"], 4)
            act.activation(w_sx[:, 0:D + 1], pt[:, 1, 0:D + 1], ACT.Copy).then_inc(S["wcopy"], 1)
            act.wait_ge(S["id1"], 1)
            act.activation(w_sx[:, D + 1:2 * D + 1], ident[:, :], ACT.Copy).then_inc(S["wcopy"], 1)

            def scale_rows(ju):
                for i in range(NA):
                    ins = act.activation(hout[ju][:, i * D:(i + 1) * D], hpre[:, ju, i * D:(i + 1) * D],
                                         ACT.Identity, bias=nb[:, ju, i:i + 1], scale=rs[:, ju, i:i + 1])
                return ins

            def store_group(tab, st, j, ju):
                if isinstance(j, int) and j == G - 1:
                    for q in range(U):
                        act.wait_ge(ring[st][q], last - (16 if q == ju else 0))
                act.dma_start(rows_of(tab, j), hout[ju]).then_inc(ring[st][ju], 16)

            def step_a(k, u, it):
                if live(k, 1, T):
                    j, ju, _ = back(k, u, it, 1)
                    wait(act, S["kv_a"], j + 1)
                    wait(act, S["pr_a"], j - 1)
                    kv = pk[:, ju % 2, DM:2 * DM].rearrange("p (h c) -> p h c", h=H)
                    vo = val[:, :, :, j] if isinstance(j, int) else \
                        val[:, :, :, bass.ds(j, 1)].rearrange("p h c a -> p h (c a)")
                    act.activation(vo, kv, ACT.Copy).then_inc(S["v_a"], 1)
                    act.activation(q_sb[:, ju % 2, :], pk[:, ju % 2, 2 * DM:3 * DM], ACT.Copy).then_inc(S["q_a"], 1)
                if live(k, 0, T):
                    wait(act, S["t_a"], k + 1)
                    wait(act, S["kv_a"], k - 1)
                    if live(k, 2, T):
                        _, su, sit = back(k, u, it, 2)
                        wait(act, ring["xdT_mv"][su], 16 * (sit + 1))
                    act.activation(pair[:, u % 2, :], pt[:, u % 2, 0:2 * P], ACT.Copy)
                    act.activation(ring_e[0:R, u % 2, :], pt[0:R, u % 2, 2 * P:3 * P], ACT.Copy)\
                        .then_inc(S["xsT_a"], 1)
                    wait(act, S["mm_d1"], k + 1)
                    wait(act, S["pre_d1"], k - 1)
                    exp_minus(act, em[:, u % 2, :], pd[:, u % 2, :, D], S["cl_d1"], S["em_d1"], k)
                    wait(act, S["xsT_a"], k + 1)
                    act.dma_start(xdT_all[:, k, :] if isinstance(k, int)
                                  else xdT_all[:, bass.ds(k, 1), :].rearrange("p a n -> p (a n)"),
                                  ring_c[:, u % 2, :]).then_inc(ring["xdT_mv"][u], 16)
                if live(k, 3, T):
                    j, ju, itj = back(k, u, it, 3)
                    wait(act, S["out_d1"], j + 1)
                    wait(act, ring["h_st"][ju], 16 * itj)
                    scale_rows(ju).then_inc(S["na_d1"], 1)
                    wait(act, S["na_d1"], j + 1)
                    store_group(h_tab, "h_st", j, ju)
                if live(k, 1, T):
                    j, ju, _ = back(k, u, it, 1)
                    inv_std(act, mv[:, ju, :, 1], lv[:, ju, :], rs[:, ju, :],
                            S["mv_d1"], S["lv_d1"], S["rs_d1"], j)
            run_steps(act, T, 3, step_a)

            act.wait_ge(S["sc"], 3)
            act.activation(decay[:, :, :], decay[:, :, :], ACT.Exp).then_inc(S["sc_act"], 1)
            act.activation(alpha[:, :, :], alpha[:, :, :], ACT.Exp).then_inc(S["sc_act"], 1)

            def step_b1(k, u, it):
                if live(k, 0, T):
                    wait(act, S["t_b1"], k + 1)
                    wait(act, S["mm_b1"], k - 1)
                    act.activation(ring_d[0:DM, u % 2, :], pt[0:DM, u % 2, 0:P], ACT.Copy).then_inc(S["oT_b1"], 1)
                if live(k, 1, T):
                    j, ju, _ = back(k, u, it, 1)
                    wait(act, S["mm_b1"], j + 1)
                    wait(act, S["pre_b1"], j - 1)
                    exp_minus(act, em[:, ju % 2, 0:1], pk[:, ju % 2, D:D + 1], S["cl_b1"], S["em_b1"], j)
                    act.activation(ring_c[:, ju % 2, :], pk[:, ju % 2, D + 1:2 * D + 1], ACT.Copy)\
                        .then_inc(S["xb_b1"], 1)
                if live(k, 2, T):
                    j, ju, _ = back(k, u, it, 2)
                    inv_std(act, mv[:, ju, 0, 1:2], lv[:, ju, 0:1], rs[:, ju, 0:1],
                            S["mv_b1"], S["lv_b1"], S["rs_b1"], j)
            run_steps(act, T, 2, step_b1)

            act.wait_ge(S["os_b1"], T)

            def step_b2(k, u, it):
                if live(k, 0, G):
                    wait(act, S["t_d2"], k + 1)
                    wait(act, S["mm_d2"], k - 1)
                    act.activation(xgT[:, u % 2, :], pt[:, u % 2, :], ACT.Copy).then_inc(S["hT_d2"], 1)
                    wait(act, ring["hs_in"][u], 16 * (it + 1))
                    if isinstance(k, int):
                        ao, es = agg[:, :, k], ew_t[:, k:k + 1]
                    else:
                        ao, es = agg[:, :, bass.ds(k, 1)].rearrange("p f a -> p (f a)"), ew_t[:, bass.ds(k, 1)]
                    act.activation(ao, ring_a[:, u, :], ACT.Copy, scale=es).then_inc(S["agg_b2"], 1)
                if live(k, 2, G):
                    j, ju, _ = back(k, u, it, 2)
                    inv_std(act, mv[:, ju, :, 1], lv[:, ju, :], rs[:, ju, :],
                            S["mv_d2"], S["lv_d2"], S["rs_d2"], j)
                if live(k, 3, G):
                    j, ju, itj = back(k, u, it, 3)
                    wait(act, S["out_d2"], j + 1)
                    wait(act, ring["z_st"][ju], 16 * itj)
                    scale_rows(ju).then_inc(S["na_d2"], 1)
                    wait(act, S["na_d2"], j + 1)
                    store_group(out, "z_st", j, ju)
            run_steps(act, T, 3, step_b2)

            def step_c(k, u, it):
                if live(k, 0, T):
                    wait(act, S["t_c"], k + 1)
                    wait(act, S["mm_c"], k - 1)
                    act.activation(xgT[:, u % 2, 0:2 * P], pt[:, u % 2, 0:2 * P], ACT.Copy).then_inc(S["tc_c"], 1)
                if live(k, 2, T):
                    j, ju, _ = back(k, u, it, 2)
                    inv_std(act, mv[:, ju, 0, 1:2], lv[:, ju, 0:1], rs[:, ju, 0:1],
                            S["mv_c"], S["lv_c"], S["rs_c"], j)
            run_steps(act, T, 2, step_c)

        @block.vector
        def _(dve):
            chain = [0]
            s_ch = sem("chain")

            def link(ins):
                chain[0] += 1
                ins.then_inc(s_ch, 1)
                dve.wait_ge(s_ch, chain[0])

            dve.memset(b_kvq[:, :], 0.0)
            dve.memset(bias3[:, :], 0.0)
            dve.memset(brow, 0.0).then_inc(S["fills"], 1)
            dve.memset(pad_i[0:1, 0:P - 1], N)
            dve.memset(pad_i[0:1, P - 1:P], -1)
            dve.memset(zrows, 0.0).then_inc(S["padded"], 1)
            dve.memset(s_int, 0)
            dve.memset(ew_t[:, :], 0.0).then_inc(S["fills"], 1)
            dve.memset(eps_c[:, :], EPS)
            dve.memset(top_c[:, :], TOP)
            dve.memset(o3[:, :, :], 0.0)
            dve.memset(ring_e[:, :, :], 1.0)
            dve.memset(ones3[:, :], 1.0)
            link(dve.memset(ones_t[:, :], 1.0))
            dve.wait_ge(S["w_in"], 16 * 16)
            dve.tensor_copy(r_c[:, 0:D], m2n_w)
            dve.tensor_copy(r_o[:, D + 1:2 * D + 1], m2n_w)
            dve.tensor_scalar(r_o[:, 0:D], m2n_w, -1.0, None, ALU.mult)
            dve.tensor_tensor(r_o[:, D:D + 1], beta_w[:, 0:1], beta_w[:, 2:3], ALU.add)
            dve.tensor_tensor(r_c[:, D:D + 1], beta_w[:, 1:2], beta_w[:, 2:3], ALU.subtract).then_inc(S["wcopy"], 1)
            dve.wait_ge(S["wprod"], 5)
            link(dve.tensor_copy(brow[0:1, 0:D + 1], pd[0:1, 0, 0, 0:D + 1]))
            link(dve.tensor_copy(brow_b[0:1, 0, :], brow))
            link(dve.tensor_tensor(brow_r, brow, brow_b[0:1, 0, :], ALU.subtract))
            link(dve.tensor_copy(brow_b[0:1, 1, :], brow_r))
            link(dve.tensor_tensor(brow, brow_r, brow_b[0:1, 1, :], ALU.subtract))
            dve.tensor_copy(brow_b[0:1, 2, :], brow).then_inc(S["rows"], 1)
            dve.wait_ge(S["edge_in"], 7 * 16)
            link(dve.tensor_tensor(drop, d_int[0], d_int[1], ALU.is_lt))
            dve.reduce_max(drop_p, drop, AX_X).then_inc(S["drops"], 1)
            dve.wait_ge(S["drop_in"], 16)
            dve.reduce_max(drop_i, drop_row, AX_X).then_inc(S["checked"], 1)
            dve.wait_ge(S["checked"], 1)
            unsorted = dve.value_load(drop_i, min_val=0, max_val=1)
            with dve.If(unsorted > 0):
                dve.wait_ge(S["g_all"], 16)
                dve.wait_ge(S["g_iota"], 2)
                dve.tensor_copy(dst_all, dst_all.bitcast(I32)).then_inc(S["g_rank"], 1)
                dve.tensor_copy(jrow, jrow.bitcast(I32)).then_inc(S["g_rank"], 1)
                dve.tensor_copy(eidx, eidx.bitcast(I32)).then_inc(S["g_rank"], 1)
                dve.tensor_copy(d_f[0], d_int[0]).then_inc(S["g_rank"], 1)
                dve.memset(rank, 0.0).then_inc(S["g_rank"], 1)
                done = 5
                dve.wait_ge(S["g_rank"], done)
                for c in range(EP // CH):
                    some = dst_all[:, c * CH:(c + 1) * CH]
                    with dve.Fori(0, T) as t:
                        own, me = d_f[0][:, bass.ds(t, 1)], eidx[:, bass.ds(t, 1)]
                        dve.tensor_scalar(hits, jrow, me, None, ALU.is_lt).then_inc(S["g_rank"], 1)
                        dve.wait_ge(S["g_rank"], t * 4 + (done + 1))
                        dve.scalar_tensor_tensor(out=hits, in0=some, scalar=own, in1=hits, op0=ALU.is_equal,
                                                 op1=ALU.mult).then_inc(S["g_rank"], 1)
                        dve.wait_ge(S["g_rank"], t * 4 + (done + 2))
                        dve.scalar_tensor_tensor(out=hits, in0=some, scalar=own, in1=hits, op0=ALU.is_lt,
                                                 op1=ALU.add).then_inc(S["g_rank"], 1)
                        dve.wait_ge(S["g_rank"], t * 4 + (done + 3))
                        dve.reduce_sum(part[:, bass.ds(t, 1)], hits, AX_X).then_inc(S["g_rank"], 1)
                        dve.wait_ge(S["g_rank"], t * 4 + (done + 4))
                    done += 4 * T
                    dve.tensor_tensor(rank, rank, part, ALU.add).then_inc(S["g_rank"], 1)
                    dve.tensor_scalar(eidx, eidx, -float(CH), None, ALU.add).then_inc(S["g_rank"], 1)
                    done += 2
                    dve.wait_ge(S["g_rank"], done)
                dve.tensor_copy(rank_i, rank).then_inc(S["g_rank"], 1)
                dve.wait_ge(S["g_rank"], done + 1)
                dve.tensor_scalar(rank1_i, rank, 1.0, None, ALU.add).then_inc(S["ranked"], 1)
            dve.wait_ge(S["ordered"], 1)
            for i in range(2):
                dve.tensor_copy(d_f[i], d_int[i])
            link(dve.tensor_copy(d_f[2], d_int[2]))
            dve.tensor_copy(gidx[:, :, 0], s_int)
            dve.tensor_scalar(clip, d_f[0], float(N - 1), None, ALU.min)
            dve.tensor_tensor(nend, d_f[0], d_f[2], ALU.is_equal)
            link(dve.tensor_tensor(same[:, :], d_f[0], d_f[1], ALU.is_equal))
            dve.tensor_copy(gidx[:, :, 1], clip)
            dve.tensor_scalar(far[:, :], same[:, :], -1.0, FAR, ALU.add, ALU.mult)
            link(dve.scalar_tensor_tensor(out=d_f[1], in0=nend, scalar=float(N), in1=d_f[0], op0=ALU.mult, op1=ALU.add))
            dve.tensor_copy(sidx[:, :], d_f[1])
            dve.tensor_tensor_scan(pfar[:, :], far[:, :], far[:, :], 0.0, ALU.min, ALU.min)\
                .then_inc(S["dsteps"], 1)
            dve.tensor_copy(em[:, 0, 0:1], ones_t[:, 0:1]).then_inc(S["wcopy"], 1)

            def row_stats(pieces, ju, n):
                for i in range(n):
                    ins = dve.bn_stats(stats[:, ju, i, :], pieces(i))
                return ins

            def mean_var(ju, n):
                for i in range(n):
                    ins = dve.bn_aggr(mv[:, ju, i, :], stats[:, ju, i, :])
                return ins

            def neg_mean(ju):
                return dve.scalar_tensor_tensor(out=nb[:, ju, :], in0=mv[:, ju, :, 0], scalar=-1.0,
                                                in1=rs[:, ju, :], op0=ALU.mult, op1=ALU.mult)

            def normalise(to, pieces, ju, n, first=0):
                for i in range(first, n):
                    ins = dve.tensor_scalar(to(i), pieces(i), mv[:, ju, i, 0:1], rs[:, ju, i:i + 1],
                                            ALU.subtract, ALU.mult)
                return ins

            def step_a(k, u, it):
                if live(k, 1, T):
                    j, ju, _ = back(k, u, it, 1)
                    wait(dve, S["q_a"], j + 1)
                    dve.scalar_tensor_tensor(out=prod[:, ju % 2, :], in0=pk[:, ju % 2, 0:DM], scalar=QSCALE,
                                             in1=q_sb[:, ju % 2, :], op0=ALU.mult, op1=ALU.mult).then_inc(S["pr_a"], 1)
                    wait(dve, S["pr_a"], j + 1)
                    ao = alpha[:, :, j:j + 1] if isinstance(j, int) else alpha[:, :, bass.ds(j, 1)]
                    dve.reduce_sum(ao, prod[:, ju % 2, :].rearrange("p (h c) -> p h c", h=H), AX_X)\
                        .then_inc(S["al_a"], 1)
                if live(k, 0, T):
                    wait(dve, S["em_d1"], k + 1)
                    dve.tensor_scalar(ep[:, u % 2, :], em[:, u % 2, :], 1.0, None, ALU.add).then_inc(S["ep_d1"], 1)
                    wait(dve, S["ep_d1"], k + 1)
                    dve.reciprocal(beta[:, u % 2, :], ep[:, u % 2, :]).then_inc(S["be_d1"], 1)
                    wait(dve, S["be_d1"], k + 1)
                    wait(dve, ring["xg_in"][u], 16 * (it + 1))
                    wait(dve, S["out_d1"], k - U + 1)
                    wait(dve, S["na_d1"], k - U + 1)
                    for j in range(NJ):
                        ins = dve.scalar_tensor_tensor(
                            out=hpre[:, u, j * D:(j + 1) * D], in0=pd[:, u % 2, j, 0:D],
                            scalar=beta[:, u % 2, j:j + 1], in1=xg[:, u, j * D:(j + 1) * D],
                            op0=ALU.mult, op1=ALU.add)
                    ins.then_inc(S["pre_d1"], 1)
                    wait(dve, S["pre_d1"], k + 1)
                    row_stats(lambda i: hpre[:, u, i * D:(i + 1) * D], u, NJ).then_inc(S["bn_d1"], 1)
                    wait(dve, S["bn_d1"], k + 1)
                if live(k, 2, T):
                    j, ju, itj = back(k, u, it, 2)
                    wait(dve, S["rs_d1"], j + 1)
                    neg_mean(ju)
                    wait(dve, ring["h_st"][ju], 16 * itj)
                    normalise(lambda i: hout[ju][:, i * D:(i + 1) * D],
                              lambda i: hpre[:, ju, i * D:(i + 1) * D], ju, NJ, NA).then_inc(S["out_d1"], 1)
                if live(k, 0, T):
                    mean_var(u, NJ).then_inc(S["mv_d1"], 1)
            run_steps(dve, T, 2, step_a)

            dve.wait_ge(S["v_a"], T)
            dve.wait_ge(S["na_d1"], T)
            dve.wait_ge(S["al_a"], T)
            for q in range(U):
                dve.wait_ge(ring["h_st"][q], last)
            for h in range(H):
                ins = dve.tensor_tensor_scan(rmax[:, h, 1:T + 1], far[:, :], alpha[:, h, :], -FAR, ALU.add, ALU.max)
            link(ins)
            dve.tensor_copy(sum_a[:, 0:H], rmax[:, :, T])
            dve.tensor_copy(sum_b[:, 0:H], pfar[:, T - 1:T].to_broadcast([P, H])).then_inc(S["sc"], 1)
            dve.wait_ge(S["sc_pe"], 1)
            dve.memset(cumT[0:H, 0:1], -FAR)
            link(dve.tensor_copy(keepT[0:H, :], pt[0:H, 0, P:2 * P]))
            dve.tensor_tensor_scan(cumT[0:H, 1:P + 1], keepT[0:H, :], pt[0:H, 0, 0:P], -FAR, ALU.add, ALU.max)\
                .then_inc(S["sc"], 1)
            dve.wait_ge(S["sc_pe"], 2)
            dve.tensor_copy(carm[:, :], pt[:, 1, 0:H])
            link(dve.tensor_copy(rmax[:, :, 0], pt[:, 1, 0:H]))
            for h in range(H):
                ins = dve.scalar_tensor_tensor(out=rmax[:, h, 1:T + 1], in0=pfar[:, :], scalar=carm[:, h:h + 1],
                                               in1=rmax[:, h, 1:T + 1], op0=ALU.add, op1=ALU.max)
            link(ins)
            dve.tensor_tensor(alpha[:, :, :], alpha[:, :, :], rmax[:, :, 1:T + 1], ALU.subtract)
            link(dve.tensor_tensor(decay[:, :, :], rmax[:, :, 0:T], rmax[:, :, 1:T + 1], ALU.subtract))
            dve.tensor_tensor(decay[:, :, :], decay[:, :, :],
                              far[:, :].rearrange("p (a t) -> p a t", a=1).to_broadcast([P, H, T]), ALU.add)\
                .then_inc(S["sc"], 1)
            dve.wait_ge(S["sc_act"], 1)
            for h in range(H):
                dve.tensor_tensor_scan(cdec[:, h, :], decay[:, h, :], ones_t[:, :], 1.0, ALU.mult, ALU.mult)
            dve.wait_ge(S["sc_act"], 2)
            for h in range(H):
                dve.tensor_tensor_scan(rden[:, h, :], decay[:, h, :], alpha[:, h, :], 0.0, ALU.mult, ALU.add)
            for h in range(H - 1):
                vh = val[:, h, :, :]
                ins = dve.tensor_tensor(vh, vh, alpha[:, h, :].rearrange("p (a t) -> p a t", a=1)
                                        .to_broadcast([P, C, T]), ALU.mult)
            link(ins)
            for h in range(H):
                if h == H - 1:
                    dve.wait_ge(S["sc_pool"], 1)
                for c in range(C):
                    ins = dve.tensor_tensor_scan(val[:, h, c, :], decay[:, h, :], val[:, h, c, :], 0.0, ALU.mult, ALU.add)
            link(ins)
            dve.tensor_copy(sum_a[:, 0:DM].rearrange("p (h c) -> p h c", h=H), val[:, :, :, T - 1])
            dve.tensor_copy(sum_a[:, DM:DM + H], rden[:, :, T - 1])
            dve.tensor_copy(sum_b[:, 0:DM].rearrange("p (h c) -> p h c", h=H),
                            cdec[:, :, T - 1:T].to_broadcast([P, H, C]))
            dve.tensor_copy(sum_b[:, DM:DM + H], cdec[:, :, T - 1]).then_inc(S["sc"], 1)
            dve.wait_ge(S["sc_pe"], 3)
            dve.memset(cumT[0:DM + H, 0:1], 0.0)
            link(dve.tensor_copy(keepT[0:DM + H, :], pt[0:DM + H, 0, P:2 * P]))
            dve.tensor_tensor_scan(cumT[0:DM + H, 1:P + 1], keepT[0:DM + H, :], pt[0:DM + H, 0, 0:P], 0.0,
                                   ALU.mult, ALU.add).then_inc(S["sc"], 1)
            dve.wait_ge(S["sc_pe"], 4)
            link(dve.tensor_copy(carn[:, :], pt[:, 1, 0:DM + H]))
            for h in range(H):
                ins = dve.scalar_tensor_tensor(out=rden[:, h, :], in0=cdec[:, h, :], scalar=carn[:, DM + h:DM + h + 1],
                                               in1=rden[:, h, :], op0=ALU.mult, op1=ALU.add)
            link(ins)
            link(dve.reciprocal(rden[:, :, :], rden[:, :, :]))
            dve.memset(em[:, 0, 0:1], 0.0).then_inc(S["sc"], 1)

            car_v = carn[:, 0:DM].rearrange("p (h c) -> p h c", h=H)

            def at(t3, k):
                a = t3[:, :, k:k + 1] if isinstance(k, int) else t3[:, :, bass.ds(k, 1)]
                return a.to_broadcast([P, H, C])

            def step_b1(k, u, it):
                if live(k, 0, T):
                    vk = val[:, :, :, k] if isinstance(k, int) else \
                        val[:, :, :, bass.ds(k, 1)].rearrange("p h c a -> p h (c a)")
                    dve.tensor_tensor(o1, at(cdec, k), car_v, ALU.mult).then_inc(S["o_b1"], 1)
                    wait(dve, S["o_b1"], 2 * k + 1)
                    dve.tensor_tensor(o2, o1, vk, ALU.add).then_inc(S["o_b1"], 1)
                    wait(dve, S["o_b1"], 2 * k + 2)
                    wait(dve, S["t_b1"], k - 1)
                    dve.tensor_tensor(o3[:, u % 2, 0:DM].rearrange("p (h c) -> p h c", h=H), o2,
                                      at(rden, k), ALU.mult).then_inc(S["os_b1"], 1)
                if live(k, 2, T):
                    j, ju, _ = back(k, u, it, 2)
                    wait(dve, S["em_b1"], j + 1)
                    dve.tensor_scalar(ep[:, ju % 2, 0:1], em[:, ju % 2, 0:1], 1.0, None, ALU.add)\
                        .then_inc(S["ep_b1"], 1)
                    wait(dve, S["ep_b1"], j + 1)
                    dve.reciprocal(beta[:, ju % 2, 0:1], ep[:, ju % 2, 0:1]).then_inc(S["be_b1"], 1)
                    wait(dve, S["be_b1"], j + 1)
                    wait(dve, S["xb_b1"], j + 1)
                    wait(dve, S["h_b1"], j - 1)
                    dve.scalar_tensor_tensor(out=ring_f[:, ju % 2, :], in0=pk[:, ju % 2, 0:D],
                                             scalar=beta[:, ju % 2, 0:1], in1=ring_c[:, ju % 2, :],
                                             op0=ALU.mult, op1=ALU.add).then_inc(S["pre_b1"], 1)
                    wait(dve, S["pre_b1"], j + 1)
                    row_stats(lambda i: ring_f[:, ju % 2, :], ju, 1).then_inc(S["bn_b1"], 1)
                    wait(dve, S["bn_b1"], j + 1)
                if live(k, 3, T):
                    j, ju, itj = back(k, u, it, 3)
                    wait(dve, S["rs_b1"], j + 1)
                    wait(dve, ring["h_sc"][ju], 16 * itj)
                    wait(dve, ring["hd_st"][ju], 16 * itj)
                    normalise(lambda i: ring_b[:, ju, :], lambda i: ring_f[:, ju % 2, :], ju, 1)\
                        .then_inc(S["h_b1"], 1)
                if live(k, 2, T):
                    mean_var(back(k, u, it, 2)[1], 1).then_inc(S["mv_b1"], 1)
            run_steps(dve, T, 3, step_b1)
            dve.wait_ge(S["os_b1"], T)

            def step_b2(k, u, it):
                if live(k, 1, G):
                    j, ju, itj = back(k, u, it, 1)
                    wait(dve, S["out_d2"], j - U + 1)
                    wait(dve, S["na_d2"], j - U + 1)
                    wait(dve, S["mm_d2"], j + 1)
                    wait(dve, ring["hg_in"][ju], 16 * (itj + 1))
                    dve.scalar_tensor_tensor(out=hpre[:, ju, :], in0=pk[:, ju % 2, :], scalar=0.0,
                                             in1=xg[:, ju, :], op0=ALU.max, op1=ALU.add).then_inc(S["u_d2"], 1)
                    wait(dve, S["u_d2"], j + 1)
                    row_stats(lambda i: hpre[:, ju, i * D:(i + 1) * D], ju, NJ).then_inc(S["bn_d2"], 1)
                    wait(dve, S["bn_d2"], j + 1)
                if live(k, 2, G):
                    j, ju, itj = back(k, u, it, 2)
                    wait(dve, S["rs_d2"], j + 1)
                    neg_mean(ju)
                    wait(dve, ring["z_st"][ju], 16 * itj)
                    normalise(lambda i: hout[ju][:, i * D:(i + 1) * D],
                              lambda i: hpre[:, ju, i * D:(i + 1) * D], ju, NJ, NA).then_inc(S["out_d2"], 1)
                if live(k, 1, G):
                    mean_var(back(k, u, it, 1)[1], NJ).then_inc(S["mv_d2"], 1)
            run_steps(dve, G, 2, step_b2)

            for q in range(U):
                dve.wait_ge(ring["z_st"][q], last)
            dve.wait_ge(S["na_d2"], G)
            dve.tensor_tensor_scan(psame[:, :], same[:, :], ones_t[:, :], 1.0, ALU.mult, ALU.mult)
            dve.wait_ge(S["agg_b2"], T)
            for f in range(D):
                ins = dve.tensor_tensor_scan(agg[:, f, :], same[:, :], agg[:, f, :], 0.0, ALU.mult, ALU.add)
            link(ins)
            dve.tensor_copy(sum_a, agg[:, :, T - 1])
            dve.tensor_copy(sum_b, psame[:, T - 1:T].to_broadcast([P, D])).then_inc(S["sc"], 1)
            dve.wait_ge(S["sc_pe"], 5)
            dve.memset(cumT[:, 0:1], 0.0)
            link(dve.tensor_copy(keepT, pt[:, 0, P:2 * P]))
            dve.tensor_tensor_scan(cumT[:, 1:P + 1], keepT, pt[:, 0, 0:P], 0.0, ALU.mult, ALU.add)\
                .then_inc(S["sc"], 1)
            dve.wait_ge(S["sc_pe"], 6)
            link(dve.tensor_copy(carg, pt[:, 1, 0:D]))

            def step_c(k, u, it):
                if live(k, 0, T):
                    wait(dve, S["t_c"], k - 1)
                    if isinstance(k, int):
                        ak, sk = agg[:, :, k], psame[:, k:k + 1]
                    else:
                        ak, sk = agg[:, :, bass.ds(k, 1)].rearrange("p f a -> p (f a)"), psame[:, bass.ds(k, 1)]
                    dve.scalar_tensor_tensor(out=ring_d[:, u % 2, :], in0=carg, scalar=sk, in1=ak,
                                             op0=ALU.mult, op1=ALU.add).then_inc(S["ag_c"], 1)
                if live(k, 2, T):
                    j, ju, itj = back(k, u, it, 2)
                    wait(dve, S["z_c"], j - 1)
                    wait(dve, S["mm_c"], j + 1)
                    wait(dve, ring["hd_in"][ju], 16 * (itj + 1))
                    dve.scalar_tensor_tensor(out=ring_f[:, ju % 2, :], in0=pk[:, ju % 2, 0:D], scalar=0.0,
                                             in1=ring_a[:, ju, :], op0=ALU.max, op1=ALU.add).then_inc(S["u_c"], 1)
                    wait(dve, S["u_c"], j + 1)
                    row_stats(lambda i: ring_f[:, ju % 2, :], ju, 1).then_inc(S["bn_c"], 1)
                    wait(dve, S["bn_c"], j + 1)
                if live(k, 3, T):
                    j, ju, itj = back(k, u, it, 3)
                    wait(dve, S["rs_c"], j + 1)
                    wait(dve, ring["z_sc"][ju], 16 * itj)
                    normalise(lambda i: ring_b[:, ju, :], lambda i: ring_f[:, ju % 2, :], ju, 1)\
                        .then_inc(S["z_c"], 1)
                if live(k, 2, T):
                    mean_var(back(k, u, it, 2)[1], 1).then_inc(S["mv_c"], 1)
            run_steps(dve, T, 3, step_c)


_OUT = ((100000, 128), "float32")


def kernel(**inputs):
    import numpy as _np
    import concourse.bacc as _bacc
    from concourse import mybir as _mybir
    from concourse.bass_utils import run_bass_kernel_spmd as _run

    a = {k: _np.ascontiguousarray(v) for k, v in inputs.items()}
    x = a["x"]
    n = x.shape[0]
    whole = n // GN
    groups = _np.concatenate([x[:whole * GN], x[n - GN:]]).reshape(whole + 1, P, NJ, D)
    row = lambda v: v.reshape(1, -1)
    arrays = {
        "x": x, "xT": _np.ascontiguousarray(groups.transpose(0, 3, 2, 1).reshape(whole + 1, D, GN)),
        "src": row(a["src"]), "dst": row(a["dst"]), "ea": a["edge_attr_50"], "ew": row(a["edge_weight"]),
        "w_n2mT": _np.ascontiguousarray(a["L0_gnn_W_n2m"].T), "w_edgeT": _np.ascontiguousarray(a["L0_gnn_W_edge"].T),
        "w_q": a["L0_gnn_W_q"], "b_q": row(a["L0_gnn_b_q"]), "w_k": a["L0_gnn_W_k"], "b_k": row(a["L0_gnn_b_k"]),
        "w_v": a["L0_gnn_W_v"], "b_v": row(a["L0_gnn_b_v"]), "w_e": a["L0_gnn_W_e"], "w_skip": a["L0_gnn_W_skip"],
        "b_skip": a["L0_gnn_b_skip"].reshape(-1, 1),
        "w_beta": _np.ascontiguousarray(a["L0_gnn_W_beta"].reshape(3, DM).T), "w_m2n": a["L0_gnn_W_m2n"],
        "w_1": a["L1_gnn_w1"], "w_2": a["L1_gnn_w2"], "b_1": row(a["L1_gnn_b"]),
    }
    nc = _bacc.Bacc("TRN2", target_bir_lowering=False, num_devices=1)
    args = {k: nc.dram_tensor(f"in_{k}", v.shape, _mybir.dt.from_np(v.dtype), kind="ExternalInput").ap()
            for k, v in arrays.items()}
    out = nc.dram_tensor("out_z", _OUT[0], _mybir.dt.from_np(_np.dtype(_OUT[1])), kind="ExternalOutput").ap()
    gnn_kernel(nc, out=out, **args)
    r = _run(nc, [{f"in_{k}": v for k, v in arrays.items()}], core_ids=[0])
    return r.results[0]["out_z"]
```

```python
from contextlib import ExitStack

import concourse.bass as bass
from concourse import mybir

F32 = mybir.dt.float32
BF16 = mybir.dt.bfloat16
I32 = mybir.dt.int32
ALU = mybir.AluOpType
ACT = mybir.ActivationFunctionType
AX_X = mybir.AxisListType.X

P = 128
D = 128
DM = 64
R = 50
H = 4
C = DM // H
NJ = 4
GN = NJ * P
U = 4
EPS = 1e-5
FAR = 1e38
TOP = 88.0
NZ = 3
NP = 1
QSCALE = 1.0 / C ** 0.5


def wait(eng, sem, value):
    if not (isinstance(value, int) and value <= 0):
        eng.wait_ge(sem, value)


def live(k, lag, n):
    return not isinstance(k, int) or 0 <= k - lag < n


def back(k, u, it, lag):
    return k - lag, (u - lag) % U, it + (u - lag) // U


def uses(n, slot):
    return -(-(n - slot) // U)


def run_steps(eng, n, lag, step):
    first, whole = max(1, -(-lag // U)), (n - 1) // U
    for k in range(first * U):
        step(k, k % U, k // U)
    with eng.Fori(first, whole) as it:
        for u in range(U):
            step(it * U + u, u, it)
    for k in range(whole * U, n + lag):
        step(k, k % U, k // U)


def gnn_kernel(nc, x, xT, src, dst, ea, ew, w_n2mT, w_edgeT, w_q, b_q, w_k, b_k, w_v, b_v,
               w_e, w_skip, b_skip, w_beta, w_m2n, w_1, w_2, b_1, out):
    N = x.shape[0]
    E = src.shape[1]
    T = -(-E // (P * U)) * U
    EP = P * T
    G = -(-N // (GN * U)) * U
    assert G == T and G * GN - N < GN and EP - E < T
    VLAST = T - (EP - E)
    T2 = T // 2

    h_tab = nc.dram_tensor("h_tab", (N, D), F32, kind="Internal").ap()
    hd_scr = nc.dram_tensor("hd_scr", (T2, P, 2 * D), F32, kind="Internal").ap()
    dst_tab = nc.dram_tensor("dst_s", (EP + 2, 1), I32, kind="Internal").ap()
    ea_s = nc.dram_tensor("ea_s", (EP, R), F32, kind="Internal").ap()
    ea_t = ea_s.rearrange("(p t) r -> p t r", p=P)
    src_tab = nc.dram_tensor("src_s", (E, 1), I32, kind="Internal").ap()
    ew_tab = nc.dram_tensor("ew_s", (E, 1), F32, kind="Internal").ap()
    dst_s, src_s, ew_s = (tab.rearrange("n a -> a n") for tab in (dst_tab, src_tab, ew_tab))

    with ExitStack() as ctx:
        def sb(name, shape, dt=F32):
            return ctx.enter_context(nc.sbuf_tensor(name, shape, dt))

        def sem(name):
            return ctx.enter_context(nc.semaphore(name))

        pt = ctx.enter_context(nc.psum_tensor("pt", [P, 2, 512], F32))
        pk = ctx.enter_context(nc.psum_tensor("pk", [P, 2, 512], F32))
        pd = ctx.enter_context(nc.psum_tensor("pd", [P, 2, NJ, 256], F32))

        pd_bank = pd[:, :, :, :].rearrange("p s (b j) n -> p s b (j n)", b=2)

        big = sb("big", [P, D * T])
        xdT_all = big[:, :].rearrange("p (t n) -> p t n", t=T)
        agg = big[:, :].rearrange("p (f t) -> p f t", t=T)
        val = sb("val", [P, H, C, T])
        alpha = sb("alpha", [P, H, T])
        scan_buf = sb("scan_buf", [P, H * (4 * T + 1)])

        def scan_part(first, n):
            return scan_buf[:, H * first:H * (first + n)].rearrange("p (h t) -> p h t", h=H)
        rmax = scan_part(0, T + 1)
        decay = scan_part(T + 1, T)
        cdec = scan_part(2 * T + 1, T)
        rden = scan_part(3 * T + 1, T)
        same = sb("same", [P, T])
        far = sb("far", [P, T])
        pfar = sb("pfar", [P, T])
        psame = pfar
        ones_t = sb("ones_t", [P, T])
        ew_t = sb("ew_t", [P, T])
        gidx = sb("gidx", [P, T, 2], I32)
        sidx = sb("sidx", [P, T], I32)

        ring_a = sb("ring_a", [P, U, D])
        ring_b = sb("ring_b", [P, U, D])
        pair = sb("pair", [P, 2, 2 * D])
        ring_d = pair[:, :, 0:D]
        ring_c = pair[:, :, D:2 * D]
        ring_e = sb("ring_e", [P, 2, D])
        ea_in = sb("ea_in", [P, U, R])
        q_sb = sb("q_sb", [P, 2, DM])
        prod = sb("prod", [P, 2, DM])
        o3 = sb("o3", [P, 2, 2 * DM])
        xg = sb("xg", [P, U, GN])
        xd2T = xg[:, :, 0:2 * D]
        hd2 = xg[:, :, 2 * D:4 * D]
        xgT = scan_buf[:, 0:U * GN].rearrange("p (u n) -> p u n", u=U)
        hpre = sb("hpre", [P, U, GN])
        hout_own = sb("hout", [P, 2, GN])
        hout = [hout_own[:, 0, :], hout_own[:, 1, :],
                scan_buf[:, U * GN:(U + 1) * GN], scan_buf[:, (U + 1) * GN:(U + 2) * GN]]
        idx2 = sb("idx2", [P, U, 2], I32)
        em = sb("em", [P, 2, NJ])
        ep = sb("ep", [P, 2, NJ])
        beta = sb("beta", [P, 2, NJ])
        stats = sb("stats", [P, U, NJ, 6])
        mv = sb("mv", [P, U, NJ, 2])
        lv = sb("lv", [P, U, NJ])
        rs = sb("rs", [P, U, NJ])
        nb = sb("nb", [P, U, NJ])

        ident = sb("ident", [P, P])
        a_kv = sb("a_kv", [P, 2 * DM])
        a_q = sb("a_q", [P, DM])
        b_kvq = sb("b_kvq", [P, 3 * DM])
        w_sx = sb("w_sx", [P, 2 * D + 1])
        r_o = sb("r_o", [P, 2, 2 * D + 1])
        r_c = sb("r_c", [DM, D + 1])
        ones3 = sb("ones3", [P, P], BF16)
        bias3 = sb("bias3", [P, 3 * D + 1], BF16)
        w1_sb = sb("w1_sb", [P, D])
        w2_sb = sb("w2_sb", [P, D])
        n2mT = hpre[0:DM, 0, 0:D]
        kvq_w = hpre[0:DM, 0, D:D + 3 * DM]
        e_w = hpre[0:DM, 0, 320:384]
        skip_w = hpre[0:DM, 0, 384:448]
        edgeT = hpre[0:DM, 0, 448:448 + R]
        m2n_w = hpre[0:DM, 1, 0:D]
        beta_w = hpre[0:DM, 1, 128:131]
        bskip = hpre[0:DM, 1, 132:133]
        wnsT = hpre[0:DM, 1, 136:264]
        brow = hout_own[0:1, 0, 0:3 * D + 1]
        brow_r = hout_own[0:1, 1, 0:3 * D + 1]
        brow_b = val[0:1, 0, :, :].rearrange("p c t -> p (c t)")[:, 0:1200].bitcast(BF16)\
            .rearrange("p (i n) -> p i n", i=3)[:, :, 0:3 * D + 1]
        d_int = [val[:, 1, c, :].bitcast(I32) for c in range(3)]
        s_int = val[:, 1, 3, :].bitcast(I32)
        d_f = [val[:, 1, 4 + c, :] for c in range(3)]
        nend = val[:, 1, 7, :]
        clip = val[:, 1, 8, :]
        pad_i = val[0:1, 1, 9, 0:P].bitcast(I32)
        zrows = big[0:EP - E, 0:R]
        dst_all = big[:, 0:EP]
        CH = EP // 8
        jrow = val[:, 2, :, :].rearrange("p c t -> p (c t)")[:, 0:CH]
        hits = val[:, 3, :, :].rearrange("p c t -> p (c t)")[:, 0:CH]
        eidx, rank, part = alpha[:, 0, :], alpha[:, 1, :], alpha[:, 2, :]
        rank_i = alpha[:, 0, :].bitcast(I32)
        rank1_i = alpha[:, 3, :].bitcast(I32)
        drop = val[:, 1, 10, :]
        drop_p = val[:, 1, 11, 0:1]
        drop_row = val[0:1, 1, 12, 0:P]
        drop_i = val[0:1, 1, 13, 0:1].bitcast(I32)
        one_dst, one_src, one_ew = (q_sb[:, 0, i:i + 1] for i in range(3))
        sum_a = hpre[:, 0, 0:D]
        sum_b = hpre[:, 0, D:2 * D]
        keepT = hpre[:, 0, 2 * D:3 * D]
        cumT = hpre[:, 1, 0:P + 1]
        carm = sb("carm", [P, H])
        carn = sb("carn", [P, DM + H])
        carg = rden[:, 0, 0:D]

        S = {n: sem(n) for n in (
            "w_in", "pad_in", "edge_in", "edge_in2", "padded", "id0", "id1", "fills", "gp_fill", "wprod", "wcopy",
            "rows", "r_o", "rows_in", "dsteps", "issued", "drops", "drop_in", "checked", "ordered",
            "g_all", "g_iota", "g_rank", "ranked", "g_one", "g_ea", "g_out", "g_back",
            "idx_a", "mv_a", "t_a", "xsT_a", "kv_a", "q_a", "v_a", "pr_a", "al_a",
            "mm_d1", "cl_d1", "em_d1", "ep_d1", "be_d1", "pre_d1", "bn_d1", "mv_d1", "lv_d1", "rs_d1", "nb_d1", "na_d1",
            "sc", "sc_pe", "sc_act", "sc_pool",
            "os_b1", "t_b1", "oT_b1", "mm_b1", "cl_b1", "em_b1", "xb_b1", "ep_b1", "be_b1", "pre_b1", "bn_b1",
            "mv_b1", "lv_b1", "rs_b1", "h_b1", "na_b1", "idx_b1",
            "idx_b2", "agg_b2", "t_d2", "hT_d2", "mm_d2", "u_d2", "bn_d2", "mv_d2", "lv_d2", "rs_d2", "out_d2", "na_d2",
            "ag_c", "t_c", "tc_c", "mm_c", "u_c", "bn_c", "mv_c", "lv_c", "rs_c", "z_c", "idx_c")}
        ring = {n: [sem(f"{n}{u}") for u in range(U)] for n in (
            "xs_in", "xd_in", "ea_in", "xg_in", "xgT_in", "h_st",
            "xl_in", "hd_st", "h_sc", "hs_in", "hg_in", "z_st", "hd_in", "z_sc")}
        last = T // U * 16

        n0 = N - GN

        def node0(g):
            return n0 if isinstance(g, int) and g == G - 1 else g * GN

        def rows_of(tab, g):
            b = node0(g)
            if isinstance(b, int):
                return tab[b:b + GN, :].rearrange("(p j) f -> p (j f)", j=NJ)
            return tab[bass.ds(b, GN), :].rearrange("(p j) f -> p (j f)", j=NJ)

        def store_group(eng, tab, st, j, ju):
            if isinstance(j, int) and j == G - 1:
                for q in range(U):
                    eng.wait_ge(ring[st][q], last - (16 if q == ju else 0))
            eng.dma_start(rows_of(tab, j), hout[ju]).then_inc(ring[st][ju], 16)

        block = ctx.enter_context(nc.Block())

        @block.sync
        def _(sp):
            loads = [(n2mT, w_n2mT), (kvq_w[:, 0:DM], w_k), (kvq_w[:, DM:2 * DM], w_v),
                     (kvq_w[:, 2 * DM:3 * DM], w_q), (e_w, w_e), (skip_w, w_skip), (edgeT, w_edgeT),
                     (m2n_w, w_m2n), (beta_w, w_beta), (bskip, b_skip), (w1_sb[:, :], w_1), (w2_sb[:, :], w_2),
                     (b_kvq[R:R + 1, 0:DM], b_k), (b_kvq[R:R + 1, DM:2 * DM], b_v),
                     (b_kvq[R:R + 1, 2 * DM:3 * DM], b_q)]
            sp.wait_ge(S["fills"], 1)
            for to, of in loads:
                sp.dma_start(to, of).then_inc(S["w_in"], 16)
            sp.dma_start(brow[0:1, 2 * D + 1:3 * D + 1], b_1).then_inc(S["w_in"], 16)
            sp.wait_ge(S["padded"], 1)
            sp.dma_start(dst_s[0:1, 0:1], pad_i[0:1, P - 1:P]).then_inc(S["pad_in"], 16)
            sp.dma_start(dst_s[0:1, 1:E + 1], dst).then_inc(S["pad_in"], 16)
            sp.dma_start(dst_s[0:1, E + 1:EP + 2], pad_i[0:1, 0:EP + 1 - E]).then_inc(S["pad_in"], 16)
            sp.dma_start(ea_s[0:E, :], ea).then_inc(S["pad_in"], 16)
            sp.dma_start(ea_s[E:EP, :], zrows).then_inc(S["pad_in"], 16)
            sp.wait_ge(S["fills"], 2)
            sp.dma_start(s_int[0:P - 1, :], src[0:1, 0:(P - 1) * T].rearrange("a (p t) -> (a p) t", t=T))\
                .then_inc(S["edge_in"], 16)
            sp.dma_start(s_int[P - 1:P, 0:VLAST], src[0:1, (P - 1) * T:E]).then_inc(S["edge_in"], 16)
            sp.dma_start(ew_t[0:P - 1, :], ew[0:1, 0:(P - 1) * T].rearrange("a (p t) -> (a p) t", t=T))\
                .then_inc(S["edge_in"], 16)
            sp.dma_start(ew_t[P - 1:P, 0:VLAST], ew[0:1, (P - 1) * T:E]).then_inc(S["edge_in"], 16)
            sp.wait_ge(S["pad_in"], 5 * 16)
            for i, shift in enumerate((1, 0, 2)):
                sp.dma_start(d_int[i], dst_s[0:1, shift:shift + EP].rearrange("a (p t) -> (a p) t", t=T))\
                    .then_inc(S["edge_in"], 16)
            sp.wait_ge(S["drops"], 1)
            sp.dma_start(drop_row, drop_p).then_inc(S["drop_in"], 16)
            sp.wait_ge(S["rows"], 1)
            for i in range(3):
                sp.dma_start(bias3[i:i + 1, :], brow_b[0:1, i, :]).then_inc(S["rows_in"], 16)
            sp.wait_ge(S["r_o"], 1)
            sp.dma_start(r_o[DM:P, 1, :], r_o[0:DM, 0, :]).then_inc(S["rows_in"], 16)
            sp.wait_ge(S["ordered"], 1)

            def step_a(k, u, it):
                if live(k, 0, T):
                    wait(sp, S["t_a"], k - U + 1)
                    sp.dma_start(ea_in[:, u, :], ea_t[:, k, :] if isinstance(k, int)
                                 else ea_t[:, bass.ds(k, 1), :].rearrange("p a r -> p (a r)"))\
                        .then_inc(ring["ea_in"][u], 16)
                    wait(sp, S["pre_d1"], k - U + 1)
                    sp.dma_start(xg[:, u, :], rows_of(x, k)).then_inc(ring["xg_in"][u], 16)
                    wait(sp, S["mm_d1"], k - U + 1)
                    sp.dma_start(xgT[:, u, :], xT[k, :, :] if isinstance(k, int)
                                 else xT[bass.ds(k, 1), :, :].rearrange("a p n -> (a p) n"))\
                        .then_inc(ring["xgT_in"][u], 16)
                if live(k, 5, T):
                    j, ju, _ = back(k, u, it, 5)
                    wait(sp, S["na_d1"], j + 1)
                    store_group(sp, h_tab, "h_st", j, ju)
            run_steps(sp, T, 5, step_a)

            sp.wait_ge(S["mv_a"], T)

            sp.wait_ge(S["pre_d1"], G)

            def step_b1(k, u, it):
                if live(k, 0, T2):
                    wait(sp, S["mm_b1"], k - U + 1)
                    sp.dma_start(xd2T[:, u, :], (xdT_all[:, 2 * k:2 * k + 2, :] if isinstance(k, int)
                                 else xdT_all[:, bass.ds(k * 2, 2), :]).rearrange("p a n -> p (a n)"))\
                        .then_inc(ring["xl_in"][u], 16)
                if live(k, 5, T2):
                    j, ju, _ = back(k, u, it, 5)
                    wait(sp, S["h_b1"], j + 1)
                    wait(sp, S["na_b1"], j + 1)
                    sp.dma_start(hd_scr[j, :, :] if isinstance(j, int)
                                 else hd_scr[bass.ds(j, 1), :, :].rearrange("a p n -> (a p) n"),
                                 hd2[:, ju, :]).then_inc(ring["hd_st"][ju], 16)
            run_steps(sp, T2, 5, step_b1)

            def step_b2(k, u, it):
                if live(k, 0, G):
                    wait(sp, S["u_d2"], k - U + 1)
                    sp.dma_start(xg[:, u, :], rows_of(h_tab, k)).then_inc(ring["hg_in"][u], 16)
            for q in range(U):
                sp.wait_ge(ring["h_sc"][q], 32 * uses(T2, q))
                sp.wait_ge(ring["hd_st"][q], 16 * uses(T2, q))
            sp.wait_ge(S["mm_b1"], T2)
            run_steps(sp, G, 0, step_b2)

            def step_c(k, u, it):
                if live(k, 0, T):
                    wait(sp, S["u_c"], k - U + 1)
                    half = slice(u % 2 * D, (u % 2 + 1) * D)
                    sp.dma_start(ring_a[:, u, :], hd_scr[k // 2, :, half] if isinstance(k, int)
                                 else hd_scr[bass.ds(it * (U // 2) + u // 2, 1), :, half]
                                 .rearrange("a p n -> (a p) n"))\
                        .then_inc(ring["hd_in"][u], 16)
            sp.wait_ge(S["agg_b2"], T)
            run_steps(sp, T, 0, step_c)
            for q in range(U):
                sp.wait_ge(ring["z_st"][q], last)
                sp.wait_ge(ring["z_sc"][q], last)

        @block.gpsimd
        def _(gp):
            gp.memset(ident[:, :], 0.0).then_inc(S["id0"], 1)
            gp.wait_ge(S["id0"], 1)
            gp.affine_select(out=ident[:, :], in_=ident[:, :], compare_op=ALU.not_equal, fill=1.0, base=0,
                             pattern=[[-1, P]], channel_multiplier=1).then_inc(S["id1"], 1)
            gp.wait_ge(S["checked"], 1)
            unsorted = gp.value_load(drop_i, min_val=0, max_val=1)
            with gp.If(unsorted > 0):
                gp.dma_start(dst_all.bitcast(I32), dst_s[0:1, 1:EP + 1].to_broadcast([P, EP])).then_inc(S["g_all"], 16)
                gp.iota(jrow.bitcast(I32), [[1, CH]], base=0, channel_multiplier=0).then_inc(S["g_iota"], 1)
                gp.iota(eidx.bitcast(I32), [[1, T]], base=0, channel_multiplier=T).then_inc(S["g_iota"], 1)
                gp.memset(ea_in[:, 0, :], 0.0).then_inc(S["g_one"], 1)
                gp.wait_ge(S["g_one"], 1)
                gp.wait_ge(S["ranked"], 1)
                top_edge, top_place = gp.to_reg(E - 1), gp.to_reg(E)

                def send(t, last_row, seen):
                    col = lambda a: a[:, bass.ds(t, 1)]
                    gp.dma_start(ea_in[0:P - 1, 0, :], ea[0:(P - 1) * T, :].rearrange("(p t) r -> p t r", t=T)
                                 [:, bass.ds(t, 1), :].rearrange("p a r -> p (a r)")).then_inc(S["g_ea"], 16)
                    if last_row:
                        gp.dma_start(ea_in[P - 1:P, 0, :], ea[bass.ds(t + (P - 1) * T, 1), :]).then_inc(S["g_ea"], 16)
                    gp.tensor_copy(idx2[:, 0, 0:1], col(rank_i)).then_inc(S["g_one"], 1)
                    gp.tensor_copy(idx2[:, 0, 1:2], col(rank1_i)).then_inc(S["g_one"], 1)
                    gp.tensor_copy(one_dst.bitcast(I32), col(d_int[0])).then_inc(S["g_one"], 1)
                    gp.tensor_copy(one_src.bitcast(I32), col(s_int)).then_inc(S["g_one"], 1)
                    gp.tensor_copy(one_ew, col(ew_t)).then_inc(S["g_one"], 1)
                    gp.wait_ge(S["g_one"], 1 + 5 * (t + 1))
                    gp.wait_ge(S["g_ea"], seen + (32 if last_row else 16))
                    gp.sem_inc(S["issued"], 1)
                    for tab, one, i, top in ((src_tab[:, :], one_src.bitcast(I32), 0, top_edge),
                                             (ew_tab[:, :], one_ew, 0, top_edge),
                                             (ea_s[:, :], ea_in[:, 0, :], 0, top_edge),
                                             (dst_tab[:, :], one_dst.bitcast(I32), 1, top_place)):
                        gp.indirect_dma_start(out=tab, in_=one, in_offset=None, bounds_check=top, oob_is_err=False,
                                              out_offset=bass.IndirectOffsetOnAxis(ap=idx2[:, 0, i:i + 1], axis=0))\
                            .then_inc(S["g_out"], 16)
                    gp.wait_ge(S["g_out"], 64 * (t + 1))

                with gp.Fori(0, VLAST) as t:
                    send(t, True, 32 * t)
                with gp.Fori(VLAST, T) as t:
                    send(t, False, 16 * t + 16 * VLAST)
                gp.dma_start(s_int[0:P - 1, :], src_s[0:1, 0:(P - 1) * T].rearrange("a (p t) -> (a p) t", t=T))\
                    .then_inc(S["g_back"], 16)
                gp.dma_start(s_int[P - 1:P, 0:VLAST], src_s[0:1, (P - 1) * T:E]).then_inc(S["g_back"], 16)
                gp.dma_start(ew_t[0:P - 1, :], ew_s[0:1, 0:(P - 1) * T].rearrange("a (p t) -> (a p) t", t=T))\
                    .then_inc(S["g_back"], 16)
                gp.dma_start(ew_t[P - 1:P, 0:VLAST], ew_s[0:1, (P - 1) * T:E]).then_inc(S["g_back"], 16)
                for i, shift in enumerate((1, 0, 2)):
                    gp.dma_start(d_int[i], dst_s[0:1, shift:shift + EP].rearrange("a (p t) -> (a p) t", t=T))\
                        .then_inc(S["g_back"], 16)
                gp.wait_ge(S["g_back"], 7 * 16)
            gp.sem_inc(S["ordered"], 1)
            gp.wait_ge(S["dsteps"], 1)
            top_row = gp.to_reg(N - 1)

            def step_a(k, u, it):
                if live(k, 3, T):
                    j, ju, _ = back(k, u, it, 3)
                    wait(gp, S["xsT_a"], j + 1)
                    gp.tensor_copy(xdT_all[:, j, :] if isinstance(j, int)
                                   else xdT_all[:, bass.ds(j, 1), :].rearrange("p a n -> p (a n)"),
                                   ring_c[:, ju % 2, :]).then_inc(S["mv_a"], 1)
                if not live(k, 0, T):
                    return
                wait(gp, S["t_a"], k - U + 1)
                gp.tensor_copy(idx2[:, u, :], gidx[:, k, :] if isinstance(k, int)
                               else gidx[:, bass.ds(k, 1), :].rearrange("p a i -> p (a i)"))\
                    .then_inc(S["idx_a"], 1)
                wait(gp, S["idx_a"], k + 1)
                gp.sem_inc(S["issued"], 1)
                for i, (rg, s) in enumerate(((ring_a, "xs_in"), (ring_b, "xd_in"))):
                    gp.indirect_dma_start(out=rg[:, u, :], out_offset=None, in_=x[:, :],
                                          in_offset=bass.IndirectOffsetOnAxis(ap=idx2[:, u, i:i + 1], axis=0))\
                        .then_inc(ring[s][u], 16)
            run_steps(gp, T, 3, step_a)

            gp.wait_ge(S["sc_act"], 2)
            vh = val[:, H - 1, :, :]
            gp.tensor_tensor(vh, vh, alpha[:, H - 1, :].rearrange("p (a t) -> p a t", a=1).to_broadcast([P, C, T]),
                             ALU.mult).then_inc(S["sc_pool"], 1)

            for q in range(U):
                gp.wait_ge(ring["h_st"][q], last)

            def step_b1(k, u, it):
                wait(gp, ring["h_sc"][u], 32 * it)
                gp.tensor_copy(idx2[:, u, :], sidx[:, 2 * k:2 * k + 2] if isinstance(k, int)
                               else sidx[:, bass.ds(k * 2, 2)]).then_inc(S["idx_b1"], 1)
                wait(gp, S["idx_b1"], k + 1)
                wait(gp, S["h_b1"], k + 1)
                wait(gp, S["na_b1"], k + 1)
                gp.sem_inc(S["issued"], 1)
                for i in range(2):
                    gp.indirect_dma_start(out=h_tab[:, :],
                                          out_offset=bass.IndirectOffsetOnAxis(ap=idx2[:, u, i:i + 1], axis=0),
                                          in_=hd2[:, u, i * D:(i + 1) * D], in_offset=None, bounds_check=top_row,
                                          oob_is_err=False).then_inc(ring["h_sc"][u], 16)
            run_steps(gp, T2, 0, step_b1)
            for q in range(U):
                gp.wait_ge(ring["h_sc"][q], 32 * uses(T2, q))
            gp.wait_ge(S["t_a"], T)

            gp.wait_ge(S["mm_b1"], T2)

            def step_b2(k, u, it):
                if live(k, 0, T):
                    wait(gp, S["agg_b2"], k - U + 1)
                    gp.tensor_copy(idx2[:, u, 0:1], gidx[:, k, 0:1] if isinstance(k, int)
                                   else gidx[:, bass.ds(k, 1), 0:1].rearrange("p a i -> p (a i)"))\
                        .then_inc(S["idx_b2"], 1)
                    wait(gp, S["idx_b2"], k + 1)
                    gp.sem_inc(S["issued"], 1)
                    gp.indirect_dma_start(out=ring_a[:, u, :], out_offset=None, in_=h_tab[:, :],
                                          in_offset=bass.IndirectOffsetOnAxis(ap=idx2[:, u, 0:1], axis=0))\
                        .then_inc(ring["hs_in"][u], 16)
                if live(k, 3, T):
                    j, ju, itj = back(k, u, it, 3)
                    wait(gp, ring["hs_in"][ju], 16 * (itj + 1))
                    if isinstance(j, int):
                        ao, es = agg[:, :, j], ew_t[:, j:j + 1]
                    else:
                        ao, es = agg[:, :, bass.ds(j, 1)].rearrange("p f a -> p (f a)"), ew_t[:, bass.ds(j, 1)]
                    gp.tensor_tensor(ao, ring_a[:, ju, :], es.to_broadcast([P, D]), ALU.mult).then_inc(S["agg_b2"], 1)
            run_steps(gp, T, 3, step_b2)
            for q in range(U):
                gp.wait_ge(ring["z_st"][q], last)
                gp.wait_ge(ring["hs_in"][q], last)

            def step_c(k, u, it):
                wait(gp, ring["z_sc"][u], 16 * it)
                gp.tensor_copy(idx2[:, u, 0:1], sidx[:, k:k + 1] if isinstance(k, int)
                               else sidx[:, bass.ds(k, 1)]).then_inc(S["idx_c"], 1)
                wait(gp, S["idx_c"], k + 1)
                wait(gp, S["z_c"], k + 1)
                gp.sem_inc(S["issued"], 1)
                gp.indirect_dma_start(out=out[:, :],
                                      out_offset=bass.IndirectOffsetOnAxis(ap=idx2[:, u, 0:1], axis=0),
                                      in_=ring_b[:, u, :], in_offset=None, bounds_check=top_row,
                                      oob_is_err=False).then_inc(ring["z_sc"][u], 16)
            run_steps(gp, T, 0, step_c)

        @block.tensor
        def _(pe):
            pe.wait_ge(S["w_in"], 16 * 16)
            pe.matmul(pk[:, 0, 0:3 * DM], n2mT, kvq_w, start=True, stop=True).then_inc(S["wprod"], 1)
            pe.matmul(pk[0:R, 1, 0:DM], edgeT, e_w, start=True, stop=True).then_inc(S["wprod"], 1)
            pe.matmul(pt[0:DM, 0, 0:P], skip_w, n2mT, start=True, stop=True).then_inc(S["wprod"], 1)
            pe.wait_ge(S["wcopy"], 2)
            pe.matmul(pt[:, 1, 0:D + 1], wnsT, r_c[:, :], start=True, stop=True).then_inc(S["wprod"], 1)
            pe.matmul(pd[0:1, 0, 0, 0:D + 1], bskip, r_c[:, :], start=True, stop=True).then_inc(S["wprod"], 1)
            pe.wait_ge(S["wcopy"], 5)
            pe.wait_ge(S["rows_in"], 4 * 16)
            pe.wait_ge(S["id1"], 1)

            def step_a(k, u, it):
                if live(k, 1, T):
                    j, ju, _ = back(k, u, it, 1)
                    wait(pe, S["xsT_a"], j + 1)
                    wait(pe, S["v_a"], j - 1)
                    wait(pe, S["pr_a"], j - 1)
                    pe.matmul(pk[:, ju % 2, 0:3 * DM], ring_e[:, ju % 2, :], b_kvq[:, :], start=True, stop=False)
                    pe.matmul(pk[:, ju % 2, 0:2 * DM], ring_d[:, ju % 2, :], a_kv[:, :], start=False, stop=False)
                    pe.matmul(pk[:, ju % 2, 2 * DM:3 * DM], ring_c[:, ju % 2, :], a_q[:, :], start=False, stop=True)\
                        .then_inc(S["kv_a"], 1)
                if live(k, 0, T):
                    wait(pe, ring["xs_in"][u], 16 * (it + 1))
                    wait(pe, ring["xd_in"][u], 16 * (it + 1))
                    wait(pe, ring["ea_in"][u], 16 * (it + 1))
                    wait(pe, S["xsT_a"], k - 1)
                    pe.transpose(pt[:, u % 2, 0:P], ring_a[:, u, :], ident[:, :])
                    pe.transpose(pt[:, u % 2, P:2 * P], ring_b[:, u, :], ident[:, :])
                    pe.transpose(pt[0:R, u % 2, 2 * P:3 * P], ea_in[:, u, :], ident[:, :]).then_inc(S["t_a"], 1)
                    wait(pe, ring["xgT_in"][u], 16 * (it + 1))
                    wait(pe, S["pre_d1"], k - 1)
                    for j in range(NJ):
                        o = pd[:, u % 2, j, 0:D + 1]
                        pe.matmul(o, ones3[:, :], bias3[:, 0:D + 1], start=True, stop=False)
                        mm = pe.matmul(o, xgT[:, u, j * P:(j + 1) * P], w_sx[:, 0:D + 1],
                                       start=False, stop=True)
                    mm.then_inc(S["mm_d1"], 1)
            run_steps(pe, T, 1, step_a)

            pe.wait_ge(S["sc"], 1)
            pe.transpose(pt[0:H, 0, 0:P], sum_a[:, 0:H], ident[:, :])
            pe.transpose(pt[0:H, 0, P:2 * P], sum_b[:, 0:H], ident[:, :]).then_inc(S["sc_pe"], 1)
            pe.wait_ge(S["sc"], 2)
            pe.transpose(pt[:, 1, 0:H], cumT[0:H, 0:P], ident[0:H, 0:H]).then_inc(S["sc_pe"], 1)
            pe.wait_ge(S["sc"], 4)
            pe.transpose(pt[0:DM + H, 0, 0:P], sum_a[:, 0:DM + H], ident[:, :])
            pe.transpose(pt[0:DM + H, 0, P:2 * P], sum_b[:, 0:DM + H], ident[:, :]).then_inc(S["sc_pe"], 1)
            pe.wait_ge(S["sc"], 5)
            pe.transpose(pt[:, 1, 0:DM + H], cumT[0:DM + H, 0:P], ident[0:DM + H, 0:DM + H]).then_inc(S["sc_pe"], 1)

            pe.wait_ge(S["sc"], 6)

            def step_b1(k, u, it):
                if live(k, 0, T2):
                    wait(pe, S["os_b1"], k + 1)
                    wait(pe, S["oT_b1"], k - 1)
                    pe.transpose(pt[:, u % 2, 0:P], o3[:, u % 2, :], ident[:, :]).then_inc(S["t_b1"], 1)
                if live(k, 1, T2):
                    j, ju, itj = back(k, u, it, 1)
                    wait(pe, ring["xl_in"][ju], 16 * (itj + 1))
                    wait(pe, S["oT_b1"], j + 1)
                    wait(pe, S["pre_b1"], j - 1)
                    for i in range(2):
                        o = pd_bank[:, ju % 2, i, 0:2 * D + 1]
                        pe.matmul(o, ones3[:, :], bias3[:, 0:2 * D + 1], start=True, stop=False)
                        pe.matmul(o, xd2T[:, ju, i * D:(i + 1) * D], w_sx[:, :], start=False, stop=False)
                        mm = pe.matmul(o, ring_b[:, ju % 2, :], r_o[:, i, :], start=False, stop=True)
                    mm.then_inc(S["mm_b1"], 1)
            run_steps(pe, T2, 1, step_b1)
            pe.wait_ge(S["pre_b1"], T2)

            def step_b2(k, u, it):
                if live(k, 0, G):
                    wait(pe, ring["hg_in"][u], 16 * (it + 1))
                    wait(pe, S["hT_d2"], k - 1)
                    for j in range(NJ):
                        mm = pe.transpose(pt[:, u % 2, j * P:(j + 1) * P], xg[:, u, j * D:(j + 1) * D], ident[:, :])
                    mm.then_inc(S["t_d2"], 1)
                if live(k, 1, G):
                    g, gu, _ = back(k, u, it, 1)
                    wait(pe, S["hT_d2"], g + 1)
                    wait(pe, S["u_d2"], g - 1)
                    for j in range(NJ):
                        o = pk[:, gu % 2, j * D:(j + 1) * D]
                        pe.matmul(o, ones3[:, :], bias3[:, 2 * D + 1:3 * D + 1], start=True, stop=False)
                        mm = pe.matmul(o, xgT[:, gu % 2, j * P:(j + 1) * P], w1_sb[:, :], start=False, stop=True)
                    mm.then_inc(S["mm_d2"], 1)
            run_steps(pe, G, 1, step_b2)
            pe.wait_ge(S["u_d2"], G)

            pe.wait_ge(S["sc"], 7)
            pe.transpose(pt[:, 0, 0:P], sum_a, ident[:, :])
            pe.transpose(pt[:, 0, P:2 * P], sum_b, ident[:, :]).then_inc(S["sc_pe"], 1)
            pe.wait_ge(S["sc"], 8)
            pe.transpose(pt[:, 1, 0:D], cumT[:, 0:P], ident[:, :]).then_inc(S["sc_pe"], 1)

            def step_c(k, u, it):
                if live(k, 0, T):
                    wait(pe, S["ag_c"], k + 1)
                    wait(pe, ring["hd_in"][u], 16 * (it + 1))
                    wait(pe, S["tc_c"], k - 1)
                    pe.transpose(pt[:, u % 2, 0:P], ring_a[:, u, :], ident[:, :])
                    pe.transpose(pt[:, u % 2, P:2 * P], ring_d[:, u % 2, :], ident[:, :]).then_inc(S["t_c"], 1)
                if live(k, 1, T):
                    j, ju, _ = back(k, u, it, 1)
                    wait(pe, S["tc_c"], j + 1)
                    wait(pe, S["u_c"], j - 1)
                    o = pk[:, ju % 2, 0:D]
                    pe.matmul(o, ones3[:, :], bias3[:, 2 * D + 1:3 * D + 1], start=True, stop=False)
                    pe.matmul(o, xgT[:, ju % 2, 0:P], w1_sb[:, :], start=False, stop=False)
                    pe.matmul(o, xgT[:, ju % 2, P:2 * P], w2_sb[:, :], start=False, stop=True)\
                        .then_inc(S["mm_c"], 1)
            run_steps(pe, T, 1, step_c)

        def inv_std(act, mean_var, log_v, r, mv_sem, lv_sem, rs_sem, j):
            wait(act, mv_sem, j + 1)
            act.activation(log_v, mean_var, ACT.Ln, bias=eps_c[:, 0:1]).then_inc(lv_sem, 1)
            wait(act, lv_sem, j + 1)
            act.activation(r, log_v, ACT.Exp, scale=-0.5).then_inc(rs_sem, 1)

        def exp_minus(act, e, logit, cl_sem, em_sem, j):
            act.activation(e, logit, ACT.Relu, bias=top_c[:, 0:1]).then_inc(cl_sem, 1)
            wait(act, cl_sem, j + 1)
            act.activation(e, e, ACT.Exp, bias=top_c[:, 0:1], scale=-1.0).then_inc(em_sem, 1)

        eps_c = sb("eps_c", [P, 1])
        top_c = sb("top_c", [P, 1])

        @block.scalar
        def _(act):
            act.preload_act_table_set("natural_log_exp_and_others")
            act.wait_ge(S["wprod"], 1)
            act.activation(a_kv[:, :], pk[:, 0, 0:2 * DM], ACT.Copy)
            act.activation(a_q[:, :], pk[:, 0, 2 * DM:3 * DM], ACT.Copy)
            act.wait_ge(S["wprod"], 2)
            act.activation(b_kvq[0:R, 0:DM], pk[0:R, 1, 0:DM], ACT.Copy)
            act.activation(b_kvq[0:R, DM:2 * DM], pk[0:R, 1, 0:DM], ACT.Copy)
            act.wait_ge(S["wprod"], 3)
            act.activation(wnsT, pt[0:DM, 0, 0:P], ACT.Copy).then_inc(S["wcopy"], 1)
            act.wait_ge(S["wprod"], 4)
            act.activation(w_sx[:, 0:D + 1], pt[:, 1, 0:D + 1], ACT.Copy).then_inc(S["wcopy"], 1)
            act.wait_ge(S["id1"], 1)
            act.activation(w_sx[:, D + 1:2 * D + 1], ident[:, :], ACT.Copy).then_inc(S["wcopy"], 1)

            def scale_rows(ju, n, first=0):
                for i in range(first, n):
                    ins = act.activation(hout[ju][:, i * D:(i + 1) * D], hpre[:, ju, i * D:(i + 1) * D],
                                         ACT.Identity, bias=nb[:, ju, i:i + 1], scale=rs[:, ju, i:i + 1])
                return ins

            def step_a(k, u, it):
                if live(k, 1, T):
                    j, ju, _ = back(k, u, it, 1)
                    wait(act, S["kv_a"], j + 1)
                    wait(act, S["pr_a"], j - 1)
                    kv = pk[:, ju % 2, DM:2 * DM].rearrange("p (h c) -> p h c", h=H)
                    vo = val[:, :, :, j] if isinstance(j, int) else \
                        val[:, :, :, bass.ds(j, 1)].rearrange("p h c a -> p h (c a)")
                    act.activation(vo, kv, ACT.Copy).then_inc(S["v_a"], 1)
                    act.activation(q_sb[:, ju % 2, :], pk[:, ju % 2, 2 * DM:3 * DM], ACT.Copy).then_inc(S["q_a"], 1)
                if live(k, 0, T):
                    wait(act, S["t_a"], k + 1)
                    wait(act, S["kv_a"], k - 1)
                    wait(act, S["mv_a"], k - 1)
                    act.activation(pair[:, u % 2, :], pt[:, u % 2, 0:2 * P], ACT.Copy)
                    act.activation(ring_e[0:R, u % 2, :], pt[0:R, u % 2, 2 * P:3 * P], ACT.Copy)\
                        .then_inc(S["xsT_a"], 1)
                    wait(act, S["mm_d1"], k + 1)
                    wait(act, S["pre_d1"], k - 1)
                    exp_minus(act, em[:, u % 2, :], pd[:, u % 2, :, D], S["cl_d1"], S["em_d1"], k)
                if live(k, 3, T):
                    g, gu, itg = back(k, u, it, 3)
                    wait(act, S["nb_d1"], g + 1)
                    wait(act, ring["h_st"][gu], 16 * itg)
                    scale_rows(gu, NJ - 1)
                if live(k, 1, T):
                    wait(act, S["mv_d1"], j + 1)
                    act.activation(lv[:, ju, :], mv[:, ju, :, 1], ACT.Ln, bias=eps_c[:, 0:1]).then_inc(S["lv_d1"], 1)
                if live(k, 3, T):
                    scale_rows(gu, NJ, NJ - 1).then_inc(S["na_d1"], 1)
                if live(k, 1, T):
                    wait(act, S["lv_d1"], j + 1)
                    act.activation(rs[:, ju, :], lv[:, ju, :], ACT.Exp, scale=-0.5).then_inc(S["rs_d1"], 1)
            run_steps(act, T, 3, step_a)

            act.wait_ge(S["sc"], 3)
            act.activation(decay[:, :, :], decay[:, :, :], ACT.Exp).then_inc(S["sc_act"], 1)
            act.activation(alpha[:, :, :], alpha[:, :, :], ACT.Exp).then_inc(S["sc_act"], 1)

            def step_b1(k, u, it):
                if live(k, 0, T2):
                    wait(act, S["t_b1"], k + 1)
                    wait(act, S["mm_b1"], k - 1)
                    act.activation(ring_b[:, u % 2, :], pt[:, u % 2, 0:P], ACT.Copy).then_inc(S["oT_b1"], 1)
                if live(k, 1, T2):
                    j, ju, _ = back(k, u, it, 1)
                    wait(act, S["mm_b1"], j + 1)
                    wait(act, S["pre_b1"], j - 1)
                    exp_minus(act, em[:, ju % 2, 0:2], pd_bank[:, ju % 2, :, D], S["cl_b1"], S["em_b1"], j)
                    act.activation(pair[:, ju % 2, :].rearrange("p (i f) -> p i f", i=2),
                                   pd_bank[:, ju % 2, :, D + 1:2 * D + 1], ACT.Copy).then_inc(S["xb_b1"], 1)
                if live(k, 4, T2):
                    j, ju, itj = back(k, u, it, 4)
                    wait(act, S["h_b1"], j + 1)
                    wait(act, ring["h_sc"][ju], 32 * itj)
                    wait(act, ring["hd_st"][ju], 16 * itj)
                    for i in range(NP):
                        ins = act.activation(hd2[:, ju, i * D:(i + 1) * D], hpre[:, ju, i * D:(i + 1) * D],
                                             ACT.Identity, bias=nb[:, ju, i:i + 1], scale=rs[:, ju, i:i + 1])
                    ins.then_inc(S["na_b1"], 1)
                if live(k, 2, T2):
                    j, ju, _ = back(k, u, it, 2)
                    inv_std(act, mv[:, ju, 0:2, 1], lv[:, ju, 0:2], rs[:, ju, 0:2],
                            S["mv_b1"], S["lv_b1"], S["rs_b1"], j)
            run_steps(act, T2, 4, step_b1)

            act.wait_ge(S["sc"], 6)

            def step_b2(k, u, it):
                if live(k, 0, G):
                    wait(act, S["t_d2"], k + 1)
                    wait(act, S["mm_d2"], k - 1)
                    act.activation(xgT[:, u % 2, :], pt[:, u % 2, :], ACT.Copy).then_inc(S["hT_d2"], 1)
                if live(k, 4, G):
                    j, ju, itj = back(k, u, it, 4)
                    wait(act, S["out_d2"], j + 1)
                    wait(act, ring["z_st"][ju], 16 * itj)
                    scale_rows(ju, NZ).then_inc(S["na_d2"], 1)
                if live(k, 5, G):
                    j, ju, _ = back(k, u, it, 5)
                    wait(act, S["na_d2"], j + 1)
                    store_group(act, out, "z_st", j, ju)
                if live(k, 2, G):
                    j, ju, _ = back(k, u, it, 2)
                    inv_std(act, mv[:, ju, :, 1], lv[:, ju, :], rs[:, ju, :],
                            S["mv_d2"], S["lv_d2"], S["rs_d2"], j)
            run_steps(act, T, 5, step_b2)

            def step_c(k, u, it):
                if live(k, 0, T):
                    wait(act, S["t_c"], k + 1)
                    wait(act, S["mm_c"], k - 1)
                    act.activation(xgT[:, u % 2, 0:2 * P], pt[:, u % 2, 0:2 * P], ACT.Copy).then_inc(S["tc_c"], 1)
                if live(k, 3, T):
                    j, ju, _ = back(k, u, it, 3)
                    inv_std(act, mv[:, ju, 0, 1:2], lv[:, ju, 0:1], rs[:, ju, 0:1],
                            S["mv_c"], S["lv_c"], S["rs_c"], j)
            run_steps(act, T, 3, step_c)

        @block.vector
        def _(dve):
            chain = [0]
            s_ch = sem("chain")

            def link(ins):
                chain[0] += 1
                ins.then_inc(s_ch, 1)
                dve.wait_ge(s_ch, chain[0])

            dve.memset(b_kvq[:, :], 0.0)
            dve.memset(bias3[:, :], 0.0)
            dve.memset(brow, 0.0).then_inc(S["fills"], 1)
            dve.memset(pad_i[0:1, 0:P - 1], N)
            dve.memset(pad_i[0:1, P - 1:P], -1)
            dve.memset(zrows, 0.0).then_inc(S["padded"], 1)
            dve.memset(s_int, 0)
            dve.memset(ew_t[:, :], 0.0).then_inc(S["fills"], 1)
            dve.memset(eps_c[:, :], EPS)
            dve.memset(top_c[:, :], TOP)
            dve.memset(r_o[:, :, :], 0.0)
            dve.memset(ring_e[:, :, :], 1.0)
            dve.memset(ones3[:, :], 1.0)
            link(dve.memset(ones_t[:, :], 1.0))
            dve.wait_ge(S["w_in"], 16 * 16)
            dve.tensor_copy(r_c[:, 0:D], m2n_w)
            dve.tensor_copy(r_o[0:DM, 0, D + 1:2 * D + 1], m2n_w)
            dve.tensor_scalar(r_o[0:DM, 0, 0:D], m2n_w, -1.0, None, ALU.mult)
            dve.tensor_tensor(r_o[0:DM, 0, D:D + 1], beta_w[:, 0:1], beta_w[:, 2:3], ALU.add).then_inc(S["r_o"], 1)
            dve.tensor_tensor(r_c[:, D:D + 1], beta_w[:, 1:2], beta_w[:, 2:3], ALU.subtract).then_inc(S["wcopy"], 1)
            dve.wait_ge(S["wprod"], 5)
            link(dve.tensor_copy(brow[0:1, 0:D + 1], pd[0:1, 0, 0, 0:D + 1]))
            link(dve.tensor_copy(brow_b[0:1, 0, :], brow))
            link(dve.tensor_tensor(brow_r, brow, brow_b[0:1, 0, :], ALU.subtract))
            link(dve.tensor_copy(brow_b[0:1, 1, :], brow_r))
            link(dve.tensor_tensor(brow, brow_r, brow_b[0:1, 1, :], ALU.subtract))
            dve.tensor_copy(brow_b[0:1, 2, :], brow).then_inc(S["rows"], 1)
            dve.wait_ge(S["edge_in"], 7 * 16)
            link(dve.tensor_tensor(drop, d_int[0], d_int[1], ALU.is_lt))
            dve.reduce_max(drop_p, drop, AX_X).then_inc(S["drops"], 1)
            dve.wait_ge(S["drop_in"], 16)
            dve.reduce_max(drop_i, drop_row, AX_X).then_inc(S["checked"], 1)
            dve.wait_ge(S["checked"], 1)
            unsorted = dve.value_load(drop_i, min_val=0, max_val=1)
            with dve.If(unsorted > 0):
                dve.wait_ge(S["g_all"], 16)
                dve.wait_ge(S["g_iota"], 2)
                dve.tensor_copy(dst_all, dst_all.bitcast(I32)).then_inc(S["g_rank"], 1)
                dve.tensor_copy(jrow, jrow.bitcast(I32)).then_inc(S["g_rank"], 1)
                dve.tensor_copy(eidx, eidx.bitcast(I32)).then_inc(S["g_rank"], 1)
                dve.tensor_copy(d_f[0], d_int[0]).then_inc(S["g_rank"], 1)
                dve.memset(rank, 0.0).then_inc(S["g_rank"], 1)
                done = 5
                dve.wait_ge(S["g_rank"], done)
                for c in range(EP // CH):
                    some = dst_all[:, c * CH:(c + 1) * CH]
                    with dve.Fori(0, T) as t:
                        own, me = d_f[0][:, bass.ds(t, 1)], eidx[:, bass.ds(t, 1)]
                        dve.tensor_scalar(hits, jrow, me, None, ALU.is_lt).then_inc(S["g_rank"], 1)
                        dve.wait_ge(S["g_rank"], t * 4 + (done + 1))
                        dve.scalar_tensor_tensor(out=hits, in0=some, scalar=own, in1=hits, op0=ALU.is_equal,
                                                 op1=ALU.mult).then_inc(S["g_rank"], 1)
                        dve.wait_ge(S["g_rank"], t * 4 + (done + 2))
                        dve.scalar_tensor_tensor(out=hits, in0=some, scalar=own, in1=hits, op0=ALU.is_lt,
                                                 op1=ALU.add).then_inc(S["g_rank"], 1)
                        dve.wait_ge(S["g_rank"], t * 4 + (done + 3))
                        dve.reduce_sum(part[:, bass.ds(t, 1)], hits, AX_X).then_inc(S["g_rank"], 1)
                        dve.wait_ge(S["g_rank"], t * 4 + (done + 4))
                    done += 4 * T
                    dve.tensor_tensor(rank, rank, part, ALU.add).then_inc(S["g_rank"], 1)
                    dve.tensor_scalar(eidx, eidx, -float(CH), None, ALU.add).then_inc(S["g_rank"], 1)
                    done += 2
                    dve.wait_ge(S["g_rank"], done)
                dve.tensor_copy(rank_i, rank).then_inc(S["g_rank"], 1)
                dve.wait_ge(S["g_rank"], done + 1)
                dve.tensor_scalar(rank1_i, rank, 1.0, None, ALU.add).then_inc(S["ranked"], 1)
            dve.wait_ge(S["ordered"], 1)
            for i in range(2):
                dve.tensor_copy(d_f[i], d_int[i])
            link(dve.tensor_copy(d_f[2], d_int[2]))
            dve.tensor_copy(gidx[:, :, 0], s_int)
            dve.tensor_scalar(clip, d_f[0], float(N - 1), None, ALU.min)
            dve.tensor_tensor(nend, d_f[0], d_f[2], ALU.is_equal)
            link(dve.tensor_tensor(same[:, :], d_f[0], d_f[1], ALU.is_equal))
            dve.tensor_copy(gidx[:, :, 1], clip)
            dve.tensor_scalar(far[:, :], same[:, :], -1.0, FAR, ALU.add, ALU.mult)
            link(dve.scalar_tensor_tensor(out=d_f[1], in0=nend, scalar=float(N), in1=d_f[0], op0=ALU.mult, op1=ALU.add))
            dve.tensor_copy(sidx[:, :], d_f[1])
            dve.tensor_tensor_scan(pfar[:, :], far[:, :], far[:, :], 0.0, ALU.min, ALU.min)\
                .then_inc(S["dsteps"], 1)
            dve.tensor_copy(em[:, 0, 0:1], ones_t[:, 0:1]).then_inc(S["wcopy"], 1)

            def row_stats(pieces, ju, n):
                for i in range(n):
                    ins = dve.bn_stats(stats[:, ju, i, :], pieces(i))
                return ins

            def mean_var(ju, n):
                for i in range(n):
                    ins = dve.bn_aggr(mv[:, ju, i, :], stats[:, ju, i, :])
                return ins

            def neg_mean(ju):
                return dve.scalar_tensor_tensor(out=nb[:, ju, :], in0=mv[:, ju, :, 0], scalar=-1.0,
                                                in1=rs[:, ju, :], op0=ALU.mult, op1=ALU.mult)

            def normalise(to, pieces, ju, n, first=0):
                for i in range(first, n):
                    ins = dve.tensor_scalar(to(i), pieces(i), mv[:, ju, i, 0:1], rs[:, ju, i:i + 1],
                                            ALU.subtract, ALU.mult)
                return ins

            def step_a(k, u, it):
                if live(k, 1, T):
                    j, ju, _ = back(k, u, it, 1)
                    wait(dve, S["q_a"], j + 1)
                    dve.scalar_tensor_tensor(out=prod[:, ju % 2, :], in0=pk[:, ju % 2, 0:DM], scalar=QSCALE,
                                             in1=q_sb[:, ju % 2, :], op0=ALU.mult, op1=ALU.mult).then_inc(S["pr_a"], 1)
                if live(k, 0, T):
                    wait(dve, S["em_d1"], k + 1)
                    dve.tensor_scalar(ep[:, u % 2, :], em[:, u % 2, :], 1.0, None, ALU.add).then_inc(S["ep_d1"], 1)
                if live(k, 1, T):
                    wait(dve, S["bn_d1"], j + 1)
                    wait(dve, S["pr_a"], j + 1)
                    ao = alpha[:, :, j:j + 1] if isinstance(j, int) else alpha[:, :, bass.ds(j, 1)]
                    dve.reduce_sum(ao, prod[:, ju % 2, :].rearrange("p (h c) -> p h c", h=H), AX_X)\
                        .then_inc(S["al_a"], 1)
                if live(k, 0, T):
                    wait(dve, S["ep_d1"], k + 1)
                    dve.reciprocal(beta[:, u % 2, :], ep[:, u % 2, :]).then_inc(S["be_d1"], 1)
                if live(k, 1, T):
                    mean_var(ju, NJ).then_inc(S["mv_d1"], 1)
                if live(k, 0, T):
                    wait(dve, ring["xg_in"][u], 16 * (it + 1))
                    wait(dve, S["na_d1"], k - U + 1)
                    wait(dve, S["be_d1"], k + 1)
                    for i in range(NJ):
                        ins = dve.scalar_tensor_tensor(
                            out=hpre[:, u, i * D:(i + 1) * D], in0=pd[:, u % 2, i, 0:D],
                            scalar=beta[:, u % 2, i:i + 1], in1=xg[:, u, i * D:(i + 1) * D],
                            op0=ALU.mult, op1=ALU.add)
                    ins.then_inc(S["pre_d1"], 1)
                if live(k, 2, T):
                    g, gu, _ = back(k, u, it, 2)
                    wait(dve, S["rs_d1"], g + 1)
                    neg_mean(gu).then_inc(S["nb_d1"], 1)
                if live(k, 0, T):
                    wait(dve, S["pre_d1"], k + 1)
                    row_stats(lambda i: hpre[:, u, i * D:(i + 1) * D], u, NJ).then_inc(S["bn_d1"], 1)
            run_steps(dve, T, 2, step_a)

            dve.wait_ge(S["v_a"], T)
            dve.wait_ge(S["na_d1"], T)
            dve.wait_ge(S["al_a"], T)
            for q in range(U):
                dve.wait_ge(ring["h_st"][q], last)
            for h in range(H):
                ins = dve.tensor_tensor_scan(rmax[:, h, 1:T + 1], far[:, :], alpha[:, h, :], -FAR, ALU.add, ALU.max)
            link(ins)
            dve.tensor_copy(sum_a[:, 0:H], rmax[:, :, T])
            dve.tensor_copy(sum_b[:, 0:H], pfar[:, T - 1:T].to_broadcast([P, H])).then_inc(S["sc"], 1)
            dve.wait_ge(S["sc_pe"], 1)
            dve.memset(cumT[0:H, 0:1], -FAR)
            link(dve.tensor_copy(keepT[0:H, :], pt[0:H, 0, P:2 * P]))
            dve.tensor_tensor_scan(cumT[0:H, 1:P + 1], keepT[0:H, :], pt[0:H, 0, 0:P], -FAR, ALU.add, ALU.max)\
                .then_inc(S["sc"], 1)
            dve.wait_ge(S["sc_pe"], 2)
            dve.tensor_copy(carm[:, :], pt[:, 1, 0:H])
            link(dve.tensor_copy(rmax[:, :, 0], pt[:, 1, 0:H]))
            for h in range(H):
                ins = dve.scalar_tensor_tensor(out=rmax[:, h, 1:T + 1], in0=pfar[:, :], scalar=carm[:, h:h + 1],
                                               in1=rmax[:, h, 1:T + 1], op0=ALU.add, op1=ALU.max)
            link(ins)
            dve.tensor_tensor(alpha[:, :, :], alpha[:, :, :], rmax[:, :, 1:T + 1], ALU.subtract)
            link(dve.tensor_tensor(decay[:, :, :], rmax[:, :, 0:T], rmax[:, :, 1:T + 1], ALU.subtract))
            dve.tensor_tensor(decay[:, :, :], decay[:, :, :],
                              far[:, :].rearrange("p (a t) -> p a t", a=1).to_broadcast([P, H, T]), ALU.add)\
                .then_inc(S["sc"], 1)
            dve.wait_ge(S["sc_act"], 1)
            for h in range(H):
                dve.tensor_tensor_scan(cdec[:, h, :], decay[:, h, :], ones_t[:, :], 1.0, ALU.mult, ALU.mult)
            dve.wait_ge(S["sc_act"], 2)
            for h in range(H):
                dve.tensor_tensor_scan(rden[:, h, :], decay[:, h, :], alpha[:, h, :], 0.0, ALU.mult, ALU.add)
            for h in range(H - 1):
                vh = val[:, h, :, :]
                ins = dve.tensor_tensor(vh, vh, alpha[:, h, :].rearrange("p (a t) -> p a t", a=1)
                                        .to_broadcast([P, C, T]), ALU.mult)
            link(ins)
            for h in range(H):
                if h == H - 1:
                    dve.wait_ge(S["sc_pool"], 1)
                for c in range(C):
                    ins = dve.tensor_tensor_scan(val[:, h, c, :], decay[:, h, :], val[:, h, c, :], 0.0, ALU.mult, ALU.add)
            link(ins)
            dve.tensor_copy(sum_a[:, 0:DM].rearrange("p (h c) -> p h c", h=H), val[:, :, :, T - 1])
            dve.tensor_copy(sum_a[:, DM:DM + H], rden[:, :, T - 1])
            dve.tensor_copy(sum_b[:, 0:DM].rearrange("p (h c) -> p h c", h=H),
                            cdec[:, :, T - 1:T].to_broadcast([P, H, C]))
            dve.tensor_copy(sum_b[:, DM:DM + H], cdec[:, :, T - 1]).then_inc(S["sc"], 1)
            dve.wait_ge(S["sc_pe"], 3)
            dve.memset(cumT[0:DM + H, 0:1], 0.0)
            link(dve.tensor_copy(keepT[0:DM + H, :], pt[0:DM + H, 0, P:2 * P]))
            dve.tensor_tensor_scan(cumT[0:DM + H, 1:P + 1], keepT[0:DM + H, :], pt[0:DM + H, 0, 0:P], 0.0,
                                   ALU.mult, ALU.add).then_inc(S["sc"], 1)
            dve.wait_ge(S["sc_pe"], 4)
            link(dve.tensor_copy(carn[:, :], pt[:, 1, 0:DM + H]))
            for h in range(H):
                ins = dve.scalar_tensor_tensor(out=rden[:, h, :], in0=cdec[:, h, :], scalar=carn[:, DM + h:DM + h + 1],
                                               in1=rden[:, h, :], op0=ALU.mult, op1=ALU.add)
            link(ins)
            dve.reciprocal(rden[:, :, :], rden[:, :, :])
            for h in range(H):
                for c in range(C):
                    ins = dve.scalar_tensor_tensor(out=val[:, h, c, :], in0=cdec[:, h, :],
                                                   scalar=carn[:, h * C + c:h * C + c + 1], in1=val[:, h, c, :],
                                                   op0=ALU.mult, op1=ALU.add)
            link(ins)
            for h in range(H):
                vh = val[:, h, :, :]
                ins = dve.tensor_tensor(vh, vh, rden[:, h, :].rearrange("p (a t) -> p a t", a=1)
                                        .to_broadcast([P, C, T]), ALU.mult)
            ins.then_inc(S["sc"], 1)
            dve.wait_ge(S["sc"], 6)

            def step_b1(k, u, it):
                if live(k, 0, T2):
                    wait(dve, S["t_b1"], k - 1)
                    dve.tensor_copy(o3[:, u % 2, :].rearrange("p (i h c) -> p h c i", i=2, h=H),
                                    val[:, :, :, 2 * k:2 * k + 2] if isinstance(k, int)
                                    else val[:, :, :, bass.ds(k * 2, 2)]).then_inc(S["os_b1"], 1)
                if live(k, 2, T2):
                    j, ju, _ = back(k, u, it, 2)
                    wait(dve, S["em_b1"], j + 1)
                    dve.tensor_scalar(ep[:, ju % 2, 0:2], em[:, ju % 2, 0:2], 1.0, None, ALU.add)\
                        .then_inc(S["ep_b1"], 1)
                    wait(dve, S["ep_b1"], j + 1)
                    dve.reciprocal(beta[:, ju % 2, 0:2], ep[:, ju % 2, 0:2]).then_inc(S["be_b1"], 1)
                    wait(dve, S["xb_b1"], j + 1)
                    wait(dve, S["h_b1"], j - U + 2)
                    wait(dve, S["na_b1"], j - U + 2)
                    wait(dve, S["be_b1"], j + 1)
                    for i in range(2):
                        ins = dve.scalar_tensor_tensor(out=hpre[:, ju, i * D:(i + 1) * D],
                                                       in0=pd_bank[:, ju % 2, i, 0:D], scalar=beta[:, ju % 2, i:i + 1],
                                                       in1=pair[:, ju % 2, i * D:(i + 1) * D],
                                                       op0=ALU.mult, op1=ALU.add)
                    ins.then_inc(S["pre_b1"], 1)
                    wait(dve, S["pre_b1"], j + 1)
                    row_stats(lambda i: hpre[:, ju, i * D:(i + 1) * D], ju, 2).then_inc(S["bn_b1"], 1)
                    wait(dve, S["bn_b1"], j + 1)
                if live(k, 3, T2):
                    j, ju, itj = back(k, u, it, 3)
                    wait(dve, S["rs_b1"], j + 1)
                    neg_mean(ju)
                    wait(dve, ring["h_sc"][ju], 32 * itj)
                    wait(dve, ring["hd_st"][ju], 16 * itj)
                    normalise(lambda i: hd2[:, ju, i * D:(i + 1) * D],
                              lambda i: hpre[:, ju, i * D:(i + 1) * D], ju, 2, NP).then_inc(S["h_b1"], 1)
                if live(k, 2, T2):
                    mean_var(back(k, u, it, 2)[1], 2).then_inc(S["mv_b1"], 1)
            run_steps(dve, T2, 3, step_b1)
            dve.wait_ge(S["na_b1"], T2)

            def step_b2(k, u, it):
                if live(k, 1, G):
                    j, ju, itj = back(k, u, it, 1)
                    wait(dve, S["out_d2"], j - U + 1)
                    wait(dve, S["na_d2"], j - U + 1)
                    wait(dve, S["mm_d2"], j + 1)
                    wait(dve, ring["hg_in"][ju], 16 * (itj + 1))
                    wait(dve, S["bn_d2"], j)
                    dve.scalar_tensor_tensor(out=hpre[:, ju, :], in0=pk[:, ju % 2, :], scalar=0.0,
                                             in1=xg[:, ju, :], op0=ALU.max, op1=ALU.add).then_inc(S["u_d2"], 1)
                elif live(k, 2, G):
                    dve.wait_ge(S["bn_d2"], G)
                    dve.memset(em[:, 0, :], 0.0)
                if live(k, 2, G):
                    mean_var(back(k, u, it, 2)[1], NJ).then_inc(S["mv_d2"], 1)
                if live(k, 3, G):
                    g, gu, itg = back(k, u, it, 3)
                    wait(dve, S["rs_d2"], g + 1)
                    neg_mean(gu)
                    wait(dve, ring["z_st"][gu], 16 * itg)
                    normalise(lambda i: hout[gu][:, i * D:(i + 1) * D],
                              lambda i: hpre[:, gu, i * D:(i + 1) * D], gu, NJ, NZ).then_inc(S["out_d2"], 1)
                if live(k, 1, G):
                    wait(dve, S["u_d2"], j + 1)
                    row_stats(lambda i: hpre[:, ju, i * D:(i + 1) * D], ju, NJ).then_inc(S["bn_d2"], 1)
            run_steps(dve, G, 3, step_b2)

            for q in range(U):
                dve.wait_ge(ring["z_st"][q], last)
            dve.wait_ge(S["na_d2"], G)
            dve.tensor_tensor_scan(psame[:, :], same[:, :], ones_t[:, :], 1.0, ALU.mult, ALU.mult)
            dve.wait_ge(S["agg_b2"], T)
            for f in range(D):
                ins = dve.tensor_tensor_scan(agg[:, f, :], same[:, :], agg[:, f, :], 0.0, ALU.mult, ALU.add)
            link(ins)
            dve.tensor_copy(sum_a, agg[:, :, T - 1])
            dve.tensor_copy(sum_b, psame[:, T - 1:T].to_broadcast([P, D])).then_inc(S["sc"], 1)
            dve.wait_ge(S["sc_pe"], 5)
            dve.memset(cumT[:, 0:1], 0.0)
            link(dve.tensor_copy(keepT, pt[:, 0, P:2 * P]))
            dve.tensor_tensor_scan(cumT[:, 1:P + 1], keepT, pt[:, 0, 0:P], 0.0, ALU.mult, ALU.add)\
                .then_inc(S["sc"], 1)
            dve.wait_ge(S["sc_pe"], 6)
            link(dve.tensor_copy(carg, pt[:, 1, 0:D]))

            def step_c(k, u, it):
                if live(k, 0, T):
                    wait(dve, S["t_c"], k - 1)
                    if isinstance(k, int):
                        ak, sk = agg[:, :, k], psame[:, k:k + 1]
                    else:
                        ak, sk = agg[:, :, bass.ds(k, 1)].rearrange("p f a -> p (f a)"), psame[:, bass.ds(k, 1)]
                    dve.scalar_tensor_tensor(out=ring_d[:, u % 2, :], in0=carg, scalar=sk, in1=ak,
                                             op0=ALU.mult, op1=ALU.add).then_inc(S["ag_c"], 1)
                if live(k, 2, T):
                    j, ju, itj = back(k, u, it, 2)
                    wait(dve, S["z_c"], j - U + 2)
                    wait(dve, S["mm_c"], j + 1)
                    wait(dve, ring["hd_in"][ju], 16 * (itj + 1))
                    wait(dve, S["bn_c"], j)
                    dve.scalar_tensor_tensor(out=hpre[:, ju, 0:D], in0=pk[:, ju % 2, 0:D], scalar=0.0,
                                             in1=ring_a[:, ju, :], op0=ALU.max, op1=ALU.add).then_inc(S["u_c"], 1)
                elif live(k, 3, T):
                    dve.wait_ge(S["bn_c"], T)
                    dve.memset(sum_b, 0.0)
                if live(k, 3, T):
                    mean_var(back(k, u, it, 3)[1], 1).then_inc(S["mv_c"], 1)
                if live(k, 4, T):
                    g, gu, itg = back(k, u, it, 4)
                    wait(dve, S["rs_c"], g + 1)
                    wait(dve, ring["z_sc"][gu], 16 * itg)
                    normalise(lambda i: ring_b[:, gu, :], lambda i: hpre[:, gu, 0:D], gu, 1)\
                        .then_inc(S["z_c"], 1)
                if live(k, 2, T):
                    wait(dve, S["u_c"], j + 1)
                    row_stats(lambda i: hpre[:, ju, 0:D], ju, 1).then_inc(S["bn_c"], 1)
            run_steps(dve, T, 4, step_c)


_OUT = ((100000, 128), "float32")


def kernel(**inputs):
    import numpy as _np
    import concourse.bacc as _bacc
    from concourse import mybir as _mybir
    from concourse.bass_utils import run_bass_kernel_spmd as _run

    a = {k: _np.ascontiguousarray(v) for k, v in inputs.items()}
    x = a["x"]
    n = x.shape[0]
    whole = n // GN
    groups = _np.concatenate([x[:whole * GN], x[n - GN:]]).reshape(whole + 1, P, NJ, D)
    row = lambda v: v.reshape(1, -1)
    arrays = {
        "x": x, "xT": _np.ascontiguousarray(groups.transpose(0, 3, 2, 1).reshape(whole + 1, D, GN)),
        "src": row(a["src"]), "dst": row(a["dst"]), "ea": a["edge_attr_50"], "ew": row(a["edge_weight"]),
        "w_n2mT": _np.ascontiguousarray(a["L0_gnn_W_n2m"].T), "w_edgeT": _np.ascontiguousarray(a["L0_gnn_W_edge"].T),
        "w_q": a["L0_gnn_W_q"], "b_q": row(a["L0_gnn_b_q"]), "w_k": a["L0_gnn_W_k"], "b_k": row(a["L0_gnn_b_k"]),
        "w_v": a["L0_gnn_W_v"], "b_v": row(a["L0_gnn_b_v"]), "w_e": a["L0_gnn_W_e"], "w_skip": a["L0_gnn_W_skip"],
        "b_skip": a["L0_gnn_b_skip"].reshape(-1, 1),
        "w_beta": _np.ascontiguousarray(a["L0_gnn_W_beta"].reshape(3, DM).T), "w_m2n": a["L0_gnn_W_m2n"],
        "w_1": a["L1_gnn_w1"], "w_2": a["L1_gnn_w2"], "b_1": row(a["L1_gnn_b"]),
    }
    nc = _bacc.Bacc("TRN2", target_bir_lowering=False, num_devices=1)
    args = {k: nc.dram_tensor(f"in_{k}", v.shape, _mybir.dt.from_np(v.dtype), kind="ExternalInput").ap()
            for k, v in arrays.items()}
    out = nc.dram_tensor("out_z", _OUT[0], _mybir.dt.from_np(_np.dtype(_OUT[1])), kind="ExternalOutput").ap()
    gnn_kernel(nc, out=out, **args)
    r = _run(nc, [{f"in_{k}": v for k, v in arrays.items()}], core_ids=[0])
    return r.results[0]["out_z"]
```
